# Optimizing a Trainium2 kernel written in Bass

```python
import numpy as np
import jax
import jax.numpy as jnp

def _softmax(x, axis=-1):
    return jax.nn.softmax(x, axis=axis)

def _gelu(x):
    return jax.nn.gelu(x, approximate=True)

def _silu(x):
    return jax.nn.silu(x)

def _sigmoid(x):
    return jax.nn.sigmoid(x)

def _layernorm(x, axis=-1, eps=1e-05):
    m = jnp.mean(x, axis=axis, keepdims=True)
    v = jnp.var(x, axis=axis, keepdims=True)
    return (x - m) / jnp.sqrt(v + eps)

def _scatter_add(tgt, idx, src, axis=0):
    return tgt.at[idx].add(src)

def _segment_sum(src, seg, n):
    return jax.ops.segment_sum(src, seg, n)
kernel_name = 'mk_lm_tower_d2_tok_ids768_r4_22989d'

def setup_inputs(seed: int=0):
    np.random.seed(seed)
    _w = jnp.asarray

    def _rec_inputs():
        import jax
        import jax.numpy as jnp
        _rk = jax.random.key(seed)
        x = jax.random.randint(jax.random.fold_in(_rk, 1), (64, 128), 0, 30522, jnp.int32)
        mask_BS_i1_0 = jnp.where(jnp.ones((64, 128), dtype=bool), 1, 0).astype(jnp.int32)
        return (x, mask_BS_i1_0)
    x, mask_BS_i1_0 = _rec_inputs()

    def _L0_tok_setup():
        import jax, jax.numpy as jnp
        import numpy as np
        VOCAB = 30522
        HIDDEN = 192
        MAX_POS = 128
        TYPE_VOCAB = 2
        EPS = 1e-05
        key = jax.random.key(seed)
        k1, k2, k3, k4, k5 = jax.random.split(key, 5)
        B, S = (32, 128)
        return {'input_ids': jax.random.randint(k1, (B, S), 0, VOCAB, dtype=jnp.int64 if jax.config.jax_enable_x64 else jnp.int32), 'token_type_ids': jax.random.randint(k2, (B, S), 0, TYPE_VOCAB, dtype=jnp.int32), 'tok_w': jax.random.normal(k3, (VOCAB, HIDDEN), dtype=jnp.float32), 'pos_w': jax.random.normal(k4, (MAX_POS, HIDDEN), dtype=jnp.float32), 'type_w': jax.random.normal(k5, (TYPE_VOCAB, HIDDEN), dtype=jnp.float32), 'gamma': jnp.ones((HIDDEN,), dtype=jnp.float32), 'beta': jnp.zeros((HIDDEN,), dtype=jnp.float32)}
    _L0_tok_all = _L0_tok_setup()
    _L0_tok_in = {k: v for k, v in _L0_tok_all.items() if k in ('tok_w', 'pos_w', 'type_w', 'gamma', 'beta')}
    del _L0_tok_all

    def _L0_attn_setup():
        import jax, jax.numpy as jnp
        import numpy as np
        SEQ, BATCH, EMBED = (512, 4, 192)
        NUM_HEADS = 12
        HEAD_DIM = EMBED // NUM_HEADS
        SCALING = HEAD_DIM ** (-0.5)
        key = jax.random.key(seed)
        ks = jax.random.split(key, 9)
        std = 0.02
        d = {'x': jax.random.normal(ks[0], (SEQ, BATCH, EMBED), dtype=jnp.float32)}
        for i, n in enumerate(['q', 'k', 'v', 'out']):
            d[f'W{n}'] = jax.random.normal(ks[1 + 2 * i], (EMBED, EMBED), dtype=jnp.float32) * std
            d[f'b{n}'] = jax.random.normal(ks[2 + 2 * i], (EMBED,), dtype=jnp.float32) * std
        return d
    _L0_attn_all = _L0_attn_setup()
    _L0_attn_in = {k: v for k, v in _L0_attn_all.items() if k in ('Wq', 'bq', 'Wk', 'bk', 'Wv', 'bv', 'Wout', 'bout')}
    del _L0_attn_all

    def _L0_ffn_setup():
        import jax, jax.numpy as jnp
        import numpy as np
        E = 8
        K = 2
        D = 192
        I = 768
        B, S = (2, 512)
        key = jax.random.key(seed)
        ks = jax.random.split(key, 8)
        x = jax.random.normal(ks[0], (B, S, D), dtype=jnp.float32)
        W1 = jax.random.normal(ks[1], (E, D, I), dtype=jnp.float32) * 0.02
        b1 = jnp.zeros((E, I), dtype=jnp.float32)
        W2 = jax.random.normal(ks[2], (E, I, D), dtype=jnp.float32) * 0.02
        b2 = jnp.zeros((E, D), dtype=jnp.float32)
        Wr = jax.random.normal(ks[3], (D, E), dtype=jnp.float32) * 0.02
        br = jnp.zeros((E,), dtype=jnp.float32)
        return {'x': x, 'W1': W1, 'b1': b1, 'W2': W2, 'b2': b2, 'Wr': Wr, 'br': br}
    _L0_ffn_all = _L0_ffn_setup()
    _L0_ffn_in = {k: v for k, v in _L0_ffn_all.items() if k in ('W1', 'b1', 'W2', 'b2', 'Wr', 'br')}
    del _L0_ffn_all

    def _L1_attn_setup():
        import jax, jax.numpy as jnp
        import numpy as np
        D_MODEL = 192
        NHEAD = 12
        HEAD_DIM = D_MODEL // NHEAD
        MAX_REL = 16
        B, T = (4, 256)
        key = jax.random.key(seed)
        ks = jax.random.split(key, 6)
        s = 0.02
        return {'x': jax.random.normal(ks[0], (B, T, D_MODEL), dtype=jnp.float32), 'qkv_w': jax.random.normal(ks[1], (3 * D_MODEL, D_MODEL), dtype=jnp.float32) * s, 'qkv_b': jax.random.normal(ks[2], (3 * D_MODEL,), dtype=jnp.float32) * s, 'out_w': jax.random.normal(ks[3], (D_MODEL, D_MODEL), dtype=jnp.float32) * s, 'out_b': jax.random.normal(ks[4], (D_MODEL,), dtype=jnp.float32) * s, 'rel_pos_emb': jax.random.normal(ks[5], (2 * MAX_REL + 1, HEAD_DIM), dtype=jnp.float32)}
    _L1_attn_all = _L1_attn_setup()
    _L1_attn_in = {k: v for k, v in _L1_attn_all.items() if k in ('qkv_w', 'qkv_b', 'out_w', 'out_b', 'rel_pos_emb')}
    del _L1_attn_all

    def _L1_ffn_setup():
        import jax, jax.numpy as jnp
        import numpy as np
        DEPTH = 11

        def _fff_forward(inputs, weights_in, weights_out, depth=DEPTH):
            B, S, _ = inputs.shape
            n_nodes = weights_in.shape[0]
            max_index = n_nodes - 1
            all_logits = jnp.einsum('bsd,nd->bsn', inputs, weights_in)

            def step(prev_idx, _):
                sel = jnp.clip(prev_idx, 0, max_index)
                logits = jnp.take_along_axis(all_logits, sel[..., None], axis=-1)[..., 0]
                new_idx = jnp.clip(2 * sel + 1 + (logits > 0).astype(sel.dtype), 0, max_index)
                return (new_idx, (logits, new_idx))
            idx0 = jnp.zeros((B, S), dtype=jnp.int32)
            _, (logits_seq, idx_seq) = jax.lax.scan(step, idx0, None, length=depth - 1)
            logits = jnp.concatenate([jnp.zeros((1, B, S), all_logits.dtype), logits_seq], axis=0)
            node_idx = jnp.concatenate([idx0[None], idx_seq], axis=0)
            act = jax.nn.gelu(logits, approximate=False)
            onehot = jax.nn.one_hot(node_idx, n_nodes, dtype=act.dtype)
            coeff = jnp.einsum('dbs,dbsn->bsn', act, onehot)
            return jnp.einsum('bsn,nd->bsd', coeff, weights_out)
        key = jax.random.key(seed)
        k1, k2, k3 = jax.random.split(key, 3)
        B, S, D = (4, 1024, 192)
        n_nodes = 2 * DEPTH - 1
        return {'inputs': jax.random.normal(k1, (B, S, D), dtype=jnp.float32), 'weights_in': jax.random.normal(k2, (n_nodes, D), dtype=jnp.float32), 'weights_out': jax.random.normal(k3, (n_nodes, D), dtype=jnp.float32)}
    _L1_ffn_all = _L1_ffn_setup()
    _L1_ffn_in = {k: v for k, v in _L1_ffn_all.items() if k in ('weights_in', 'weights_out')}
    del _L1_ffn_all
    return {'x': x, 'mask_BS_i1_0': mask_BS_i1_0, 'L0_tok_tok_w': _L0_tok_in['tok_w'], 'L0_tok_pos_w': _L0_tok_in['pos_w'], 'L0_tok_type_w': _L0_tok_in['type_w'], 'L0_tok_gamma': _L0_tok_in['gamma'], 'L0_tok_beta': _L0_tok_in['beta'], 'L0_attn_Wq': _L0_attn_in['Wq'], 'L0_attn_bq': _L0_attn_in['bq'], 'L0_attn_Wk': _L0_attn_in['Wk'], 'L0_attn_bk': _L0_attn_in['bk'], 'L0_attn_Wv': _L0_attn_in['Wv'], 'L0_attn_bv': _L0_attn_in['bv'], 'L0_attn_Wout': _L0_attn_in['Wout'], 'L0_attn_bout': _L0_attn_in['bout'], 'L0_ffn_W1': _L0_ffn_in['W1'], 'L0_ffn_b1': _L0_ffn_in['b1'], 'L0_ffn_W2': _L0_ffn_in['W2'], 'L0_ffn_b2': _L0_ffn_in['b2'], 'L0_ffn_Wr': _L0_ffn_in['Wr'], 'L0_ffn_br': _L0_ffn_in['br'], 'L1_attn_qkv_w': _L1_attn_in['qkv_w'], 'L1_attn_qkv_b': _L1_attn_in['qkv_b'], 'L1_attn_out_w': _L1_attn_in['out_w'], 'L1_attn_out_b': _L1_attn_in['out_b'], 'L1_attn_rel_pos_emb': _L1_attn_in['rel_pos_emb'], 'L1_ffn_weights_in': _L1_ffn_in['weights_in'], 'L1_ffn_weights_out': _L1_ffn_in['weights_out']}

def reference(x, mask_BS_i1_0, L0_tok_tok_w, L0_tok_pos_w, L0_tok_type_w, L0_tok_gamma, L0_tok_beta, L0_attn_Wq, L0_attn_bq, L0_attn_Wk, L0_attn_bk, L0_attn_Wv, L0_attn_bv, L0_attn_Wout, L0_attn_bout, L0_ffn_W1, L0_ffn_b1, L0_ffn_W2, L0_ffn_b2, L0_ffn_Wr, L0_ffn_br, L1_attn_qkv_w, L1_attn_qkv_b, L1_attn_out_w, L1_attn_out_b, L1_attn_rel_pos_emb, L1_ffn_weights_in, L1_ffn_weights_out):
    import jax
    import jax.numpy as jnp

    def _L0_tok_ref(input_ids, token_type_ids, tok_w, pos_w, type_w, gamma, beta):
        import jax, jax.numpy as jnp
        import numpy as np
        VOCAB = 30522
        HIDDEN = 192
        MAX_POS = 128
        TYPE_VOCAB = 2
        EPS = 1e-05
        S = input_ids.shape[-1]
        emb = tok_w[input_ids] + pos_w[jnp.arange(S)] + type_w[token_type_ids]
        mean = jnp.mean(emb, axis=-1, keepdims=True)
        var = jnp.mean(jnp.square(emb - mean), axis=-1, keepdims=True)
        out = (emb - mean) * gamma * jax.lax.rsqrt(var + EPS) + beta
        return out

    def _L0_attn_ref(x, Wq, bq, Wk, bk, Wv, bv, Wout, bout):
        import jax, jax.numpy as jnp
        import numpy as np
        SEQ, BATCH, EMBED = (512, 4, 192)
        NUM_HEADS = 12
        HEAD_DIM = EMBED // NUM_HEADS
        SCALING = HEAD_DIM ** (-0.5)
        T, B, E = x.shape
        H, Dh = (NUM_HEADS, HEAD_DIM)
        q = (x @ Wq.T + bq) * SCALING
        k = x @ Wk.T + bk
        v = x @ Wv.T + bv
        q = q.reshape(T, B * H, Dh).transpose(1, 0, 2)
        k = k.reshape(T, B * H, Dh).transpose(1, 0, 2)
        v = v.reshape(T, B * H, Dh).transpose(1, 0, 2)
        scores = jnp.einsum('bqd,bkd->bqk', q, k)
        probs = jax.nn.softmax(scores.astype(jnp.float32), axis=-1).astype(scores.dtype)
        attn = jnp.einsum('bqk,bkd->bqd', probs, v)
        attn = attn.transpose(1, 0, 2).reshape(T, B, E)
        return attn @ Wout.T + bout

    def _L0_ffn_ref(x, W1, b1, W2, b2, Wr, br):
        import jax, jax.numpy as jnp
        import numpy as np
        E = 8
        K = 2
        D = 192
        I = 768
        B, S = (2, 512)
        Bv, Sv, Dv = x.shape
        xf = x.reshape(-1, Dv)
        logits = xf @ Wr + br
        gates = jax.nn.softmax(logits, axis=-1)
        top_g, top_i = jax.lax.top_k(gates, K)
        out = jnp.zeros_like(xf)
        for e in range(E):
            w_e = jnp.sum(top_g * (top_i == e), axis=-1)
            h = jax.nn.gelu(xf @ W1[e] + b1[e], approximate=False)
            y = h @ W2[e] + b2[e]
            out = out + w_e[:, None] * y
        return out.reshape(Bv, Sv, Dv)

    def _L1_attn_ref(x, qkv_w, qkv_b, out_w, out_b, rel_pos_emb):
        import jax, jax.numpy as jnp
        import numpy as np
        D_MODEL = 192
        NHEAD = 12
        HEAD_DIM = D_MODEL // NHEAD
        MAX_REL = 16
        B, T = (4, 256)
        Bx, Tx, _ = x.shape
        scale = HEAD_DIM ** (-0.5)
        qkv = x @ qkv_w.T + qkv_b
        qkv = qkv.reshape(Bx, Tx, 3, NHEAD, HEAD_DIM)
        q = qkv[:, :, 0].transpose(0, 2, 1, 3)
        k = qkv[:, :, 1].transpose(0, 2, 1, 3)
        v = qkv[:, :, 2].transpose(0, 2, 1, 3)
        attn_scores = jnp.einsum('bhtd,bhsd->bhts', q, k)
        rng = jnp.arange(Tx)
        rel_pos = jnp.clip(rng[None, :] - rng[:, None], -MAX_REL, MAX_REL) + MAX_REL
        rel_emb = rel_pos_emb[rel_pos]
        rel_scores = jnp.einsum('bhtd,tsd->bhts', q, rel_emb)
        attn = jax.nn.softmax((attn_scores + rel_scores) * scale, axis=-1)
        out = jnp.einsum('bhts,bhsd->bhtd', attn, v)
        out = out.transpose(0, 2, 1, 3).reshape(Bx, Tx, D_MODEL)
        return out @ out_w.T + out_b

    def _L1_ffn_ref(inputs, weights_in, weights_out):
        import jax, jax.numpy as jnp
        import numpy as np
        DEPTH = 11

        def _fff_forward(inputs, weights_in, weights_out, depth=DEPTH):
            B, S, _ = inputs.shape
            n_nodes = weights_in.shape[0]
            max_index = n_nodes - 1
            all_logits = jnp.einsum('bsd,nd->bsn', inputs, weights_in)

            def step(prev_idx, _):
                sel = jnp.clip(prev_idx, 0, max_index)
                logits = jnp.take_along_axis(all_logits, sel[..., None], axis=-1)[..., 0]
                new_idx = jnp.clip(2 * sel + 1 + (logits > 0).astype(sel.dtype), 0, max_index)
                return (new_idx, (logits, new_idx))
            idx0 = jnp.zeros((B, S), dtype=jnp.int32)
            _, (logits_seq, idx_seq) = jax.lax.scan(step, idx0, None, length=depth - 1)
            logits = jnp.concatenate([jnp.zeros((1, B, S), all_logits.dtype), logits_seq], axis=0)
            node_idx = jnp.concatenate([idx0[None], idx_seq], axis=0)
            act = jax.nn.gelu(logits, approximate=False)
            onehot = jax.nn.one_hot(node_idx, n_nodes, dtype=act.dtype)
            coeff = jnp.einsum('dbs,dbsn->bsn', act, onehot)
            return jnp.einsum('bsn,nd->bsd', coeff, weights_out)
        return _fff_forward(inputs, weights_in, weights_out)
    h = _L0_tok_ref(x, mask_BS_i1_0, L0_tok_tok_w, L0_tok_pos_w, L0_tok_type_w, L0_tok_gamma, L0_tok_beta)
    h = h + _L0_attn_ref(_layernorm(h, axis=-1), L0_attn_Wq, L0_attn_bq, L0_attn_Wk, L0_attn_bk, L0_attn_Wv, L0_attn_bv, L0_attn_Wout, L0_attn_bout)
    h = h + _L0_ffn_ref(_layernorm(h, axis=-1), L0_ffn_W1, L0_ffn_b1, L0_ffn_W2, L0_ffn_b2, L0_ffn_Wr, L0_ffn_br)
    h = h + _L1_attn_ref(_layernorm(h, axis=-1), L1_attn_qkv_w, L1_attn_qkv_b, L1_attn_out_w, L1_attn_out_b, L1_attn_rel_pos_emb)
    h = h + _L1_ffn_ref(_layernorm(h, axis=-1), L1_ffn_weights_in, L1_ffn_weights_out)
    return h

_drawn_inputs = setup_inputs


def setup_inputs(seed=0):
    import zlib

    import numpy as np

    out = dict(_drawn_inputs(seed))
    spreads = {'L0_tok_gamma': (1.0, 0.2),
     'L0_tok_beta': (0.0, 0.1),
     'L0_ffn_b1': (0.0, 0.1),
     'L0_ffn_b2': (0.0, 0.1),
     'L0_ffn_br': (0.0, 0.1)}
    factors = {'L0_attn_Wq': 8.0,
     'L0_attn_bq': 8.0,
     'L0_attn_Wk': 8.0,
     'L0_attn_bk': 8.0,
     'L1_attn_rel_pos_emb': 3.076}
    for name, (base, spread) in spreads.items():
        noise = np.random.default_rng([zlib.crc32(name.encode()), seed]).standard_normal(out[name].shape)
        drawn = base * np.exp(spread * noise) if base else spread * noise
        out[name] = jnp.asarray(drawn.astype(out[name].dtype))
    for name, factor in factors.items():
        out[name] = (out[name] * factor).astype(out[name].dtype)
    return out
```

```python
from contextlib import ExitStack

import numpy as np

import concourse.bass as bass
from concourse import mybir

F32 = mybir.dt.float32
I32 = mybir.dt.int32
U32 = mybir.dt.uint32
ALU = mybir.AluOpType
ACT = mybir.ActivationFunctionType
AX = mybir.AxisListType

T, B = 64, 128
D = 192
D1 = D - 128
NT = T * B // 128
H, DH = 12, 16
G, A = 4, 3
E, TOPK, I = 8, 2, 768
NI = I // 128
BLK = 256
NBLK = T * B * TOPK // BLK + E
REL = 33
MAXREL = 16
LPAD = B - 1 - MAXREL
ROWW = (2 * B - 1) * H
NODES = 21
LAST = NODES - 1
EPS = 1e-5
SCALE = DH ** -0.5


class Chain:

    def __init__(self, eng, sem, per):
        self.eng, self.sem, self.per, self.at, self.base = eng, sem, per, 0, 0

    def start(self, i):
        self.base, self.at = i * self.per, 0

    def link(self, ins):
        self.at += 1
        ins.then_inc(self.sem, 1)
        self.eng.wait_ge(self.sem, self.base + self.at)

    def end(self):
        assert self.at == self.per, (self.at, self.per)


def settle(eng, spare):
    eng.sem_inc(spare, 1)


def tower(nc, dbg, ids_h, typ_h, tok_w, pos_w, type_w, gamma, beta,
          wqk0, wv0, wo0, w1h, w2h, b2h, wr, wqk1, wv1, wo1, relblk, rel32, win, wout, out):
    h1_d = nc.dram_tensor("h1_d", [T * B, D], F32, **dbg).ap()
    xs_d = nc.dram_tensor("xs_d", [NBLK * BLK, D], F32, **dbg).ap()
    ys_d = nc.dram_tensor("ys_d", [NBLK * BLK, D], F32, **dbg).ap()
    rel_d = [nc.dram_tensor(f"rel_d{p}", [B, ROWW], F32).ap() for p in range(2)]

    with ExitStack() as ctx:
        def sb(name, shape, dt=F32):
            return ctx.enter_context(nc.sbuf_tensor(name, shape, dt))

        def two(name, shape, dt=F32):
            return [sb(f"{name}{p}", shape, dt) for p in range(2)]

        def sem(name):
            return ctx.enter_context(nc.semaphore(name))

        ps_s = ctx.enter_context(nc.psum_tensor("ps_s", [128, G, 512], F32))
        ps_t = ctx.enter_context(nc.psum_tensor("ps_t", [128, 512], F32))
        ps_q = ctx.enter_context(nc.psum_tensor("ps_q", [128, 512], F32))
        ps_k = ctx.enter_context(nc.psum_tensor("ps_k", [128, 512], F32))
        ps_v = ctx.enter_context(nc.psum_tensor("ps_v", [128, 512], F32))
        ps_pt = [ps_q, ps_k]

        ident = sb("ident", [128, 128])
        tri = sb("tri", [128, 128])
        ones = sb("ones", [128, 128])
        mhalf = sb("mhalf", [128, NT])
        epsc = sb("epsc", [128, 1])
        zrow = sb("zrow", [128, LPAD * H])
        gam = sb("gam", [128, D])
        bet = sb("bet", [128, D])
        typ0 = sb("typ0", [128, D])
        typ1 = sb("typ1", [128, D])
        ids = sb("ids", [128, NT], I32)
        typi = sb("typi", [128, NT], I32)
        typf = sb("typf", [128, NT])
        typn = sb("typn", [128, NT])
        relw = sb("relw", [128, G * REL])
        rel32s = sb("rel32s", [128, 1])

        def weights(name, n):
            return sb(name + "_c0", [128, n]), sb(name + "_c1", [D1 + 1, n])

        qk_w = [weights("wqk0", 2 * A * 128), weights("wqk1", 2 * A * 128)]
        v_w = [weights("wv0", D), weights("wv1", D)]
        o_w = [weights("wo0", D), weights("wo1", D)]
        r_w = weights("wr", E)
        in_w = (sb("win_c0", [128, NODES]), sb("win_c1", [D1, NODES]))

        hres = sb("hres", [128, NT, D])
        stats = sb("stats", [128, NT, 6])
        mvar = sb("mvar", [128, NT, 2])
        rstd = sb("rstd", [128, NT])
        gat = sb("gat", [128, NT, E])
        wk = [sb(f"wk{k}", [128, NT]) for k in range(TOPK)]
        posi = [sb(f"posi{k}", [128, NT], U32) for k in range(TOPK)]
        flog = sb("flog", [128, NT, NODES])

        idx = two("idx", [128, 1], U32)
        idxb = two("idxb", [128, 1], U32)
        tok = two("tok", [128, D])
        posb = two("posb", [128, D])
        emb = two("emb", [128, D])
        st6 = two("st6", [128, 6])
        mv = two("mv", [128, 2])
        veps = two("veps", [128, 1])
        rs = two("rs", [128, 1])
        rs2 = two("rs2", [128, 1])
        res = two("res", [128, D])
        xn = two("xn", [128, D])
        xT0 = two("xT0", [128, 128])
        xT1 = two("xT1", [D1 + 1, 128])
        qT = two("qT", [128, A, 128])
        kT = two("kT", [128, A, 128])
        vv = two("vv", [128, 2 * (H // 2) * 2 * (DH + 1)])
        score = two("score", [128, G, A, 128])
        mx = two("mx", [128, H])
        prob = two("prob", [128, H * 128])
        probT = two("probT", [128, H * 128])
        rden = two("rden", [128, H])
        on = two("on", [128, D])
        oT0 = two("oT0", [128, 128])
        oT1 = two("oT1", [D1 + 1, 128])
        hout = two("hout", [128, D])
        rpad = two("rpad", [128, LPAD + REL, H])
        relb = two("relb", [128, B, H])
        cT = two("cT", [NODES, 128])

        w1 = [(score[p][:].rearrange("p g a k -> p (g a k)")[:, 0:I],
               score[p][:].rearrange("p g a k -> p (g a k)")[0:D1 + 1, I:2 * I]) for p in range(2)]
        w2 = [probT[p][:, 0:NI * D].rearrange("p (c d) -> p c d", c=NI) for p in range(2)]
        hT = [prob[p][:].rearrange("p (c t) -> p c t", c=NI) for p in range(2)]
        xs = [relb[p][:].rearrange("p s h -> p (s h)")[:, 0:2 * D].rearrange("p (s d) -> p s d", s=2)
              for p in range(2)]
        ys = [rpad[p][:].rearrange("p s h -> p (s h)")[:, 0:2 * D].rearrange("p (s d) -> p s d", s=2)
              for p in range(2)]
        xsT0 = [qT[p][:].rearrange("p a t -> p (a t)")[:, 0:BLK] for p in range(2)]
        xsT1 = [kT[p][:].rearrange("p a t -> p (a t)")[0:D1 + 1, 0:BLK] for p in range(2)]
        b2s = [tok[p][:] for p in range(2)]
        big = sb("big", [128, 6, NT * E])
        small = sb("small", [128, 12, NT])
        etab = sb("etab", [128, NBLK])
        etabi = sb("etabi", [128, NBLK], I32)
        cnt = sb("cnt", [128, 6, E])
        cnti = sb("cnti", [128, E], I32)
        etmp = sb("etmp", [128, NBLK, E])
        fg = relb[0][:].rearrange("p s h -> p (s h)")[:, 0:NT * NODES].rearrange("p (t n) -> p t n", n=NODES)
        fs = relb[1][:].rearrange("p s h -> p (s h)")[:, 0:NT * NODES].rearrange("p (t n) -> p t n", n=NODES)
        fr = rpad[0][:].rearrange("p s h -> p (s h)")[:, 0:NT * NODES].rearrange("p (t n) -> p t n", n=NODES)
        fc = sb("fc", [128, NT, 32])
        wout4 = sb("wout4", [128, D])

        ctx2 = ExitStack()
        dma = {}

        def dsem(name):
            dma[name] = sem("ld_" + name)
            return dma[name]

        const_ld = dsem("const")
        N_CONST = 28
        pool_c = sem("pool_c")
        const_ok = sem("const_ok")
        zero_ok = sem("zero_ok")
        xs_zero = sem("xs_zero")
        rel_zero = sem("rel_zero")
        NAMES = ("xn_ok", "xT_ps", "xT_sb", "q_ps", "q_sb", "k_ps", "k_sb", "v_ps", "v_sb", "s_ps", "s_sub",
                 "p_sb", "pt_ps", "pt_sb", "o_ps", "o_sb", "oT_ps", "oT_sb", "y_ps", "y_ok", "mv_ok",
                 "rs_ok", "dve", "idx_ok", "pool", "h_ok")
        L = [{n: sem(f"L{l}_{n}") for n in NAMES} for l in range(2)]
        tok_ld = [sem(f"tok_ld{p}") for p in range(2)]
        pos_ld = [sem(f"pos_ld{p}") for p in range(2)]
        h1_st = [sem(f"h1_st{p}") for p in range(2)]
        tok_free = sem("tok_free")
        dve_c = sem("dve_c")
        spare = sem("spare")
        rel_st = [sem(f"rel_st{p}") for p in range(2)]
        rel_ld = [sem(f"rel_ld{p}") for p in range(2)]
        y2_ld = [sem(f"y2_ld{p}") for p in range(2)]
        for n in ("r_ps", "r_sb", "pad_ok", "fT_ps", "fT_sb", "f_ps", "f_sb"):
            L[1][n] = sem("L1_" + n)

        block_a = ctx2.enter_context(nc.Block())
        def bcast_rows(ap, n):
            return ap.to_broadcast([n, ap.shape[1]])

        @block_a.sync
        def _(sp):
            loads = [(ids, ids_h), (typi, typ_h), (relw, relblk), (rel32s, rel32)]
            loads += [(wout4[32 * k:32 * k + NODES], wout) for k in range(4)]
            for (c0, c1), src in [(qk_w[0], wqk0), (v_w[0], wv0), (o_w[0], wo0), (r_w, wr),
                                  (qk_w[1], wqk1), (v_w[1], wv1), (o_w[1], wo1), (in_w, win)]:
                loads += [(c0, src[0:128, :]), (c1, src[128:, :])]
            for dst, src in loads:
                sp.dma_start(dst[:], src).then_inc(const_ld, 16)
            for dst, src in [(gam, gamma), (bet, beta), (typ0, type_w[0:1, :]), (typ1, type_w[1:2, :])]:
                sp.dma_start(dst[:], src.to_broadcast([128, D])).then_inc(const_ld, 16)
            assert len(loads) + 4 == N_CONST, len(loads)
            sp.wait_ge(zero_ok, 1)
            for p in range(2):
                sp.dma_start(rel_d[p][:, (LPAD + REL) * H:], zrow[:]).then_inc(rel_zero, 16)
            zr = xs_d.rearrange("(n p r) d -> n p (r d)", p=128, r=6)
            for n in range(zr.shape[0]):
                sp.dma_start(zr[n], zrow[:, 0:6 * D]).then_inc(xs_zero, 16)
            S = L[0]
            h1_v = h1_d.rearrange("(t n c) d -> n c t d", n=NT, c=2)
            with sp.Fori(0, NT // 2) as i:
                for p in range(2):
                    n = 2 * i + p
                    sp.wait_ge(tok_free, n + 1)
                    for c in range(2):
                        sp.dma_start(posb[p][64 * c:64 * c + 64, :],
                                     pos_w[bass.ds(2 * n + c, 1), :].to_broadcast([64, D])).then_inc(pos_ld[p], 16)
                for p in range(2):
                    n = 2 * i + p
                    sp.wait_ge(S["y_ok"], n + 1)
                    for c in range(2):
                        sp.dma_start(h1_v[bass.ds(n, 1), c].rearrange("a t d -> (a t) d"),
                                     hout[p][64 * c:64 * c + 64, :]).then_inc(h1_st[p], 16)
            for p in range(2):
                sp.wait_ge(h1_st[p], 32 * (NT // 2))

        @block_a.gpsimd
        def _(pool):
            S = L[0]
            pool.memset(zrow[:], 0.0).then_inc(zero_ok, 1)
            pool.memset(ident[:], 0.0).then_inc(pool_c, 1)
            pool.memset(tri[:], 1.0).then_inc(pool_c, 1)
            pool.memset(ones[:], 1.0).then_inc(const_ok, 1)
            pool.memset(mhalf[:], -0.5).then_inc(const_ok, 1)
            pool.memset(epsc[:], EPS).then_inc(pool_c, 1)
            pool.wait_ge(pool_c, 3)
            pool.affine_select(out=ident[:], in_=ident[:], compare_op=ALU.not_equal, fill=1.0, base=0,
                               pattern=[[-1, 128]], channel_multiplier=1).then_inc(const_ok, 1)
            pool.affine_select(out=tri[:], in_=tri[:], compare_op=ALU.is_gt, fill=0.0, base=0,
                               pattern=[[1, 128]], channel_multiplier=-1).then_inc(const_ok, 1)
            pool.wait_ge(const_ld, 16 * N_CONST)
            with pool.Fori(0, NT // 2) as i:
                for p in range(2):
                    n = 2 * i + p
                    pool.wait_ge(tok_ld[p], 16 * i)
                    pool.tensor_copy(idx[p][:], ids[:, bass.ds(n, 1)]).then_inc(S["idx_ok"], 1)
                    pool.wait_ge(S["idx_ok"], n + 1)
                    pool.wait_ge(tok_free, n + 1)
                    settle(pool, spare)
                    pool.indirect_dma_start(tok[p][:], None, tok_w,
                                            bass.IndirectOffsetOnAxis(ap=idx[p][:], axis=0)).then_inc(tok_ld[p], 16)
                for r in range(2):
                    for p in range(2):
                        n = 2 * i + p
                        pool.wait_ge(S["mv_ok"], 4 * i + 2 * r + p + 1)
                        pool.tensor_tensor(veps[p][:], mv[p][:, 1:2], epsc[:], ALU.add).then_inc(S["pool"], 1)
                        pool.wait_ge(S["pool"], 4 * i + 2 * r + p + 1)
                        pool.tensor_tensor(rs[p][:] if r == 0 else rs2[p][:], veps[p][:], mhalf[:, 0:1],
                                           ALU.pow).then_inc(S["rs_ok"], 1)

        def act_attention(act, l, keys, i, stage, p):
            S = L[l]
            n = 2 * i + p
            npt = 2 if l == 0 else 3
            if stage == "xT":
                act.wait_ge(S["xT_ps"], n + 1)
                act.activation(xT0[p][:], ps_t[:, 0:128], ACT.Copy)
                act.activation(xT1[p][0:D1, :], ps_t[0:D1, 128:256], ACT.Copy).then_inc(S["xT_sb"], 1)
            if stage == "qkv":
                act.wait_ge(S["q_ps"], n + 1)
                act.activation(qT[p][:], ps_q[:, 0:A * 128].rearrange("p (a t) -> p a t", a=A),
                               ACT.Copy).then_inc(S["q_sb"], 1)
                act.wait_ge(S["k_ps"], n + 1)
                if l == 0:
                    act.activation(kT[p][:], ps_k[:, 0:A * 128].rearrange("p (a t) -> p a t", a=A),
                                   ACT.Copy).then_inc(S["k_sb"], 1)
                else:
                    act.activation(kT[p][:], ps_k[:, 0:A * 128].rearrange("p (a t) -> p a t", a=A),
                                   ACT.Identity, bias=rel32s[:, 0:1]).then_inc(S["k_sb"], 1)
                act.wait_ge(S["v_ps"], n + 1)
                if l == 0:
                    vb = vv[p][:].rearrange("p (c r s e) -> p c r s e", c=2, r=H // 2, s=2)
                    pv = ps_v[:, 0:2 * D].rearrange("p (w r s e) -> p w r s e", w=2, r=H // 2, s=2)
                    for c in range(2):
                        for s in range(2):
                            ins = act.activation(vb[64 * s:64 * s + 64, c, :, s, 0:DH],
                                                 pv[64 * s:64 * s + 64, 0 if s == c else 1, :, s, :], ACT.Copy)
                    ins.then_inc(S["v_sb"], 1)
                else:
                    vj = vv[p][:, 0:H * (DH + 1)].rearrange("p (h e) -> p h e", h=H)
                    act.activation(vj[:, :, 0:DH], ps_v[:, 0:D].rearrange("p (h e) -> p h e", h=H),
                                   ACT.Copy).then_inc(S["v_sb"], 1)
            if stage == "exp":
                act.wait_ge(S["s_sub"], n + 1)
                act.activation(prob[p][:, 0:H * keys].rearrange("p (g a k) -> p g a k", g=G, a=A),
                               score[p][:, :, :, 0:keys], ACT.Exp, scale=SCALE).then_inc(S["p_sb"], 1)
            if stage == "pt":
                w = 384 if l == 0 else 512
                for u in range(npt):
                    act.wait_ge(S["pt_ps"], n * npt + u + 1)
                    act.activation(probT[p][:, u * w:(u + 1) * w], ps_pt[(p * npt + u) % 2][:, 0:w],
                                   ACT.Copy).then_inc(S["pt_sb"], 1)
            if stage == "oT":
                act.wait_ge(S["oT_ps"], n + 1)
                act.activation(oT0[p][:], ps_t[:, 0:128], ACT.Copy)
                act.activation(oT1[p][0:D1, :], ps_t[0:D1, 128:256], ACT.Copy).then_inc(S["oT_sb"], 1)

        def pe_transpose(pe, dst, src, width=D):
            pe.transpose(dst[:, 0:128], src[:, 0:128], ident[:])
            return pe.transpose(dst[0:width - 128, 128:256], src[:, 128:width], ident[:])

        def pe_project(pe, dst, x0, x1, w, lo, hi):
            pe.matmul(dst, x0, w[0][:, lo:hi], start=True, stop=False)
            return pe.matmul(dst, x1, w[1][:, lo:hi], start=False, stop=True)

        def pe_attention(pe, l, keys, i, stage, p):
            S = L[l]
            n = 2 * i + p
            npt = 2 if l == 0 else 3
            if stage == "xT":
                pe.wait_ge(S["xn_ok"], n + 1)
                pe.wait_ge(S["xT_sb" if p else ("oT_sb" if l == 0 else "f_sb")], n)
                pe_transpose(pe, ps_t, xn[p][:]).then_inc(S["xT_ps"], 1)
            if stage == "qkv":
                pe.wait_ge(S["xT_sb"], n + 1)
                if p:
                    pe.wait_ge(S["q_sb"], n)
                else:
                    pe.wait_ge(S["pt_sb"], n * npt)
                for side, dst in enumerate((ps_q, ps_k)):
                    if p and side:
                        pe.wait_ge(S["k_sb"], n)
                    for a in range(A):
                        o = (side * A + a) * 128
                        pe.matmul(dst[:, a * 128:a * 128 + 128], qk_w[l][0][:, o:o + 128], xT0[p][:],
                                  start=True, stop=False)
                        last = pe.matmul(dst[:, a * 128:a * 128 + 128], qk_w[l][1][:, o:o + 128], xT1[p][:],
                                         start=False, stop=True)
                    last.then_inc(S["k_ps" if side else "q_ps"], 1)
                pe.wait_ge(S["v_sb" if p else "y_ok"], n)
                last = pe_project(pe, ps_v[:, 0:D], xT0[p][:], xT1[p][:], v_w[l], 0, D)
                if l == 0:
                    for c in range(2):
                        dst = ps_v[64 * c:64 * c + 64, D:2 * D]
                        q = 64 * (1 - c)
                        last = pe_project(pe, dst, xT0[p][:, q:q + 64], xT1[p][:, q:q + 64], v_w[l], 0, D)
                last.then_inc(S["v_ps"], 1)
            if stage == "s":
                pe.wait_ge(S["q_sb"], n + 1)
                pe.wait_ge(S["k_sb"], n + 1)
                pe.wait_ge(S["s_sub"], n)
                for a in range(A):
                    for g in range(G):
                        q = slice(32 * g, 32 * g + DH)
                        for c in range(128 // keys):
                            t = slice(keys * c, keys * c + keys)
                            last = pe.matmul(ps_s[t, g, a * keys:a * keys + keys], qT[p][q, a, t], kT[p][q, a, t],
                                             start=True, stop=True)
                last.then_inc(S["s_ps"], 1)
            if stage == "pt":
                pe.wait_ge(S["p_sb"], n + 1)
                per = 3 if l == 0 else 4
                for u in range(npt):
                    at = p * npt + u
                    bank = ps_pt[at % 2]
                    if at < 2:
                        pe.wait_ge(S["q_sb" if at == 0 else "k_sb"], 2 * i + 2)
                    else:
                        pe.wait_ge(S["pt_sb"], n * npt + u - 1)
                    for j in range(per):
                        o = (u * per + j) * 128
                        last = pe.transpose(bank[:, j * 128:j * 128 + 128], prob[p][:, o:o + 128], ident[:])
                    last.then_inc(S["pt_ps"], 1)
            if stage == "o":
                pe.wait_ge(S["pt_sb"], (n + 1) * npt)
                if p:
                    pe.wait_ge(S["o_sb"], n)
                else:
                    pe.wait_ge(S["v_sb"], n + 2)
                W = DH + 1
                if l == 0:
                    for r in range(H // 2):
                        for c in range(2):
                            q = slice(64 * c, 64 * c + 64)
                            o = (c * (H // 2) + r) * 2 * W
                            last = pe.matmul(ps_v[q, r * 2 * W:(r + 1) * 2 * W],
                                             probT[p][:, r * 128 + 64 * c:r * 128 + 64 * c + 64],
                                             vv[p][:, o:o + 2 * W], start=True, stop=True)
                else:
                    for h in range(H):
                        last = pe.matmul(ps_v[:, h * W:(h + 1) * W], probT[p][:, h * 128:h * 128 + 128],
                                         vv[p][:, h * W:(h + 1) * W], start=True, stop=True)
                last.then_inc(S["o_ps"], 1)
            if stage == "oT":
                pe.wait_ge(S["o_sb"], n + 1)
                if p:
                    pe.wait_ge(S["oT_sb"], n)
                elif l == 1:
                    pe.wait_ge(S["r_sb"], n + 2)
                pe_transpose(pe, ps_t, on[p][:]).then_inc(S["oT_ps"], 1)
            if stage == "y":
                pe.wait_ge(S["oT_sb"], n + 1)
                pe.wait_ge(S["y_ok" if p else "o_sb"], n if p else n + 2)
                pe_project(pe, ps_v[:, 0:D], oT0[p][:], oT1[p][:], o_w[l], 0, D).then_inc(S["y_ps"], 1)

        def dve_softmax(dve, ch, l, keys, i, stage, p):
            S = L[l]
            n = 2 * i + p
            sc = score[p][:, :, :, 0:keys]
            psv = ps_s[:, :, 0:A * keys].rearrange("p g (a k) -> p g a k", a=A)
            if stage == "s":
                dve.wait_ge(S["s_ps"], n + 1)
                if l == 0:
                    src = psv
                else:
                    dve.wait_ge(rel_ld[p], 16 * i + 16)
                    for g in range(G):
                        ins = dve.tensor_tensor(sc[:, g], psv[:, g],
                                                relb[p][:, :, 3 * g:3 * g + 3].rearrange("p s a -> p a s"), ALU.add)
                        if g < G - 1:
                            ins.then_inc(S["dve"], 1)
                            ch.at += 1
                        else:
                            ch.link(ins)
                    src = sc
                ch.link(dve.tensor_reduce(mx[p][:].rearrange("p (g a) -> p g a", g=G), src, AX.X, ALU.max))
                m4 = mx[p][:].rearrange("p (g a o) -> p g a o", g=G, o=1).to_broadcast([128, G, A, keys])
                dve.tensor_tensor(sc, src, m4, ALU.subtract).then_inc(S["s_sub"], 1)
            if stage == "o":
                dve.wait_ge(S["o_ps"], n + 1)
                o = ps_v[:, 0:H * (DH + 1)].rearrange("p (h e) -> p h e", h=H)
                ch.link(dve.reciprocal(rden[p][:].rearrange("p (h o) -> p h o", o=1), o[:, :, DH:DH + 1]))
                dve.tensor_tensor(on[p][:].rearrange("p (h e) -> p h e", h=H), o[:, :, 0:DH],
                                  rden[p][:].rearrange("p (h o) -> p h o", o=1).to_broadcast([128, H, DH]),
                                  ALU.mult).then_inc(S["o_sb"], 1)

        @block_a.tensor
        def _(pe):
            pe.wait_ge(const_ld, 16 * N_CONST)
            pe.wait_ge(const_ok, 6)
            with pe.Fori(0, NT // 2) as i:
                for stage in ("xT", "qkv", "s", "pt", "o", "oT", "y"):
                    for p in range(2):
                        pe_attention(pe, 0, 64, i, stage, p)

        @block_a.scalar
        def _(act):
            act.wait_ge(const_ok, 6)
            act.wait_ge(const_ld, 16 * N_CONST)
            with act.Fori(0, NT // 2) as i:
                for stage in ("xT", "qkv", "exp", "pt", "oT"):
                    for p in range(2):
                        act_attention(act, 0, 64, i, stage, p)

        @block_a.vector
        def _(dve):
            S = L[0]
            for p in range(2):
                ins = dve.memset(xT1[p][D1:D1 + 1, :], 1.0)
                ins = dve.memset(oT1[p][D1:D1 + 1, :], 1.0)
                dve.memset(vv[p][:], 0.0).then_inc(dve_c, 1)
            dve.wait_ge(dve_c, 2)
            for p in range(2):
                vb = vv[p][:].rearrange("p (c r s e) -> p c r s e", c=2, r=H // 2, s=2)
                for s in range(2):
                    ins = dve.memset(vb[64 * s:64 * s + 64, :, :, s, DH:DH + 1], 1.0)
                ins.then_inc(const_ok, 1)
            dve.wait_ge(const_ld, 16 * N_CONST)
            dve.tensor_copy(typf[:], typi[:]).then_inc(dve_c, 1)
            dve.wait_ge(dve_c, 3)
            dve.tensor_scalar(typn[:], typf[:], -1.0, 1.0, ALU.mult, ALU.add).then_inc(dve_c, 1)
            for g in range(G):
                q = slice(32 * g, 32 * g + 32)
                ins = dve.tensor_scalar(relw[q, g * REL:(g + 1) * REL], relw[q, g * REL:(g + 1) * REL],
                                        rel32s[q, 0:1], None, ALU.subtract)
            ins.then_inc(dve_c, 1)
            dve.wait_ge(dve_c, 5)
            dve.sem_inc(tok_free, 2)
            ch = Chain(dve, S["dve"], 2 * 9)
            with dve.Fori(0, NT // 2) as i:
                ch.start(i)
                for p in range(2):
                    n = 2 * i + p
                    dve.wait_ge(tok_ld[p], 16 * i + 16)
                    dve.wait_ge(pos_ld[p], 32 * i + 32)
                    ch.link(dve.tensor_tensor(emb[p][:], tok[p][:], posb[p][:], ALU.add))
                    ch.link(dve.scalar_tensor_tensor(emb[p][:], typ0[:], typn[:, bass.ds(n, 1)], emb[p][:],
                                                     ALU.mult, ALU.add))
                    ch.link(dve.scalar_tensor_tensor(emb[p][:], typ1[:], typf[:, bass.ds(n, 1)], emb[p][:],
                                                     ALU.mult, ALU.add))
                    dve.sem_inc(tok_free, 1)
                    ch.link(dve.bn_stats(st6[p][:], emb[p][:]))
                    settle(dve, spare)
                    dve.bn_aggr(mv[p][:], st6[p][:]).then_inc(S["mv_ok"], 1)
                for p in range(2):
                    dve.wait_ge(S["rs_ok"], 4 * i + p + 1)
                    dve.wait_ge(S["mv_ok"], 4 * i + p + 1)
                    ch.link(dve.scalar_tensor_tensor(emb[p][:], emb[p][:], mv[p][:, 0:1], gam[:],
                                                     ALU.subtract, ALU.mult))
                    ch.link(dve.scalar_tensor_tensor(res[p][:], emb[p][:], rs[p][:, 0:1], bet[:],
                                                     ALU.mult, ALU.add))
                    ch.link(dve.bn_stats(st6[p][:], res[p][:]))
                    settle(dve, spare)
                    dve.bn_aggr(mv[p][:], st6[p][:]).then_inc(S["mv_ok"], 1)
                for p in range(2):
                    dve.wait_ge(S["rs_ok"], 4 * i + 2 + p + 1)
                    dve.wait_ge(S["mv_ok"], 4 * i + 2 + p + 1)
                    dve.tensor_scalar(xn[p][:], res[p][:], mv[p][:, 0:1], rs2[p][:, 0:1],
                                      ALU.subtract, ALU.mult).then_inc(S["xn_ok"], 1)
                for stage in ("s", "o"):
                    for p in range(2):
                        dve_softmax(dve, ch, 0, 64, i, stage, p)
                for p in range(2):
                    n = 2 * i + p
                    dve.wait_ge(S["y_ps"], n + 1)
                    dve.wait_ge(h1_st[p], 32 * i)
                    dve.tensor_tensor(hout[p][:], ps_v[:, 0:D], res[p][:], ALU.add).then_inc(S["y_ok"], 1)
                ch.end()

        ctx2.close()

        B_ = {n: sem("B_" + n) for n in ("ld", "st", "ag", "rs", "xn", "xT_ps", "xT_sb", "lg", "g_ex", "dve",
                                         "cnt_ps", "ready", "pool")}
        scat = [sem(f"scat{p}") for p in range(2)]
        with nc.Block() as block:
            @block.sync
            def _(sp):
                hv = h1_d.rearrange("(t b) d -> b t d", b=B)
                for c in range(4):
                    sp.dma_start(hres[:, 16 * c:16 * c + 16, :], hv[:, 16 * c:16 * c + 16, :]).then_inc(B_["ld"], 16)

            @block.gpsimd
            def _(pool):
                pool.iota(etabi[:], pattern=[[BLK, NBLK]], base=0, channel_multiplier=0).then_inc(B_["pool"], 1)
                pool.iota(cnti[:], pattern=[[-1, E]], base=E, channel_multiplier=0).then_inc(B_["pool"], 1)
                pool.wait_ge(B_["ag"], NT)
                pool.tensor_scalar(rstd[:], mvar[:, :, 1], EPS, None, ALU.add).then_inc(B_["pool"], 1)
                pool.wait_ge(B_["pool"], 3)
                pool.tensor_tensor(rstd[:], rstd[:], mhalf[:], ALU.pow).then_inc(B_["rs"], 1)

            @block.tensor
            def _(pe):
                with pe.Fori(0, NT // 2) as i:
                    for p in range(2):
                        n = 2 * i + p
                        pe.wait_ge(B_["xn"], n + 1)
                        pe.wait_ge(B_["xT_sb"], n)
                        pe_transpose(pe, ps_t, xn[p][:]).then_inc(B_["xT_ps"], 1)
                    for p in range(2):
                        n = 2 * i + p
                        pe.wait_ge(B_["xT_sb"], n + 1)
                        pe_project(pe, ps_q[:, bass.ds(n * E, E)], xT0[p][:], xT1[p][:], r_w, 0, E)\
                            .then_inc(B_["lg"], 1)
                pe.wait_ge(B_["ready"], 1)
                pe.matmul(ps_k[:], tri[:], big[:, 5, :], start=True, stop=True).then_inc(B_["cnt_ps"], 1)
                pe.matmul(ps_v[:], ones[:], big[:, 5, :], start=True, stop=True).then_inc(B_["cnt_ps"], 1)

            @block.scalar
            def _(act):
                with act.Fori(0, NT // 2) as i:
                    for p in range(2):
                        n = 2 * i + p
                        act.wait_ge(B_["xT_ps"], n + 1)
                        act.activation(xT0[p][:], ps_t[:, 0:128], ACT.Copy)
                        act.activation(xT1[p][0:D1, :], ps_t[0:D1, 128:256], ACT.Copy).then_inc(B_["xT_sb"], 1)
                act.wait_ge(B_["g_ex"], 1)
                act.activation(gat[:], gat[:], ACT.Exp).then_inc(B_["g_ex"], 1)

            @block.vector
            def _(dve):
                dve.wait_ge(B_["ld"], 64)
                with dve.Fori(0, NT // 8) as i:
                    for k in range(8):
                        n = 8 * i + k
                        dve.bn_stats(stats[:, bass.ds(n, 1), :], hres[:, bass.ds(n, 1), :]).then_inc(B_["st"], 1)
                dve.wait_ge(B_["st"], NT)
                for n in range(NT):
                    dve.bn_aggr(mvar[:, n, :], stats[:, n, :]).then_inc(B_["ag"], 1)
                dve.wait_ge(B_["ag"], NT)
                dve.wait_ge(B_["rs"], 1)
                with dve.Fori(0, NT // 2) as i:
                    for p in range(2):
                        n = 2 * i + p
                        dve.wait_ge(B_["xT_ps"], 2 * i)
                        dve.wait_ge(B_["rs"], 1)
                        dve.tensor_scalar(xn[p][:].rearrange("p (o d) -> p o d", o=1), hres[:, bass.ds(n, 1), :],
                                          mvar[:, bass.ds(n, 1), 0], rstd[:, bass.ds(n, 1)],
                                          ALU.subtract, ALU.mult).then_inc(B_["xn"], 1)
                ch = Chain(dve, B_["dve"], 1000)
                k = ch.link
                def flat(j):
                    return big[:, j, :].rearrange("p (t e) -> p t e", e=E)
                def col(j):
                    return small[:, j, :].rearrange("p (t o) -> p t o", o=1)
                def wide(ap):
                    return ap.to_broadcast([128, NT, E])
                rev = cnt[:, 0, :].rearrange("p (o e) -> p o e", o=1).to_broadcast([128, NT, E])
                dve.wait_ge(B_["pool"], 3)
                k(dve.tensor_copy(cnt[:, 0, :], cnti[:]))
                k(dve.tensor_copy(etab[:], etabi[:]))
                dve.wait_ge(B_["lg"], NT)
                lg = ps_q[:].rearrange("p (t e) -> p t e", e=E)
                k(dve.tensor_reduce(small[:, 0, :], lg, AX.X, ALU.max))
                dve.tensor_tensor(gat[:], lg, wide(col(0)), ALU.subtract).then_inc(B_["g_ex"], 1)
                dve.wait_ge(B_["g_ex"], 2)
                k(dve.tensor_reduce(small[:, 1, :], gat[:], AX.X, ALU.add))
                k(dve.reciprocal(small[:, 2, :], small[:, 1, :]))
                k(dve.tensor_tensor(gat[:], gat[:], wide(col(2)), ALU.mult))
                for r in range(TOPK):
                    k(dve.tensor_reduce(wk[r][:], gat[:], AX.X, ALU.max))
                    k(dve.tensor_tensor(flat(2), gat[:], wide(wk[r][:].rearrange("p (t o) -> p t o", o=1)), ALU.is_equal))
                    k(dve.tensor_tensor(flat(2), flat(2), rev, ALU.mult))
                    k(dve.tensor_reduce(small[:, 3, :], flat(2), AX.X, ALU.max))
                    k(dve.tensor_tensor(flat(r), flat(2), wide(col(3)), ALU.is_equal))
                    if r == 0:
                        k(dve.scalar_tensor_tensor(gat[:], flat(0), -2.0, gat[:], ALU.mult, ALU.add))
                dve.tensor_tensor(big[:, 5, :], big[:, 0, :], big[:, 1, :], ALU.add).then_inc(B_["ready"], 1)
                dve.wait_ge(B_["cnt_ps"], 2)
                k(dve.memset(small[:, 4, :], 1.0))
                for e in range(E):
                    sc = dve.tensor_tensor_scan(flat(3)[:, :, e], small[:, 4, :],
                                                ps_v[:].rearrange("p (t e) -> p t e", e=E)[:, :, e],
                                                0.0, ALU.mult, ALU.add)
                    k(sc)
                k(dve.tensor_tensor(big[:, 4, :], big[:, 3, :], ps_v[:], ALU.subtract))
                k(dve.tensor_tensor(big[:, 4, :], big[:, 4, :], ps_k[:], ALU.add))
                k(dve.tensor_scalar(cnti[:], flat(3)[:, NT - 1, :], float(BLK - 1), None, ALU.add))
                k(dve.tensor_scalar(cnti[:], cnti[:], BLK.bit_length() - 1, None, ALU.arith_shift_right))
                k(dve.tensor_copy(cnt[:, 1, :], cnti[:]))
                k(dve.tensor_scalar(cnt[:, 1, :], cnt[:, 1, :], float(BLK), None, ALU.mult))
                k(dve.tensor_tensor_scan(cnt[:, 2, :], small[:, 4, 0:E], cnt[:, 1, :], 0.0, ALU.mult, ALU.add))
                k(dve.tensor_tensor(cnt[:, 3, :], cnt[:, 2, :], cnt[:, 1, :], ALU.subtract))
                start = cnt[:, 3, :].rearrange("p (o e) -> p o e", o=1)
                k(dve.tensor_tensor(flat(4), flat(4), start.to_broadcast([128, NT, E]), ALU.add))
                for r in range(TOPK):
                    k(dve.tensor_tensor(flat(2), flat(r), flat(4), ALU.mult))
                    k(dve.tensor_reduce(small[:, 5 + r, :], flat(2), AX.X, ALU.add))
                    k(dve.tensor_copy(posi[r][:], small[:, 5 + r, :]))
                k(dve.tensor_tensor(etmp[:], etab[:].rearrange("p (j o) -> p j o", o=1).to_broadcast([128, NBLK, E]),
                                    start.to_broadcast([128, NBLK, E]), ALU.is_ge))
                k(dve.tensor_reduce(etab[:], etmp[:], AX.X, ALU.add))
                k(dve.tensor_scalar(etabi[:], etab[:], -1.0, None, ALU.add))

        C_ = {n: sem("C_" + n) for n in ("ready",)}
        with nc.Block() as block:
            @block.vector
            def _(dve):
                with dve.Fori(0, NT // 2) as i:
                    for p in range(2):
                        n = 2 * i + p
                        dve.wait_ge(scat[p], 32 * i)
                        dve.wait_ge(B_["rs"], 1)
                        dve.tensor_copy(idx[p][:], posi[0][:, bass.ds(n, 1)])
                        dve.tensor_copy(idxb[p][:], posi[1][:, bass.ds(n, 1)])
                        dve.tensor_scalar(xn[p][:].rearrange("p (o d) -> p o d", o=1), hres[:, bass.ds(n, 1), :],
                                          mvar[:, bass.ds(n, 1), 0], rstd[:, bass.ds(n, 1)],
                                          ALU.subtract, ALU.mult).then_inc(C_["ready"], 1)

            @block.gpsimd
            def _(pool):
                pool.wait_ge(xs_zero, 16 * (NBLK * BLK // (128 * 6)))
                with pool.Fori(0, NT // 2) as i:
                    for p in range(2):
                        n = 2 * i + p
                        for ix in (idx, idxb):
                            pool.wait_ge(C_["ready"], n + 1)
                            settle(pool, spare)
                            pool.indirect_dma_start(xs_d, bass.IndirectOffsetOnAxis(ap=ix[p][:], axis=0),
                                                    xn[p][:], None).then_inc(scat[p], 16)
                for p in range(2):
                    pool.wait_ge(scat[p], 32 * (NT // 2))

        D_ = {n: sem("D_" + n) for n in ("xT_ps", "xT_sb", "h_ps", "h_sb", "y_ps", "y_sb", "one")}
        w_ld = [sem(f"w_ld{p}") for p in range(2)]
        y_st = [sem(f"y_st{p}") for p in range(2)]
        w_free = sem("w_free")
        ps_h = [ps_s[:, g, :] for g in range(4)]
        with nc.Block() as block:
            @block.sync
            def _(sp):
                with sp.Fori(0, NBLK // 2) as i:
                    for p in range(2):
                        n = 2 * i + p
                        ex = sp.value_load(etabi[0:1, bass.ds(n, 1)], min_val=0, max_val=E - 1)
                        sp.wait_ge(w_free, n + 1)
                        sp.dma_start(xs[p], xs_d[bass.ds(n * BLK, BLK), :].rearrange("(s p) d -> p s d", s=2))\
                            .then_inc(w_ld[p], 16)
                        sp.dma_start(w1[p][0], w1h[bass.ds(ex, 1), 0:128, :].rearrange("o k i -> (o k) i"))\
                            .then_inc(w_ld[p], 16)
                        sp.dma_start(w1[p][1], w1h[bass.ds(ex, 1), 128:, :].rearrange("o k i -> (o k) i"))\
                            .then_inc(w_ld[p], 16)
                        sp.dma_start(probT[p][:, 0:NI * D], w2h[bass.ds(ex, 1), :, :].rearrange("o k i -> (o k) i"))\
                            .then_inc(w_ld[p], 16)
                        sp.dma_start(b2s[p], b2h[bass.ds(ex, 1), :].to_broadcast([128, D])).then_inc(w_ld[p], 16)
                    for p in range(2):
                        n = 2 * i + p
                        sp.wait_ge(D_["y_sb"], n + 1)
                        sp.dma_start(ys_d[bass.ds(n * BLK, BLK), :].rearrange("(s p) d -> p s d", s=2), ys[p])\
                            .then_inc(y_st[p], 16)
                for p in range(2):
                    sp.wait_ge(y_st[p], 16 * (NBLK // 2))

            @block.tensor
            def _(pe):
                with pe.Fori(0, NBLK // 2) as i:
                    for p in range(2):
                        n = 2 * i + p
                        pe.wait_ge(w_ld[p], 80 * i + 80)
                        pe.wait_ge(D_["xT_sb"], n)
                        for s in range(2):
                            pe.transpose(ps_t[:, s * 128:s * 128 + 128], xs[p][:, s, 0:128], ident[:])
                            last = pe.transpose(ps_t[0:D1, BLK + s * 128:BLK + s * 128 + 128], xs[p][:, s, 128:D],
                                                ident[:])
                        last.then_inc(D_["xT_ps"], 1)
                    for p in range(2):
                        n = 2 * i + p
                        pe.wait_ge(D_["xT_sb"], n + 1)
                        pe.wait_ge(D_["one"], 1)
                        for j in range(NI // 2):
                            bank = (p * 3 + j) % 3
                            pe.wait_ge(D_["h_sb"], n * 3)
                            for c in (2 * j, 2 * j + 1):
                                dst = ps_h[bank][:, (c % 2) * BLK:(c % 2) * BLK + BLK]
                                pe.matmul(dst, w1[p][0][:, c * 128:c * 128 + 128], xsT0[p], start=True, stop=False)
                                last = pe.matmul(dst, w1[p][1][:, c * 128:c * 128 + 128], xsT1[p],
                                                 start=False, stop=True)
                            last.then_inc(D_["h_ps"], 1)
                        pe.wait_ge(D_["h_sb"], n * 3 + 3)
                        pe.wait_ge(D_["y_sb"], n)
                        for s in range(2):
                            for c in range(NI):
                                last = pe.matmul(ps_v[:, s * D:s * D + D], hT[p][:, c, s * 128:s * 128 + 128],
                                                 w2[p][:, c, :], start=(c == 0), stop=(c == NI - 1))
                        last.then_inc(D_["y_ps"], 1)

            @block.scalar
            def _(act):
                with act.Fori(0, NBLK // 2) as i:
                    for p in range(2):
                        n = 2 * i + p
                        act.wait_ge(D_["xT_ps"], n + 1)
                        act.activation(xsT0[p], ps_t[:, 0:BLK], ACT.Copy)
                        act.activation(xsT1[p][0:D1, :], ps_t[0:D1, BLK:2 * BLK], ACT.Copy).then_inc(D_["xT_sb"], 1)
                    for p in range(2):
                        n = 2 * i + p
                        for j in range(NI // 2):
                            act.wait_ge(D_["h_ps"], n * 3 + j + 1)
                            act.activation(hT[p][:, 2 * j:2 * j + 2, :].rearrange("p c t -> p (c t)"), ps_h[j],
                                           ACT.Gelu).then_inc(D_["h_sb"], 1)

            @block.vector
            def _(dve):
                for p in range(2):
                    ins = dve.memset(xsT1[p][D1:D1 + 1, :], 1.0)
                ins.then_inc(D_["one"], 1)
                dve.sem_inc(w_free, 2)
                with dve.Fori(0, NBLK // 2) as i:
                    for p in range(2):
                        n = 2 * i + p
                        dve.wait_ge(D_["y_ps"], n + 1)
                        dve.wait_ge(y_st[p], 16 * i)
                        dve.tensor_tensor(ys[p], ps_v[:, 0:2 * D].rearrange("p (s d) -> p s d", s=2),
                                          b2s[p].rearrange("p (o d) -> p o d", o=1).to_broadcast([128, 2, D]),
                                          ALU.add).then_inc(D_["y_sb"], 1)
                        dve.wait_ge(D_["y_sb"], n + 1)
                        dve.sem_inc(w_free, 1)

        with nc.Block() as block:
            @block.sync
            def _(sp):
                S = L[1]
                with sp.Fori(0, NT // 2) as i:
                    for p in range(2):
                        n = 2 * i + p
                        sp.wait_ge(S["pad_ok"], n + 1)
                        sp.wait_ge(rel_zero, 32)
                        sp.dma_start(rel_d[p][:, 0:(LPAD + REL) * H], rpad[p][:].rearrange("p s h -> p (s h)"))\
                            .then_inc(rel_st[p], 16)
                    for p in range(2):
                        sp.wait_ge(rel_st[p], 16 * i + 16)
                        w = ROWW - H
                        src = rel_d[p].rearrange("t w -> (t w)")[(B - 1) * H:(B - 1) * H + B * w]
                        sp.dma_start(relb[p][:].rearrange("p s h -> p (s h)"),
                                     src.rearrange("(t w) -> t w", w=w)[:, 0:B * H]).then_inc(rel_ld[p], 16)

            @block.gpsimd
            def _(pool):
                S = L[1]
                with pool.Fori(0, NT // 2) as i:
                    for p in range(2):
                        n = 2 * i + p
                        pool.wait_ge(tok_ld[p], 16 * (NT // 2) + 16 * i)
                        pool.wait_ge(y2_ld[p], 16 * i)
                        pool.wait_ge(const_ok, 6)
                        pool.tensor_copy(idx[p][:], posi[0][:, bass.ds(n, 1)]).then_inc(S["idx_ok"], 1)
                        pool.tensor_copy(idxb[p][:], posi[1][:, bass.ds(n, 1)]).then_inc(S["idx_ok"], 1)
                        pool.wait_ge(S["idx_ok"], 2 * n + 2)
                        pool.wait_ge(tok_free, NT + n + 1)
                        settle(pool, spare)
                        pool.indirect_dma_start(tok[p][:], None, ys_d,
                                                bass.IndirectOffsetOnAxis(ap=idx[p][:], axis=0)).then_inc(tok_ld[p], 16)
                        pool.indirect_dma_start(posb[p][:], None, ys_d,
                                                bass.IndirectOffsetOnAxis(ap=idxb[p][:], axis=0)).then_inc(y2_ld[p], 16)
                    for r in range(2):
                        for p in range(2):
                            n = 2 * i + p
                            pool.wait_ge(S["mv_ok"], 4 * i + 2 * r + p + 1)
                            pool.tensor_tensor(veps[p][:], mv[p][:, 1:2], epsc[:], ALU.add).then_inc(S["pool"], 1)
                            pool.wait_ge(S["pool"], 4 * i + 2 * r + p + 1)
                            pool.tensor_tensor(rs[p][:] if r == 0 else rs2[p][:], veps[p][:], mhalf[:, 0:1],
                                               ALU.pow).then_inc(S["rs_ok"], 1)
                        if r == 0:
                            for p in range(2):
                                n = 2 * i + p
                                pool.wait_ge(S["r_sb"], n + 1)
                                settle(pool, spare)
                                pool.tensor_scalar(rpad[p][:, 0:LPAD, :],
                                                   rpad[p][:, LPAD:LPAD + 1, :].to_broadcast([128, LPAD, H]),
                                                   1.0, None, ALU.mult).then_inc(S["pad_ok"], 1)

            @block.tensor
            def _(pe):
                S = L[1]
                with pe.Fori(0, NT // 2) as i:
                    for stage in ("xT", "qkv", "r", "s", "pt", "o", "oT", "y", "fT", "f"):
                        for p in range(2):
                            n = 2 * i + p
                            if stage == "r":
                                pe.wait_ge(S["q_sb"], n + 1)
                                pe.wait_ge(S["r_sb" if p else "xT_sb"], n if p else n + 2)
                                for a in range(A):
                                    last = pe.matmul(ps_t[:, a * G * REL:(a + 1) * G * REL], qT[p][:, a, :], relw[:],
                                                     start=True, stop=True)
                                last.then_inc(S["r_ps"], 1)
                            elif stage == "fT":
                                pe.wait_ge(S["xn_ok"], 4 * i + 2 + p + 1)
                                pe.wait_ge(S["fT_sb" if p else "oT_sb"], n if p else n + 2)
                                pe_transpose(pe, ps_t, xn[p][:]).then_inc(S["fT_ps"], 1)
                            elif stage == "f":
                                pe.wait_ge(S["fT_sb"], n + 1 if p else n + 2)
                                pe.wait_ge(S["f_sb"], n)
                                pe.matmul(ps_t[:, 0:NODES], xT0[p][:], in_w[0][:], start=True, stop=False)
                                pe.matmul(ps_t[:, 0:NODES], xT1[p][0:D1, :], in_w[1][:], start=False,
                                          stop=True).then_inc(S["f_ps"], 1)
                            elif stage == "xT":
                                pe.wait_ge(S["xn_ok"], 4 * i + p + 1)
                                pe.wait_ge(S["xT_sb" if p else "f_sb"], n)
                                pe_transpose(pe, ps_t, xn[p][:]).then_inc(S["xT_ps"], 1)
                            else:
                                pe_attention(pe, 1, 128, i, stage, p)

            @block.scalar
            def _(act):
                S = L[1]
                with act.Fori(0, NT // 2) as i:
                    for stage in ("xT", "qkv", "r", "exp", "pt", "oT", "fT"):
                        for p in range(2):
                            n = 2 * i + p
                            if stage == "r":
                                act.wait_ge(S["r_ps"], n + 1)
                                for a in range(A):
                                    dst = rpad[p][:, LPAD:LPAD + REL, :].rearrange("p j (g a) -> p a g j", g=G)
                                    src = ps_t[:, 0:A * G * REL].rearrange("p (a g j) -> p a g j", a=A, g=G)
                                    ins = act.activation(dst[:, a], src[:, a], ACT.Copy)
                                ins.then_inc(S["r_sb"], 1)
                            elif stage == "fT":
                                act.wait_ge(S["fT_ps"], n + 1)
                                act.activation(xT0[p][:], ps_t[:, 0:128], ACT.Copy)
                                act.activation(xT1[p][0:D1, :], ps_t[0:D1, 128:256], ACT.Copy)\
                                    .then_inc(S["fT_sb"], 1)
                            else:
                                act_attention(act, 1, 128, i, stage, p)

            @block.vector
            def _(dve):
                S = L[1]
                for p in range(2):
                    vj = vv[p][:, 0:H * (DH + 1)].rearrange("p (h e) -> p h e", h=H)
                    ins = dve.memset(vj[:, :, DH:DH + 1], 1.0)
                ins.then_inc(dve_c, 1)
                dve.wait_ge(dve_c, 6)
                ch = Chain(dve, S["dve"], 2 * 11)
                with dve.Fori(0, NT // 2) as i:
                    ch.start(i)
                    for p in range(2):
                        n = 2 * i + p
                        dve.wait_ge(tok_ld[p], 16 * (NT // 2) + 16 * i + 16)
                        dve.wait_ge(y2_ld[p], 16 * i + 16)
                        ch.link(dve.tensor_scalar(emb[p][:], tok[p][:], wk[0][:, bass.ds(n, 1)], None, ALU.mult))
                        ch.link(dve.scalar_tensor_tensor(emb[p][:], posb[p][:], wk[1][:, bass.ds(n, 1)], emb[p][:],
                                                         ALU.mult, ALU.add))
                        dve.sem_inc(tok_free, 1)
                        ch.link(dve.tensor_tensor(res[p][:].rearrange("p (o d) -> p o d", o=1),
                                                  emb[p][:].rearrange("p (o d) -> p o d", o=1),
                                                  hres[:, bass.ds(n, 1), :], ALU.add))
                        ch.link(dve.bn_stats(st6[p][:], res[p][:]))
                        settle(dve, spare)
                        dve.bn_aggr(mv[p][:], st6[p][:]).then_inc(S["mv_ok"], 1)
                    for p in range(2):
                        dve.wait_ge(S["rs_ok"], 4 * i + p + 1)
                        dve.wait_ge(S["mv_ok"], 4 * i + p + 1)
                        dve.tensor_scalar(xn[p][:], res[p][:], mv[p][:, 0:1], rs[p][:, 0:1],
                                          ALU.subtract, ALU.mult).then_inc(S["xn_ok"], 1)
                    for stage in ("s", "o"):
                        for p in range(2):
                            dve_softmax(dve, ch, 1, 128, i, stage, p)
                    for p in range(2):
                        n = 2 * i + p
                        dve.wait_ge(S["y_ps"], n + 1)
                        dve.tensor_tensor(emb[p][:], ps_v[:, 0:D], res[p][:], ALU.add).then_inc(S["y_ok"], 1)
                        dve.wait_ge(S["y_ok"], n + 1)
                        ch.link(dve.bn_stats(st6[p][:], emb[p][:]))
                        settle(dve, spare)
                        dve.bn_aggr(mv[p][:], st6[p][:]).then_inc(S["mv_ok"], 1)
                    for p in range(2):
                        n = 2 * i + p
                        dve.wait_ge(S["rs_ok"], 4 * i + 2 + p + 1)
                        dve.wait_ge(S["mv_ok"], 4 * i + 2 + p + 1)
                        dve.tensor_scalar(xn[p][:], emb[p][:], mv[p][:, 0:1], rs2[p][:, 0:1],
                                          ALU.subtract, ALU.mult).then_inc(S["xn_ok"], 1)
                        dve.wait_ge(const_ok, 6)
                        dve.tensor_copy(hres[:, bass.ds(n, 1), :], emb[p][:].rearrange("p (o d) -> p o d", o=1))\
                            .then_inc(S["h_ok"], 1)
                    for p in range(2):
                        n = 2 * i + p
                        dve.wait_ge(S["f_ps"], n + 1)
                        dve.wait_ge(const_ok, 6)
                        dve.tensor_copy(flog[:, bass.ds(n, 1), :], ps_t[:, 0:NODES].rearrange("p (o d) -> p o d", o=1))\
                            .then_inc(S["f_sb"], 1)
                    ch.end()

        F_ = {n: sem("F_" + n) for n in ("gelu", "dve", "c_ok", "cT_ps", "cT_sb", "o_ps", "o_sb")}
        out_st = [sem(f"out_st{p}") for p in range(2)]
        c4 = [prob[p][:, 0:128] for p in range(2)]
        cT4 = [prob[p][:, 128:256] for p in range(2)]
        ho4 = [score[p][:].rearrange("p g a k -> p (g a k)")[:, 0:4 * D].rearrange("p (k d) -> p k d", k=4)
               for p in range(2)]
        NM = NT // 4
        with nc.Block() as block:
            @block.scalar
            def _(act):
                act.activation(fg, flog[:], ACT.Gelu).then_inc(F_["gelu"], 1)
                with act.Fori(0, NM // 2) as i:
                    for p in range(2):
                        m = 2 * i + p
                        act.wait_ge(F_["cT_ps"], m + 1)
                        act.activation(cT4[p], ps_t[:, 0:128], ACT.Copy).then_inc(F_["cT_sb"], 1)

            @block.tensor
            def _(pe):
                with pe.Fori(0, NM // 2) as i:
                    for p in range(2):
                        m = 2 * i + p
                        pe.wait_ge(F_["c_ok"], m + 1)
                        pe.wait_ge(F_["cT_sb"], m)
                        pe.transpose(ps_t[:, 0:128], c4[p], ident[:]).then_inc(F_["cT_ps"], 1)
                        pe.wait_ge(F_["cT_sb"], m + 1)
                        pe.wait_ge(F_["o_sb"], m)
                        for k in range(4):
                            r = slice(32 * k, 32 * k + NODES)
                            last = pe.matmul(ps_s[:, k, 0:D], cT4[p][r, :], wout4[r, :], start=True, stop=True)
                        last.then_inc(F_["o_ps"], 1)

            @block.vector
            def _(dve):
                ch = Chain(dve, F_["dve"], 1000)
                k = ch.link
                k(dve.tensor_scalar(fs, flog[:], 0.0, None, ALU.is_gt))
                k(dve.memset(fc[:], 0.0))
                k(dve.memset(fr, 1.0))
                dve.wait_ge(F_["gelu"], 1)

                def children(t, lo, n, side):
                    return t[:, :, 2 * lo + 1:2 * lo + 1 + 2 * n].rearrange("p t (n s) -> p t n s", s=2)[:, :, :, side]

                for lo, n in ((0, 1), (1, 2), (3, 4), (7, 3)):
                    parent = fr[:, :, lo:lo + n]
                    k(dve.tensor_tensor(children(fr, lo, n, 1), parent, fs[:, :, lo:lo + n], ALU.mult))
                    k(dve.tensor_tensor(children(fr, lo, n, 0), parent, children(fr, lo, n, 1), ALU.subtract))
                    for side in range(2):
                        k(dve.tensor_tensor(children(fc, lo, n, side), children(fr, lo, n, side),
                                            fg[:, :, lo:lo + n], ALU.mult))
                last_r, last_c = fr[:, :, LAST:NODES], fc[:, :, LAST:NODES]
                c3 = lambda j: small[:, j, :].rearrange("p (t o) -> p t o", o=1)
                k(dve.tensor_reduce(small[:, 0, :], fr[:, :, 10:15], AX.X, ALU.add))
                k(dve.tensor_tensor(last_r, last_r, c3(0), ALU.add))
                prod = big[:, 0:3, :].rearrange("p a b -> p (a b)")[:, 0:NT * NODES]\
                    .rearrange("p (t n) -> p t n", n=NODES)
                k(dve.tensor_tensor(prod, fr, fg, ALU.mult))
                k(dve.tensor_reduce(small[:, 1, :], prod[:, :, 10:NODES], AX.X, ALU.add))
                k(dve.tensor_tensor(last_c, last_c, c3(1), ALU.add))
                k(dve.scalar_tensor_tensor(last_c, fg[:, :, LAST:NODES], 5.0, last_c, ALU.mult, ALU.add))
                with dve.Fori(0, NM // 2) as i:
                    for p in range(2):
                        m = 2 * i + p
                        dve.wait_ge(F_["cT_ps"], 2 * i)
                        dve.wait_ge(F_["gelu"], 1)
                        dve.tensor_copy(c4[p].rearrange("p (k n) -> p k n", k=4), fc[:, bass.ds(4 * m, 4), :])\
                            .then_inc(F_["c_ok"], 1)
                    for p in range(2):
                        m = 2 * i + p
                        dve.wait_ge(F_["o_ps"], m + 1)
                        dve.wait_ge(out_st[p], 16 * i)
                        dve.tensor_tensor(ho4[p], ps_s[:, :, 0:D], hres[:, bass.ds(4 * m, 4), :], ALU.add)\
                            .then_inc(F_["o_sb"], 1)

            @block.sync
            def _(sp):
                ov = out.rearrange("t b d -> b t d")
                with sp.Fori(0, NM // 2) as i:
                    for p in range(2):
                        m = 2 * i + p
                        sp.wait_ge(F_["o_sb"], m + 1)
                        sp.dma_start(ov[:, bass.ds(4 * m, 4), :], ho4[p]).then_inc(out_st[p], 16)
                for p in range(2):
                    sp.wait_ge(out_st[p], 16 * (NM // 2))


def rows(w, b):
    out = np.zeros((w.shape[0] + 1, w.shape[1]), np.float32)
    out[:-1] = w
    out[-1] = b
    return out


def head_slots(wq, bq, wk, bk):
    out = np.zeros((D + 1, 2, A, G, 32), np.float32)
    for side, (w, b) in enumerate(((wq, bq), (wk, bk))):
        out[:, side, :, :, 0:DH] = rows(w, b).reshape(D + 1, G, A, DH).transpose(0, 2, 1, 3)
    return out.reshape(D + 1, 2 * A * 128)


def laid_out(v):
    a = {k: np.asarray(x) for k, x in v.items()}
    qkv, qb = a["L1_attn_qkv_w"], a["L1_attn_qkv_b"]
    rel = a["L1_attn_rel_pos_emb"]
    relblk = np.zeros((G, 32, G, REL), np.float32)
    rel32 = np.zeros((G, 32, 1), np.float32)
    for g in range(G):
        relblk[g, 0:DH, g, :] = rel.T
        rel32[g, 0:DH, 0] = rel[REL - 1]
    w1 = np.zeros((E, D + 1, I), np.float32)
    w1[:, :D] = a["L0_ffn_W1"]
    w1[:, D] = a["L0_ffn_b1"]
    return {
        "ids_h": a["x"].T.reshape(NT, 128).T,
        "typ_h": a["mask_BS_i1_0"].T.reshape(NT, 128).T,
        "tok_w": a["L0_tok_tok_w"], "pos_w": a["L0_tok_pos_w"], "type_w": a["L0_tok_type_w"],
        "gamma": a["L0_tok_gamma"].reshape(1, D), "beta": a["L0_tok_beta"].reshape(1, D),
        "wqk0": head_slots(a["L0_attn_Wq"].T, a["L0_attn_bq"], a["L0_attn_Wk"].T, a["L0_attn_bk"]),
        "wv0": rows(a["L0_attn_Wv"].T, a["L0_attn_bv"]),
        "wo0": rows(a["L0_attn_Wout"].T, a["L0_attn_bout"]),
        "w1h": w1,
        "w2h": a["L0_ffn_W2"].reshape(E, NI, 128, D).transpose(0, 2, 1, 3).reshape(E, 128, NI * D),
        "b2h": a["L0_ffn_b2"],
        "wr": rows(a["L0_ffn_Wr"], a["L0_ffn_br"]),
        "wqk1": head_slots(qkv[0:D].T, qb[0:D], qkv[D:2 * D].T, qb[D:2 * D]),
        "wv1": rows(qkv[2 * D:].T, qb[2 * D:]),
        "wo1": rows(a["L1_attn_out_w"].T, a["L1_attn_out_b"]),
        "relblk": relblk.reshape(128, G * REL), "rel32": rel32.reshape(128, 1),
        "win": a["L1_ffn_weights_in"].T, "wout": a["L1_ffn_weights_out"],
    }


def build(nc, arrays, dbg):
    args = [nc.dram_tensor(n, x.shape, mybir.dt.from_np(x.dtype), kind="ExternalInput").ap()
            for n, x in arrays.items()]
    out = nc.dram_tensor("out_0_dram", [T, B, D], F32, kind="ExternalOutput").ap()
    tower(nc, dbg, *args, out)


def kernel(**inputs):
    import concourse.bacc as bacc
    from concourse.bass_utils import run_bass_kernel_spmd

    arrays = {n: np.ascontiguousarray(x) for n, x in laid_out(inputs).items()}
    nc = bacc.Bacc("TRN2", target_bir_lowering=False, num_devices=1)
    build(nc, arrays, {})
    r = run_bass_kernel_spmd(nc, [arrays], core_ids=[0])
    return r.results[0]["out_0_dram"]
```

```python
from contextlib import ExitStack

import numpy as np

import concourse.bass as bass
from concourse import mybir

F32 = mybir.dt.float32
I32 = mybir.dt.int32
U32 = mybir.dt.uint32
ALU = mybir.AluOpType
ACT = mybir.ActivationFunctionType
AX = mybir.AxisListType

T, B = 64, 128
D = 192
D1 = D - 128
NT = T * B // 128
H, DH = 12, 16
G, A = 4, 3
E, TOPK, I = 8, 2, 768
NI = I // 128
BLK = 256
NBLK = T * B * TOPK // BLK + E
REL = 33
MAXREL = 16
LPAD = B - 1 - MAXREL
ROWW = (2 * B - 1) * H
NODES = 21
LAST = NODES - 1
EPS = 1e-5
SCALE = DH ** -0.5


class Chain:

    def __init__(self, eng, sem):
        self.eng, self.sem, self.at, self.base, self.per = eng, sem, 0, 0, 0

    def loop(self, step, per):
        self.base, self.at = self.at + step * per, 0

    def link(self, ins):
        self.at += 1
        ins.then_inc(self.sem, 1)
        self.eng.wait_ge(self.sem, self.base + self.at)


def upto(t):
    return max(0, min(t + 1, NT)) if isinstance(t, int) else t + 1


def after(eng, sem, value):
    if not isinstance(value, int) or value > 0:
        eng.wait_ge(sem, value)


UNROLL = 4


class Step:

    def __init__(self, ages, n, half_n, p):
        self.ages, self.n, self.half_n, self.p = ages, n, half_n, p

    def has(self, k):
        return k in self.ages and (not isinstance(self.n, int) or 0 <= self.n - self.ages[k] < NT)

    def tile(self, k):
        return self.n - self.ages[k]

    def pair(self, k):
        return self.half_n + (self.p % 2 - self.ages[k]) // 2

    def two(self, k):
        return (self.p - self.ages[k]) % 2

    def four(self, k):
        return (self.p - self.ages[k]) % 4


def pipeline(eng, ages, body, links=None, per=0):
    head = 2 * UNROLL

    for n in range(head):
        body(Step(ages, n, n // 2, n % UNROLL))
    at0 = links.at if links else 0
    with eng.Fori(0, (NT - head) // UNROLL) as i:
        if links:
            links.base, links.at = at0 + i * (per * UNROLL), 0
        for p in range(UNROLL):
            body(Step(ages, UNROLL * i + (head + p), 2 * i + (head + p) // 2, p))
    if links:
        assert links.at == per * UNROLL, (links.at, per)
        links.base, links.at = 0, at0 + per * (NT - head)
    for n in range(NT, NT + max(ages.values())):
        body(Step(ages, n, n // 2, n % UNROLL))


AGES = [dict(gather=0, emb=1, ln=2, xn=3, qk=3, v=3, s=4, pt=5, o=6),
        dict(gather=0, emb=1, xn=2, qk=2, r=3, v=3, s=4, pt=5, o=6)]


def settle(eng, spare):
    eng.sem_inc(spare, 1)


def tower(nc, dbg, ids_h, typ_h, tok_w, pos_w, type_w, gamma, beta,
          wqk0, wv0, wo0, w1h, w2h, b2h, wr, wqk1, wv1, wo1, relblk, rel32, win, wout, out):
    h1_d = nc.dram_tensor("h1_d", [T * B, D], F32, **dbg).ap()
    xs_d = nc.dram_tensor("xs_d", [NBLK * BLK, D], F32, **dbg).ap()
    ys_d = nc.dram_tensor("ys_d", [NBLK * BLK, D], F32, **dbg).ap()
    rel_d = [nc.dram_tensor(f"rel_d{p}", [B, ROWW], F32).ap() for p in range(2)]

    with ExitStack() as ctx:
        def sb(name, shape, dt=F32):
            return ctx.enter_context(nc.sbuf_tensor(name, shape, dt))

        def two(name, shape, dt=F32):
            return [sb(f"{name}{p}", shape, dt) for p in range(2)]

        def sem(name):
            return ctx.enter_context(nc.semaphore(name))

        ps_s = ctx.enter_context(nc.psum_tensor("ps_s", [128, G, 512], F32))
        ps_t = ctx.enter_context(nc.psum_tensor("ps_t", [128, 512], F32))
        ps_q = ctx.enter_context(nc.psum_tensor("ps_q", [128, 512], F32))
        ps_k = ctx.enter_context(nc.psum_tensor("ps_k", [128, 512], F32))
        ps_v = ctx.enter_context(nc.psum_tensor("ps_v", [128, 512], F32))
        ps_pt = [ps_q, ps_k]

        ident = sb("ident", [128, 128])
        tri = sb("tri", [128, 128])
        ones = sb("ones", [128, 128])
        mhalf = sb("mhalf", [128, NT])
        epsc = sb("epsc", [128, 1])
        zrow = sb("zrow", [128, LPAD * H])
        gam = sb("gam", [128, D])
        bet = sb("bet", [128, D])
        typ0 = sb("typ0", [128, D])
        typ1 = sb("typ1", [128, D])
        ids = sb("ids", [128, NT], I32)
        typi = sb("typi", [128, NT], I32)
        typf = sb("typf", [128, NT])
        typn = sb("typn", [128, NT])
        relw = sb("relw", [128, G * REL])
        rel32s = sb("rel32s", [128, 1])

        def weights(name, n):
            return sb(name + "_c0", [128, n]), sb(name + "_c1", [D1 + 1, n])

        qk_w = [weights("wqk0", 2 * A * 128), weights("wqk1", 2 * A * 128)]
        v_w = [weights("wv0", D), weights("wv1", D)]
        o_w = [weights("wo0", D), weights("wo1", D)]
        r_w = weights("wr", E)
        in_w = (sb("win_c0", [128, NODES]), sb("win_c1", [D1, NODES]))

        hres = sb("hres", [128, NT, D])
        stats = sb("stats", [128, NT, 6])
        mvar = sb("mvar", [128, NT, 2])
        rstd = sb("rstd", [128, NT])
        wk = [sb(f"wk{k}", [128, NT]) for k in range(TOPK)]
        posi = [sb(f"posi{k}", [128, NT], U32) for k in range(TOPK)]

        def four(name, shape, dt=F32):
            return [sb(f"{name}{p}", shape, dt) for p in range(4)]

        idx = two("idx", [128, 1], U32)
        idxb = two("idxb", [128, 1], U32)
        tok = two("tok", [128, D])
        posb = two("posb", [128, D])
        emb = two("emb", [128, D])
        st6 = two("st6", [128, 6])
        mv = two("mv", [128, 2])
        mvb = two("mvb", [128, 2])
        veps = two("veps", [128, 1])
        rs = two("rs", [128, 1])
        rs2 = two("rs2", [128, 1])
        xn = two("xn", [128, D])
        xT0 = two("xT0", [128, 128])
        xT1 = two("xT1", [D1 + 1, 128])
        qT = four("qT", [128, A, 128])
        kT = four("kT", [128, A, 128])
        vv = four("vv", [128, 2 * (H // 2) * 2 * (DH + 1)])
        score = two("score", [128, G, A, 128])
        mx = two("mx", [128, H])
        prob = two("prob", [128, H * 128])
        probT = two("probT", [128, H * 128])
        rden = two("rden", [128, H])
        on = two("on", [128, D])
        oT0 = two("oT0", [128, 128])
        oT1 = two("oT1", [D1 + 1, 128])
        hout = two("hout", [128, D])
        rpad = two("rpad", [128, LPAD + REL, H])
        relb = two("relb", [128, B, H])

        w1 = [(score[p][:].rearrange("p g a k -> p (g a k)")[:, 0:I],
               score[p][:].rearrange("p g a k -> p (g a k)")[0:D1 + 1, I:2 * I]) for p in range(2)]
        w2 = [probT[p][:, 0:NI * D].rearrange("p (c d) -> p c d", c=NI) for p in range(2)]
        hT = [prob[p][:].rearrange("p (c t) -> p c t", c=NI) for p in range(2)]
        xs = [relb[p][:].rearrange("p s h -> p (s h)")[:, 0:2 * D].rearrange("p (s d) -> p s d", s=2)
              for p in range(2)]
        ys = [rpad[p][:].rearrange("p s h -> p (s h)")[:, 0:2 * D].rearrange("p (s d) -> p s d", s=2)
              for p in range(2)]
        xsT0 = [qT[p][:].rearrange("p a t -> p (a t)")[:, 0:BLK] for p in range(2)]
        xsT1 = [kT[p][:].rearrange("p a t -> p (a t)")[0:D1 + 1, 0:BLK] for p in range(2)]
        b2s = [tok[p][:] for p in range(2)]
        gat = probT[1][:, 0:NT * E].rearrange("p (t e) -> p t e", e=E)
        bigs = [score[j // 3][:].rearrange("p g a k -> p (g a k)")[:, 512 * (j % 3):512 * (j % 3) + 512]
                for j in range(6)]
        small = sb("small", [128, 12, NT])
        etab = sb("etab", [128, NBLK])
        etabi = sb("etabi", [128, NBLK], I32)
        cnt = sb("cnt", [128, 6, E])
        cnti = sb("cnti", [128, E], I32)
        etmp = probT[0][:, 0:NBLK * E].rearrange("p (j e) -> p j e", e=E)
        fg = relb[0][:].rearrange("p s h -> p (s h)")[:, 0:NT * NODES].rearrange("p (t n) -> p t n", n=NODES)
        fs = relb[1][:].rearrange("p s h -> p (s h)")[:, 0:NT * NODES].rearrange("p (t n) -> p t n", n=NODES)
        fr = rpad[0][:].rearrange("p s h -> p (s h)")[:, 0:NT * NODES].rearrange("p (t n) -> p t n", n=NODES)
        fc = sb("fc", [128, NT, 32])
        wout4 = sb("wout4", [128, D])

        dma = {}

        def dsem(name):
            dma[name] = sem("ld_" + name)
            return dma[name]

        const_ld = dsem("const")
        N_CONST = 28
        pool_c = sem("pool_c")
        const_ok = sem("const_ok")
        zero_ok = sem("zero_ok")
        xs_zero = sem("xs_zero")
        rel_zero = sem("rel_zero")
        NAMES = ("idx_ok", "emb_rd", "mv_ok", "rs_ok", "mvb_ok", "rsb_ok", "pool", "dve", "xn_ok", "xT_ps",
                 "xT_sb", "q_ps", "q_sb", "k_ps", "k_sb", "r_ps", "r_sb", "pad_ok", "v_ps", "v_sb", "s_ps",
                 "s_sub", "p_sb", "pt_ps", "pt_sb", "o_ps", "o_sb", "oT_ps", "oT_sb", "y_ps", "y_ok")
        L = [{n: sem(f"L{l}_{n}") for n in NAMES} for l in range(2)]
        DMAS = ("tok", "pos", "h1", "rst", "rld")
        M = [{n: [sem(f"L{l}_{n}{p}") for p in range(2)] for n in DMAS} for l in range(2)]
        dve_c = sem("dve_c")
        spare = sem("spare")
        ctx2 = ExitStack()
        block_a = ctx2.enter_context(nc.Block())
        def bcast_rows(ap, n):
            return ap.to_broadcast([n, ap.shape[1]])

        def pool_steps(pool, l):
            S, M_, ages = L[l], M[l], AGES[l]
            src = [(idx, ids, tok, tok_w, M_["tok"])]
            if l == 1:
                src = [(idx, posi[0], tok, ys_d, M_["tok"]), (idxb, posi[1], posb, ys_d, M_["pos"])]

            def rsqrt(t, b, var_ok, var, out_ok, out):
                pool.wait_ge(S[var_ok], upto(t))
                pool.tensor_tensor(veps[b][:], var[b][:, 1:2], epsc[:], ALU.add).then_inc(S["pool"], 1)
                ch.at += 1
                pool.wait_ge(S["pool"], ch.base + ch.at)
                pool.tensor_tensor(out[b][:], veps[b][:], mhalf[:, 0:1], ALU.pow).then_inc(S[out_ok], 1)

            ch = Chain(pool, S["pool"])

            def body(st):
                if st.has("gather"):
                    t, b = st.tile("gather"), st.two("gather")
                    for ix, ids_, dst, table, ld in src:
                        after(pool, ld[b], 16 * st.pair("gather"))
                        pool.tensor_copy(ix[b][:], ids_[:, bass.ds(t, 1)]).then_inc(S["idx_ok"], 1)
                    pool.wait_ge(S["idx_ok"], len(src) * upto(t))
                    after(pool, S["emb_rd"], upto(t - 2))
                    settle(pool, spare)
                    for ix, ids_, dst, table, ld in src:
                        pool.indirect_dma_start(dst[b][:], None, table,
                                                bass.IndirectOffsetOnAxis(ap=ix[b][:], axis=0)).then_inc(ld[b], 16)
                if st.has("r"):
                    t, b = st.tile("r"), st.two("r")
                    pool.wait_ge(S["r_sb"], upto(t))
                    settle(pool, spare)
                    pool.tensor_scalar(rpad[b][:, 0:LPAD, :],
                                       rpad[b][:, LPAD:LPAD + 1, :].to_broadcast([128, LPAD, H]),
                                       1.0, None, ALU.mult).then_inc(S["pad_ok"], 1)
                if st.has("ln"):
                    rsqrt(st.tile("ln"), st.two("ln"), "mvb_ok", mvb, "rsb_ok", rs2)
                if st.has("emb"):
                    rsqrt(st.tile("emb"), st.two("emb"), "mv_ok", mv, "rs_ok", rs)
            pipeline(pool, ages, body, ch, 2 - l)

        def pe_transpose(pe, dst, src):
            pe.transpose(dst[:, 0:128], src[:, 0:128], ident[:])
            return pe.transpose(dst[0:D1, 128:256], src[:, 128:D], ident[:])

        def pe_project(pe, dst, x0, x1, w):
            pe.matmul(dst, x0, w[0][:], start=True, stop=False)
            return pe.matmul(dst, x1, w[1][:], start=False, stop=True)

        def pe_steps(pe, l):
            S, ages = L[l], AGES[l]
            keys = 64 if l == 0 else 128
            npt = 2 if l == 0 else 3
            W = DH + 1

            def body(st):
                n = st.n
                done = lambda k: upto(n - ages[k])
                before = lambda k: upto(n - ages[k] - 1)
                if st.has("qk"):
                    b = st.two("qk")
                    pe.wait_ge(S["xn_ok"], done("qk"))
                    after(pe, S["oT_sb"], before("o"))
                    if l == 1:
                        after(pe, S["r_sb"], before("r"))
                    after(pe, S["xT_sb"], before("qk"))
                    pe_transpose(pe, ps_t, xn[b][:]).then_inc(S["xT_ps"], 1)
                if st.has("o"):
                    b, v = st.two("o"), st.four("o")
                    pe.wait_ge(S["pt_sb"], npt * done("o"))
                    after(pe, S["v_sb"], before("v"))
                    after(pe, S["y_ok"], before("o"))
                    if l == 0:
                        for r in range(H // 2):
                            for c in range(2):
                                o = (c * (H // 2) + r) * 2 * W
                                last = pe.matmul(ps_v[64 * c:64 * c + 64, r * 2 * W:(r + 1) * 2 * W],
                                                 probT[b][:, r * 128 + 64 * c:r * 128 + 64 * c + 64],
                                                 vv[v][:, o:o + 2 * W], start=True, stop=True)
                    else:
                        for h in range(H):
                            last = pe.matmul(ps_v[:, h * W:(h + 1) * W], probT[b][:, h * 128:h * 128 + 128],
                                             vv[v][:, h * W:(h + 1) * W], start=True, stop=True)
                    last.then_inc(S["o_ps"], 1)
                if st.has("s"):
                    q4 = st.four("s")
                    pe.wait_ge(S["q_sb"], done("s"))
                    pe.wait_ge(S["k_sb"], done("s"))
                    after(pe, S["s_sub"], before("s"))
                    for a in range(A):
                        for g in range(G):
                            q = slice(32 * g, 32 * g + DH)
                            for c in range(128 // keys):
                                t = slice(keys * c, keys * c + keys)
                                last = pe.matmul(ps_s[t, g, a * keys:a * keys + keys], qT[q4][q, a, t],
                                                 kT[q4][q, a, t], start=True, stop=True)
                    last.then_inc(S["s_ps"], 1)
                if st.has("r"):
                    q4 = st.four("r")
                    pe.wait_ge(S["q_sb"], done("r"))
                    after(pe, S["xT_sb"], done("qk"))
                    after(pe, S["oT_sb"], before("o"))
                    for a in range(A):
                        last = pe.matmul(ps_t[:, a * G * REL:(a + 1) * G * REL], qT[q4][:, a, :], relw[:],
                                         start=True, stop=True)
                    last.then_inc(S["r_ps"], 1)
                if st.has("qk"):
                    b = st.two("qk")
                    pe.wait_ge(S["xT_sb"], done("qk"))
                    after(pe, S["pt_sb"], npt * before("pt"))
                    for side, dst in enumerate((ps_q, ps_k)):
                        after(pe, S["k_sb" if side else "q_sb"], before("qk"))
                        for a in range(A):
                            o = (side * A + a) * 128
                            pe.matmul(dst[:, a * 128:a * 128 + 128], qk_w[l][0][:, o:o + 128], xT0[b][:],
                                      start=True, stop=False)
                            last = pe.matmul(dst[:, a * 128:a * 128 + 128], qk_w[l][1][:, o:o + 128], xT1[b][:],
                                             start=False, stop=True)
                        last.then_inc(S["k_ps" if side else "q_ps"], 1)
                if st.has("o"):
                    b = st.two("o")
                    pe.wait_ge(S["o_sb"], done("o"))
                    after(pe, S["xT_sb"], done("qk"))
                    if l == 1:
                        after(pe, S["r_sb"], done("r"))
                    pe_transpose(pe, ps_t, on[b][:]).then_inc(S["oT_ps"], 1)
                if st.has("v"):
                    b = st.two("v")
                    pe.wait_ge(S["xT_sb"], done("v"))
                    after(pe, S["o_sb"], done("o"))
                    after(pe, S["y_ok"], before("o"))
                    after(pe, S["v_sb"], before("v"))
                    last = pe_project(pe, ps_v[:, 0:D], xT0[b][:], xT1[b][:], v_w[l])
                    if l == 0:
                        for c in range(2):
                            q = slice(64 * (1 - c), 64 * (1 - c) + 64)
                            last = pe_project(pe, ps_v[64 * c:64 * c + 64, D:2 * D], xT0[b][:, q], xT1[b][:, q],
                                              v_w[l])
                    last.then_inc(S["v_ps"], 1)
                for u in range(npt):
                    if st.has("pt"):
                        b = st.two("pt")
                        t = st.tile("pt")
                        per = 3 if l == 0 else 4
                        if u == 0:
                            pe.wait_ge(S["p_sb"], upto(t))
                        after(pe, S["k_sb" if u == 1 else "q_sb"], done("qk"))
                        if u == 2:
                            pe.wait_ge(S["pt_sb"], npt * t + 1)
                        for j in range(per):
                            o = (u * per + j) * 128
                            last = pe.transpose(ps_pt[u % 2][:, j * 128:j * 128 + 128], prob[b][:, o:o + 128],
                                                ident[:])
                        last.then_inc(S["pt_ps"], 1)
                    if u == 0 and st.has("o"):
                        b = st.two("o")
                        pe.wait_ge(S["oT_sb"], done("o"))
                        after(pe, S["v_sb"], done("v"))
                        pe_project(pe, ps_v[:, 0:D], oT0[b][:], oT1[b][:], o_w[l]).then_inc(S["y_ps"], 1)
            pipeline(pe, ages, body)

        def act_steps(act, l):
            S, ages = L[l], AGES[l]
            keys = 64 if l == 0 else 128
            npt = 2 if l == 0 else 3

            def body(st):
                done = lambda k: upto(st.n - ages[k])
                if st.has("pt"):
                    b = st.two("pt")
                    act.wait_ge(S["s_sub"], done("pt"))
                    act.activation(prob[b][:, 0:H * keys].rearrange("p (g a k) -> p g a k", g=G, a=A),
                                   score[b][:, :, :, 0:keys], ACT.Exp, scale=SCALE).then_inc(S["p_sb"], 1)
                if st.has("qk"):
                    b = st.two("qk")
                    act.wait_ge(S["xT_ps"], done("qk"))
                    act.activation(xT0[b][:], ps_t[:, 0:128], ACT.Copy)
                    act.activation(xT1[b][0:D1, :], ps_t[0:D1, 128:256], ACT.Copy).then_inc(S["xT_sb"], 1)
                if st.has("r"):
                    b = st.two("r")
                    act.wait_ge(S["r_ps"], done("r"))
                    after(act, M[l]["rst"][b], 16 * st.pair("r"))
                    src = ps_t[:, 0:A * G * REL].rearrange("p (a g j) -> p a g j", a=A, g=G)
                    dst = rpad[b][:, LPAD:LPAD + REL, :].rearrange("p j (g a) -> p a g j", g=G)
                    for a in range(A):
                        ins = act.activation(dst[:, a], src[:, a], ACT.Copy)
                    ins.then_inc(S["r_sb"], 1)
                if st.has("qk"):
                    q4 = st.four("qk")
                    act.wait_ge(S["q_ps"], done("qk"))
                    act.activation(qT[q4][:], ps_q[:, 0:A * 128].rearrange("p (a t) -> p a t", a=A),
                                   ACT.Copy).then_inc(S["q_sb"], 1)
                    act.wait_ge(S["k_ps"], done("qk"))
                    src = ps_k[:, 0:A * 128].rearrange("p (a t) -> p a t", a=A)
                    if l == 0:
                        act.activation(kT[q4][:], src, ACT.Copy).then_inc(S["k_sb"], 1)
                    else:
                        act.activation(kT[q4][:], src, ACT.Identity, bias=rel32s[:, 0:1]).then_inc(S["k_sb"], 1)
                if st.has("o"):
                    b = st.two("o")
                    act.wait_ge(S["oT_ps"], done("o"))
                    act.activation(oT0[b][:], ps_t[:, 0:128], ACT.Copy)
                    act.activation(oT1[b][0:D1, :], ps_t[0:D1, 128:256], ACT.Copy).then_inc(S["oT_sb"], 1)
                if st.has("v"):
                    v = st.four("v")
                    act.wait_ge(S["v_ps"], done("v"))
                    if l == 0:
                        vb = vv[v][:].rearrange("p (c r s e) -> p c r s e", c=2, r=H // 2, s=2)
                        pv = ps_v[:, 0:2 * D].rearrange("p (w r s e) -> p w r s e", w=2, r=H // 2, s=2)
                        for c in range(2):
                            for s in range(2):
                                ins = act.activation(vb[64 * s:64 * s + 64, c, :, s, 0:DH],
                                                     pv[64 * s:64 * s + 64, 0 if s == c else 1, :, s, :], ACT.Copy)
                    else:
                        vj = vv[v][:, 0:H * (DH + 1)].rearrange("p (h e) -> p h e", h=H)
                        ins = act.activation(vj[:, :, 0:DH], ps_v[:, 0:D].rearrange("p (h e) -> p h e", h=H),
                                             ACT.Copy)
                    ins.then_inc(S["v_sb"], 1)
                if st.has("pt"):
                    b = st.two("pt")
                    w = 384 if l == 0 else 512
                    for u in range(npt):
                        act.wait_ge(S["pt_ps"], npt * st.tile("pt") + u + 1)
                        act.activation(probT[b][:, u * w:(u + 1) * w], ps_pt[u % 2][:, 0:w],
                                       ACT.Copy).then_inc(S["pt_sb"], 1)
            pipeline(act, ages, body)

        def dve_steps(dve, l):
            S, M_, ages = L[l], M[l], AGES[l]
            keys = 64 if l == 0 else 128
            ch = Chain(dve, S["dve"])

            def moments(x, b, mom, name):
                settle(dve, spare)
                ch.link(dve.bn_stats(st6[b][:], x))
                settle(dve, spare)
                dve.bn_aggr(mom[b][:], st6[b][:]).then_inc(S[name], 1)

            def body(st):
                done = lambda k: upto(st.n - ages[k])
                before2 = lambda k: upto(st.n - ages[k] - 2)
                if st.has("xn"):
                    t, b = st.tile("xn"), st.two("xn")
                    dve.wait_ge(S["rsb_ok" if l == 0 else "rs_ok"], upto(t))
                    after(dve, S["xT_ps"], before2("xn"))
                    m, r = (mvb, rs2) if l == 0 else (mv, rs)
                    dve.tensor_scalar(xn[b][:].rearrange("p (o d) -> p o d", o=1), hres[:, bass.ds(t, 1), :],
                                      m[b][:, 0:1], r[b][:, 0:1], ALU.subtract, ALU.mult).then_inc(S["xn_ok"], 1)
                if st.has("s"):
                    b = st.two("s")
                    sc = score[b][:, :, :, 0:keys]
                    psv = ps_s[:, :, 0:A * keys].rearrange("p g (a k) -> p g a k", a=A)
                    dve.wait_ge(S["s_ps"], done("s"))
                    if l == 0:
                        src = psv
                    else:
                        dve.wait_ge(M_["rld"][b], 16 * (st.pair("s") + 1))
                        for g in range(G):
                            ins = dve.tensor_tensor(sc[:, g], psv[:, g],
                                                    relb[b][:, :, 3 * g:3 * g + 3].rearrange("p s a -> p a s"),
                                                    ALU.add)
                        ch.link(ins)
                        src = sc
                    ch.link(dve.tensor_reduce(mx[b][:].rearrange("p (g a) -> p g a", g=G), src, AX.X, ALU.max))
                    m4 = mx[b][:].rearrange("p (g a o) -> p g a o", g=G, o=1).to_broadcast([128, G, A, keys])
                    dve.tensor_tensor(sc, src, m4, ALU.subtract).then_inc(S["s_sub"], 1)
                if st.has("o"):
                    b = st.two("o")
                    dve.wait_ge(S["o_ps"], done("o"))
                    o = ps_v[:, 0:H * (DH + 1)].rearrange("p (h e) -> p h e", h=H)
                    ch.link(dve.reciprocal(rden[b][:].rearrange("p (h o) -> p h o", o=1), o[:, :, DH:DH + 1]))
                    dve.tensor_tensor(on[b][:].rearrange("p (h e) -> p h e", h=H), o[:, :, 0:DH],
                                      rden[b][:].rearrange("p (h o) -> p h o", o=1).to_broadcast([128, H, DH]),
                                      ALU.mult).then_inc(S["o_sb"], 1)
                if st.has("emb"):
                    t, b = st.tile("emb"), st.two("emb")
                    dve.wait_ge(M_["tok"][b], 16 * (st.pair("emb") + 1))
                    dve.wait_ge(M_["pos"][b], (32 if l == 0 else 16) * (st.pair("emb") + 1))
                    if l == 0:
                        ch.link(dve.tensor_tensor(emb[b][:], tok[b][:], posb[b][:], ALU.add))
                        ch.link(dve.scalar_tensor_tensor(emb[b][:], typ0[:], typn[:, bass.ds(t, 1)], emb[b][:],
                                                         ALU.mult, ALU.add))
                        ch.link(dve.scalar_tensor_tensor(emb[b][:], typ1[:], typf[:, bass.ds(t, 1)], emb[b][:],
                                                         ALU.mult, ALU.add))
                        dve.sem_inc(S["emb_rd"], 1)
                        moments(emb[b][:], b, mv, "mv_ok")
                    else:
                        ch.link(dve.tensor_scalar(emb[b][:], tok[b][:], wk[0][:, bass.ds(t, 1)], None, ALU.mult))
                        ch.link(dve.scalar_tensor_tensor(emb[b][:], posb[b][:], wk[1][:, bass.ds(t, 1)], emb[b][:],
                                                         ALU.mult, ALU.add))
                        dve.sem_inc(S["emb_rd"], 1)
                        ch.link(dve.tensor_tensor(hres[:, bass.ds(t, 1), :],
                                                  emb[b][:].rearrange("p (o d) -> p o d", o=1),
                                                  hres[:, bass.ds(t, 1), :], ALU.add))
                        moments(hres[:, bass.ds(t, 1), :], b, mv, "mv_ok")
                if st.has("ln"):
                    t, b = st.tile("ln"), st.two("ln")
                    dve.wait_ge(S["rs_ok"], upto(t))
                    dve.wait_ge(S["mv_ok"], upto(t))
                    ch.link(dve.scalar_tensor_tensor(emb[b][:], emb[b][:], mv[b][:, 0:1], gam[:],
                                                     ALU.subtract, ALU.mult))
                    h = hres[:, bass.ds(t, 1), :].rearrange("p o d -> p (o d)")
                    ch.link(dve.scalar_tensor_tensor(h, emb[b][:], rs[b][:, 0:1], bet[:], ALU.mult, ALU.add))
                    moments(h, b, mvb, "mvb_ok")
                if st.has("o"):
                    t, b = st.tile("o"), st.two("o")
                    dve.wait_ge(S["y_ps"], upto(t))
                    h = hres[:, bass.ds(t, 1), :].rearrange("p o d -> p (o d)")
                    if l == 0:
                        after(dve, M_["h1"][b], 32 * st.pair("o"))
                        dve.tensor_tensor(hout[b][:], ps_v[:, 0:D], h, ALU.add).then_inc(S["y_ok"], 1)
                    else:
                        dve.tensor_tensor(h, ps_v[:, 0:D], h, ALU.add).then_inc(S["y_ok"], 1)
            pipeline(dve, ages, body, ch, 9 if l == 0 else 7)

        @block_a.sync
        def _(sp):
            loads = [(ids, ids_h), (typi, typ_h), (relw, relblk), (rel32s, rel32)]
            loads += [(wout4[32 * k:32 * k + NODES], wout) for k in range(4)]
            for (c0, c1), src in [(qk_w[0], wqk0), (v_w[0], wv0), (o_w[0], wo0), (r_w, wr),
                                  (qk_w[1], wqk1), (v_w[1], wv1), (o_w[1], wo1), (in_w, win)]:
                loads += [(c0, src[0:128, :]), (c1, src[128:, :])]
            for dst, src in loads:
                sp.dma_start(dst[:], src).then_inc(const_ld, 16)
            for dst, src in [(gam, gamma), (bet, beta), (typ0, type_w[0:1, :]), (typ1, type_w[1:2, :])]:
                sp.dma_start(dst[:], src.to_broadcast([128, D])).then_inc(const_ld, 16)
            assert len(loads) + 4 == N_CONST, len(loads)
            sp.wait_ge(zero_ok, 1)
            for p in range(2):
                sp.dma_start(rel_d[p][:, (LPAD + REL) * H:], zrow[:]).then_inc(rel_zero, 16)
            zr = xs_d.rearrange("(n p r) d -> n p (r d)", p=128, r=6)
            for n in range(zr.shape[0]):
                sp.dma_start(zr[n], zrow[:, 0:6 * D]).then_inc(xs_zero, 16)
            M_, S, ages = M[0], L[0], AGES[0]
            h1_v = h1_d.rearrange("(t n c) d -> n c t d", n=NT, c=2)

            def body(st):
                if st.has("gather"):
                    t, b = st.tile("gather"), st.two("gather")
                    after(sp, S["emb_rd"], upto(t - 2))
                    settle(sp, spare)
                    for c in range(2):
                        sp.dma_start(posb[b][64 * c:64 * c + 64, :],
                                     pos_w[bass.ds(2 * t + c, 1), :].to_broadcast([64, D])).then_inc(M_["pos"][b], 16)
                if st.has("o"):
                    t, b = st.tile("o"), st.two("o")
                    sp.wait_ge(S["y_ok"], upto(t))
                    settle(sp, spare)
                    for c in range(2):
                        sp.dma_start(h1_v[bass.ds(t, 1), c].rearrange("a t d -> (a t) d"),
                                     hout[b][64 * c:64 * c + 64, :]).then_inc(M_["h1"][b], 16)
            pipeline(sp, ages, body)
            for p in range(2):
                sp.wait_ge(M_["h1"][p], 32 * (NT // 2))

        @block_a.gpsimd
        def _(pool):
            S = L[0]
            pool.memset(zrow[:], 0.0).then_inc(zero_ok, 1)
            pool.memset(ident[:], 0.0).then_inc(pool_c, 1)
            pool.memset(tri[:], 1.0).then_inc(pool_c, 1)
            pool.memset(ones[:], 1.0).then_inc(const_ok, 1)
            pool.memset(mhalf[:], -0.5).then_inc(const_ok, 1)
            pool.memset(epsc[:], EPS).then_inc(pool_c, 1)
            pool.wait_ge(pool_c, 3)
            pool.affine_select(out=ident[:], in_=ident[:], compare_op=ALU.not_equal, fill=1.0, base=0,
                               pattern=[[-1, 128]], channel_multiplier=1).then_inc(const_ok, 1)
            pool.affine_select(out=tri[:], in_=tri[:], compare_op=ALU.is_gt, fill=0.0, base=0,
                               pattern=[[1, 128]], channel_multiplier=-1).then_inc(const_ok, 1)
            pool.wait_ge(const_ld, 16 * N_CONST)
            pool_steps(pool, 0)

        @block_a.tensor
        def _(pe):
            pe.wait_ge(const_ld, 16 * N_CONST)
            pe.wait_ge(const_ok, 8)
            pe_steps(pe, 0)

        @block_a.scalar
        def _(act):
            act.wait_ge(const_ok, 8)
            act.wait_ge(const_ld, 16 * N_CONST)
            act_steps(act, 0)

        @block_a.vector
        def _(dve):
            for p in range(2):
                dve.memset(xT1[p][D1:D1 + 1, :], 1.0)
                dve.memset(oT1[p][D1:D1 + 1, :], 1.0).then_inc(dve_c, 1)
            for p in range(4):
                dve.memset(vv[p][:], 0.0).then_inc(dve_c, 1)
            dve.wait_ge(dve_c, 6)
            for p in range(4):
                vb = vv[p][:].rearrange("p (c r s e) -> p c r s e", c=2, r=H // 2, s=2)
                for s in range(2):
                    ins = dve.memset(vb[64 * s:64 * s + 64, :, :, s, DH:DH + 1], 1.0)
                ins.then_inc(const_ok, 1)
            dve.wait_ge(const_ld, 16 * N_CONST)
            dve.tensor_copy(typf[:], typi[:]).then_inc(dve_c, 1)
            dve.wait_ge(dve_c, 7)
            dve.tensor_scalar(typn[:], typf[:], -1.0, 1.0, ALU.mult, ALU.add).then_inc(dve_c, 1)
            for g in range(G):
                q = slice(32 * g, 32 * g + 32)
                ins = dve.tensor_scalar(relw[q, g * REL:(g + 1) * REL], relw[q, g * REL:(g + 1) * REL],
                                        rel32s[q, 0:1], None, ALU.subtract)
            ins.then_inc(dve_c, 1)
            dve.wait_ge(dve_c, 9)
            dve_steps(dve, 0)

        ctx2.close()

        B_ = {n: sem("B_" + n) for n in ("g_ex", "dve", "cnt_ps", "ready", "pool")}
        h1_ld = [sem(f"h1_ld{c}") for c in range(4)]
        scat = [sem(f"scat{p}") for p in range(2)]
        PER = 16
        Z = [{n: sem(f"Z{z}_{n}") for n in ("st", "ag", "ve", "rs", "xn", "xT_ps", "xT_sb", "lg")} for z in range(2)]
        zT = [ps_t, ps_v]

        def moments_pool(pool, z):
            pool.wait_ge(Z[z]["ag"], NT)
            pool.tensor_scalar(rstd[:], mvar[:, :, 1], EPS, None, ALU.add).then_inc(Z[z]["ve"], 1)
            pool.wait_ge(Z[z]["ve"], 1)
            pool.tensor_tensor(rstd[:], rstd[:], mhalf[:], ALU.pow).then_inc(Z[z]["rs"], 1)

        def moments_dve(dve, z):
            for n in range(NT):
                if z == 0 and n % 16 == 0:
                    dve.wait_ge(h1_ld[n // 16], 16)
                dve.bn_stats(stats[:, n, :], hres[:, n, :]).then_inc(Z[z]["st"], 1)
            for n in range(NT):
                if n % 16 == 0:
                    dve.wait_ge(Z[z]["st"], NT)
                dve.bn_aggr(mvar[:, n, :], stats[:, n, :]).then_inc(Z[z]["ag"], 1)
            dve.wait_ge(Z[z]["ag"], NT)
            dve.wait_ge(Z[z]["rs"], 1)

        def twos(eng, body):
            for n in range(2):
                body(n, n)
            with eng.Fori(0, NT // 2 - 1) as i:
                for p in range(2):
                    body(2 * i + (2 + p), p)

        def norm_all_dve(dve, z):
            def body(n, p):
                after(dve, Z[z]["xT_ps"], upto(n - 2))
                dve.tensor_scalar(xn[p][:].rearrange("p (o d) -> p o d", o=1), hres[:, bass.ds(n, 1), :],
                                  mvar[:, bass.ds(n, 1), 0], rstd[:, bass.ds(n, 1)],
                                  ALU.subtract, ALU.mult).then_inc(Z[z]["xn"], 1)
            twos(dve, body)

        def norm_all_act(act, z):
            def body(n, p):
                act.wait_ge(Z[z]["xT_ps"], upto(n))
                after(act, Z[z]["lg"], upto(n - 2))
                act.activation(xT0[p][:], zT[p][:, 0:128], ACT.Copy)
                act.activation(xT1[p][0:D1, :], zT[p][0:D1, 128:256], ACT.Copy).then_inc(Z[z]["xT_sb"], 1)
            twos(act, body)

        def project_all_pe(pe, z, w, width):
            def project(n, p, out):
                pe.wait_ge(Z[z]["xT_sb"], upto(n))
                rows1 = D1 + 1 if z == 0 else D1
                pe.matmul(out, xT0[p][:], w[0][:], start=True, stop=False)
                pe.matmul(out, xT1[p][0:rows1, :], w[1][:], start=False, stop=True).then_inc(Z[z]["lg"], 1)

            def at(bank, k):
                return ps_s[:, bank, k * width:(k + 1) * width]

            def turn(n, p):
                pe.wait_ge(Z[z]["xn"], upto(n))
                after(pe, Z[z]["xT_sb"], upto(n - 2))
                pe_transpose(pe, zT[p], xn[p][:]).then_inc(Z[z]["xT_ps"], 1)
            for bank in range(NT // PER):
                for k in range(PER):
                    n = bank * PER + k
                    turn(n, n % 2)
                    if n:
                        project(n - 1, (n - 1) % 2, at((n - 1) // PER, (n - 1) % PER))
            project(NT - 1, 1, at(NT // PER - 1, PER - 1))

        with nc.Block() as block:
            @block.sync
            def _(sp):
                hv = h1_d.rearrange("(t b) d -> b t d", b=B)
                for c in range(4):
                    sp.dma_start(hres[:, 16 * c:16 * c + 16, :], hv[:, 16 * c:16 * c + 16, :]).then_inc(h1_ld[c], 16)

            @block.gpsimd
            def _(pool):
                pool.iota(etabi[:], pattern=[[BLK, NBLK]], base=0, channel_multiplier=0).then_inc(B_["pool"], 1)
                pool.iota(cnti[:], pattern=[[-1, E]], base=E, channel_multiplier=0).then_inc(B_["pool"], 1)
                moments_pool(pool, 0)

            @block.tensor
            def _(pe):
                project_all_pe(pe, 0, r_w, E)
                pe.wait_ge(B_["ready"], 1)
                pe.matmul(ps_k[:], tri[:], bigs[5], start=True, stop=True).then_inc(B_["cnt_ps"], 1)
                pe.matmul(ps_v[:], ones[:], bigs[5], start=True, stop=True).then_inc(B_["cnt_ps"], 1)

            @block.scalar
            def _(act):
                norm_all_act(act, 0)
                act.wait_ge(B_["g_ex"], 1)
                act.activation(gat, gat, ACT.Exp).then_inc(B_["g_ex"], 1)

            @block.vector
            def _(dve):
                moments_dve(dve, 0)
                norm_all_dve(dve, 0)
                ch = Chain(dve, B_["dve"])
                k = ch.link
                def flat(j):
                    return bigs[j].rearrange("p (t e) -> p t e", e=E)
                def col(j):
                    return small[:, j, :].rearrange("p (t o) -> p t o", o=1)
                def wide(ap):
                    return ap.to_broadcast([128, NT, E])
                rev = cnt[:, 0, :].rearrange("p (o e) -> p o e", o=1).to_broadcast([128, NT, E])
                dve.wait_ge(B_["pool"], 2)
                k(dve.tensor_copy(cnt[:, 0, :], cnti[:]))
                k(dve.tensor_copy(etab[:], etabi[:]))
                dve.wait_ge(Z[0]["lg"], NT)
                lg = ps_s[:, :, 0:PER * E].rearrange("p b (t e) -> p b t e", e=E)
                gb = gat.rearrange("p (b t) e -> p b t e", b=4)
                k(dve.tensor_copy(gb, lg))
                k(dve.tensor_reduce(small[:, 0, :], gat, AX.X, ALU.max))
                dve.tensor_tensor(gat, gat, wide(col(0)), ALU.subtract).then_inc(B_["g_ex"], 1)
                dve.wait_ge(B_["g_ex"], 2)
                k(dve.tensor_reduce(small[:, 1, :], gat, AX.X, ALU.add))
                k(dve.reciprocal(small[:, 2, :], small[:, 1, :]))
                k(dve.tensor_tensor(gat, gat, wide(col(2)), ALU.mult))
                for r in range(TOPK):
                    k(dve.tensor_reduce(wk[r][:], gat, AX.X, ALU.max))
                    k(dve.tensor_tensor(flat(2), gat, wide(wk[r][:].rearrange("p (t o) -> p t o", o=1)), ALU.is_equal))
                    k(dve.tensor_tensor(flat(2), flat(2), rev, ALU.mult))
                    k(dve.tensor_reduce(small[:, 3, :], flat(2), AX.X, ALU.max))
                    k(dve.tensor_tensor(flat(r), flat(2), wide(col(3)), ALU.is_equal))
                    if r == 0:
                        k(dve.scalar_tensor_tensor(gat, flat(0), -2.0, gat, ALU.mult, ALU.add))
                dve.tensor_tensor(bigs[5], bigs[0], bigs[1], ALU.add).then_inc(B_["ready"], 1)
                dve.wait_ge(B_["cnt_ps"], 2)
                k(dve.memset(small[:, 4, :], 1.0))
                for e in range(E):
                    sc = dve.tensor_tensor_scan(flat(3)[:, :, e], small[:, 4, :],
                                                ps_v[:].rearrange("p (t e) -> p t e", e=E)[:, :, e],
                                                0.0, ALU.mult, ALU.add)
                    k(sc)
                k(dve.tensor_tensor(bigs[4], bigs[3], ps_v[:], ALU.subtract))
                k(dve.tensor_tensor(bigs[4], bigs[4], ps_k[:], ALU.add))
                k(dve.tensor_scalar(cnti[:], flat(3)[:, NT - 1, :], float(BLK - 1), None, ALU.add))
                k(dve.tensor_scalar(cnti[:], cnti[:], BLK.bit_length() - 1, None, ALU.arith_shift_right))
                k(dve.tensor_copy(cnt[:, 1, :], cnti[:]))
                k(dve.tensor_scalar(cnt[:, 1, :], cnt[:, 1, :], float(BLK), None, ALU.mult))
                k(dve.tensor_tensor_scan(cnt[:, 2, :], small[:, 4, 0:E], cnt[:, 1, :], 0.0, ALU.mult, ALU.add))
                k(dve.tensor_tensor(cnt[:, 3, :], cnt[:, 2, :], cnt[:, 1, :], ALU.subtract))
                start = cnt[:, 3, :].rearrange("p (o e) -> p o e", o=1)
                k(dve.tensor_tensor(flat(4), flat(4), start.to_broadcast([128, NT, E]), ALU.add))
                for r in range(TOPK):
                    k(dve.tensor_tensor(flat(2), flat(r), flat(4), ALU.mult))
                    k(dve.tensor_reduce(small[:, 5 + r, :], flat(2), AX.X, ALU.add))
                    k(dve.tensor_copy(posi[r][:], small[:, 5 + r, :]))
                k(dve.tensor_tensor(etmp, etab[:].rearrange("p (j o) -> p j o", o=1).to_broadcast([128, NBLK, E]),
                                    start.to_broadcast([128, NBLK, E]), ALU.is_ge))
                k(dve.tensor_reduce(etab[:], etmp, AX.X, ALU.add))
                k(dve.tensor_scalar(etabi[:], etab[:], -1.0, None, ALU.add))

        C_ = {n: sem("C_" + n) for n in ("ready",)}
        with nc.Block() as block:
            @block.vector
            def _(dve):
                def body(n, p, k):
                    after(dve, scat[p], 32 * k)
                    dve.tensor_copy(idx[p][:], posi[0][:, bass.ds(n, 1)])
                    dve.tensor_copy(idxb[p][:], posi[1][:, bass.ds(n, 1)])
                    dve.tensor_scalar(xn[p][:].rearrange("p (o d) -> p o d", o=1), hres[:, bass.ds(n, 1), :],
                                      mvar[:, bass.ds(n, 1), 0], rstd[:, bass.ds(n, 1)],
                                      ALU.subtract, ALU.mult).then_inc(C_["ready"], 1)
                for p in range(2):
                    body(p, p, 0)
                with dve.Fori(0, NT // 2 - 1) as i:
                    for p in range(2):
                        body(2 * i + (2 + p), p, i + 1)

            @block.gpsimd
            def _(pool):
                pool.wait_ge(xs_zero, 16 * (NBLK * BLK // (128 * 6)))
                with pool.Fori(0, NT // 2) as i:
                    for p in range(2):
                        n = 2 * i + p
                        for ix in (idx, idxb):
                            pool.wait_ge(C_["ready"], n + 1)
                            settle(pool, spare)
                            pool.indirect_dma_start(xs_d, bass.IndirectOffsetOnAxis(ap=ix[p][:], axis=0),
                                                    xn[p][:], None).then_inc(scat[p], 16)
                for p in range(2):
                    pool.wait_ge(scat[p], 32 * (NT // 2))

        D_ = {n: sem("D_" + n) for n in ("xT_ps", "xT_sb", "h_ps", "h_sb", "y_ps", "y_sb", "one")}
        w_ld = [sem(f"w_ld{p}") for p in range(2)]
        y_st = [sem(f"y_st{p}") for p in range(2)]
        w_free = sem("w_free")
        ps_h = [ps_s[:, g, :] for g in range(4)]
        with nc.Block() as block:
            @block.sync
            def _(sp):
                with sp.Fori(0, NBLK // 2) as i:
                    for p in range(2):
                        n = 2 * i + p
                        ex = sp.value_load(etabi[0:1, bass.ds(n, 1)], min_val=0, max_val=E - 1)
                        sp.wait_ge(w_free, n + 1)
                        settle(sp, spare)
                        sp.dma_start(xs[p], xs_d[bass.ds(n * BLK, BLK), :].rearrange("(s p) d -> p s d", s=2))\
                            .then_inc(w_ld[p], 16)
                        sp.dma_start(w1[p][0], w1h[bass.ds(ex, 1), 0:128, :].rearrange("o k i -> (o k) i"))\
                            .then_inc(w_ld[p], 16)
                        sp.dma_start(w1[p][1], w1h[bass.ds(ex, 1), 128:, :].rearrange("o k i -> (o k) i"))\
                            .then_inc(w_ld[p], 16)
                        sp.dma_start(probT[p][:, 0:NI * D], w2h[bass.ds(ex, 1), :, :].rearrange("o k i -> (o k) i"))\
                            .then_inc(w_ld[p], 16)
                        sp.dma_start(b2s[p], b2h[bass.ds(ex, 1), :].to_broadcast([128, D])).then_inc(w_ld[p], 16)
                    for p in range(2):
                        n = 2 * i + p
                        sp.wait_ge(D_["y_sb"], n + 1)
                        settle(sp, spare)
                        sp.dma_start(ys_d[bass.ds(n * BLK, BLK), :].rearrange("(s p) d -> p s d", s=2), ys[p])\
                            .then_inc(y_st[p], 16)
                for p in range(2):
                    sp.wait_ge(y_st[p], 16 * (NBLK // 2))

            @block.tensor
            def _(pe):
                with pe.Fori(0, NBLK // 2) as i:
                    for p in range(2):
                        n = 2 * i + p
                        pe.wait_ge(w_ld[p], 80 * i + 80)
                        pe.wait_ge(D_["xT_sb"], n)
                        for s in range(2):
                            pe.transpose(ps_t[:, s * 128:s * 128 + 128], xs[p][:, s, 0:128], ident[:])
                            last = pe.transpose(ps_t[0:D1, BLK + s * 128:BLK + s * 128 + 128], xs[p][:, s, 128:D],
                                                ident[:])
                        last.then_inc(D_["xT_ps"], 1)
                    for p in range(2):
                        n = 2 * i + p
                        pe.wait_ge(D_["xT_sb"], n + 1)
                        pe.wait_ge(D_["one"], 1)
                        for j in range(NI // 2):
                            bank = (p * 3 + j) % 3
                            pe.wait_ge(D_["h_sb"], n * 3)
                            for c in (2 * j, 2 * j + 1):
                                dst = ps_h[bank][:, (c % 2) * BLK:(c % 2) * BLK + BLK]
                                pe.matmul(dst, w1[p][0][:, c * 128:c * 128 + 128], xsT0[p], start=True, stop=False)
                                last = pe.matmul(dst, w1[p][1][:, c * 128:c * 128 + 128], xsT1[p],
                                                 start=False, stop=True)
                            last.then_inc(D_["h_ps"], 1)
                        pe.wait_ge(D_["h_sb"], n * 3 + 3)
                        pe.wait_ge(D_["y_sb"], n)
                        for s in range(2):
                            for c in range(NI):
                                last = pe.matmul(ps_v[:, s * D:s * D + D], hT[p][:, c, s * 128:s * 128 + 128],
                                                 w2[p][:, c, :], start=(c == 0), stop=(c == NI - 1))
                        last.then_inc(D_["y_ps"], 1)

            @block.scalar
            def _(act):
                with act.Fori(0, NBLK // 2) as i:
                    for p in range(2):
                        n = 2 * i + p
                        act.wait_ge(D_["xT_ps"], n + 1)
                        act.activation(xsT0[p], ps_t[:, 0:BLK], ACT.Copy)
                        act.activation(xsT1[p][0:D1, :], ps_t[0:D1, BLK:2 * BLK], ACT.Copy).then_inc(D_["xT_sb"], 1)
                    for p in range(2):
                        n = 2 * i + p
                        for j in range(NI // 2):
                            act.wait_ge(D_["h_ps"], n * 3 + j + 1)
                            act.activation(hT[p][:, 2 * j:2 * j + 2, :].rearrange("p c t -> p (c t)"), ps_h[j],
                                           ACT.Gelu).then_inc(D_["h_sb"], 1)

            @block.vector
            def _(dve):
                for p in range(2):
                    ins = dve.memset(xsT1[p][D1:D1 + 1, :], 1.0)
                ins.then_inc(D_["one"], 1)
                dve.sem_inc(w_free, 2)
                with dve.Fori(0, NBLK // 2) as i:
                    for p in range(2):
                        n = 2 * i + p
                        dve.wait_ge(D_["y_ps"], n + 1)
                        dve.wait_ge(y_st[p], 16 * i)
                        dve.tensor_tensor(ys[p], ps_v[:, 0:2 * D].rearrange("p (s d) -> p s d", s=2),
                                          b2s[p].rearrange("p (o d) -> p o d", o=1).to_broadcast([128, 2, D]),
                                          ALU.add).then_inc(D_["y_sb"], 1)
                        dve.wait_ge(D_["y_sb"], n + 1)
                        dve.sem_inc(w_free, 1)

        with nc.Block() as block:
            @block.sync
            def _(sp):
                S, M_ = L[1], M[1]
                sp.wait_ge(rel_zero, 32)

                def body(st):
                    if st.has("r"):
                        t, b = st.tile("r"), st.two("r")
                        sp.wait_ge(S["pad_ok"], upto(t))
                        settle(sp, spare)
                        after(sp, M_["rld"][b], 16 * st.pair("r"))
                        settle(sp, spare)
                        sp.dma_start(rel_d[b][:, 0:(LPAD + REL) * H], rpad[b][:].rearrange("p s h -> p (s h)"))\
                            .then_inc(M_["rst"][b], 16)
                        sp.wait_ge(M_["rst"][b], 16 * (st.pair("r") + 1))
                        settle(sp, spare)
                        after(sp, S["s_sub"], upto(t - 2))
                        settle(sp, spare)
                        w = ROWW - H
                        src = rel_d[b].rearrange("t w -> (t w)")[(B - 1) * H:(B - 1) * H + B * w]
                        sp.dma_start(relb[b][:].rearrange("p s h -> p (s h)"),
                                     src.rearrange("(t w) -> t w", w=w)[:, 0:B * H]).then_inc(M_["rld"][b], 16)
                pipeline(sp, AGES[1], body)

            @block.gpsimd
            def _(pool):
                pool_steps(pool, 1)

            @block.tensor
            def _(pe):
                pe_steps(pe, 1)

            @block.scalar
            def _(act):
                act_steps(act, 1)

            @block.vector
            def _(dve):
                for p in range(4):
                    vj = vv[p][:, 0:H * (DH + 1)].rearrange("p (h e) -> p h e", h=H)
                    ins = dve.memset(vj[:, :, DH:DH + 1], 1.0)
                ins.then_inc(dve_c, 1)
                dve.wait_ge(dve_c, 10)
                dve_steps(dve, 1)

        F_ = {n: sem("F_" + n) for n in ("gelu", "dve", "c_ok", "cT_ps", "cT_sb", "o_ps", "o_sb")}
        out_st = [sem(f"out_st{p}") for p in range(2)]
        c4 = [prob[p][:, 0:128] for p in range(2)]
        cT4 = [prob[p][:, 128:256] for p in range(2)]
        ho4 = [score[p][:].rearrange("p g a k -> p (g a k)")[:, 0:4 * D].rearrange("p (k d) -> p k d", k=4)
               for p in range(2)]
        NM = NT // 4
        flog = ps_s[:, :, 0:PER * NODES].rearrange("p b (t n) -> p b t n", n=NODES)
        with nc.Block() as block:
            @block.gpsimd
            def _(pool):
                moments_pool(pool, 1)

            @block.scalar
            def _(act):
                norm_all_act(act, 1)
                act.wait_ge(F_["dve"], 1)
                act.activation(fg.rearrange("p (b t) n -> p b t n", b=4), flog, ACT.Gelu).then_inc(F_["gelu"], 1)
                with act.Fori(0, NM // 2) as i:
                    for p in range(2):
                        m = 2 * i + p
                        act.wait_ge(F_["cT_ps"], m + 1)
                        act.activation(cT4[p], ps_t[:, 0:128], ACT.Copy).then_inc(F_["cT_sb"], 1)

            @block.tensor
            def _(pe):
                project_all_pe(pe, 1, in_w, NODES)
                with pe.Fori(0, NM // 2) as i:
                    for p in range(2):
                        m = 2 * i + p
                        pe.wait_ge(F_["c_ok"], m + 1)
                        pe.wait_ge(F_["cT_sb"], m)
                        pe.transpose(ps_t[:, 0:128], c4[p], ident[:]).then_inc(F_["cT_ps"], 1)
                        pe.wait_ge(F_["cT_sb"], m + 1)
                        pe.wait_ge(F_["o_sb"], m)
                        pe.wait_ge(F_["c_ok"], m + 1)
                        for k in range(4):
                            r = slice(32 * k, 32 * k + NODES)
                            last = pe.matmul(ps_s[:, k, 0:D], cT4[p][r, :], wout4[r, :], start=True, stop=True)
                        last.then_inc(F_["o_ps"], 1)

            @block.vector
            def _(dve):
                ch = Chain(dve, F_["dve"])
                k = ch.link
                moments_dve(dve, 1)
                norm_all_dve(dve, 1)
                dve.wait_ge(Z[1]["lg"], NT)
                k(dve.tensor_scalar(fs.rearrange("p (b t) n -> p b t n", b=4), flog, 0.0, None, ALU.is_gt))
                k(dve.memset(fc[:], 0.0))
                k(dve.memset(fr, 1.0))
                dve.wait_ge(F_["gelu"], 1)

                def children(t, lo, n, side):
                    return t[:, :, 2 * lo + 1:2 * lo + 1 + 2 * n].rearrange("p t (n s) -> p t n s", s=2)[:, :, :, side]

                for lo, n in ((0, 1), (1, 2), (3, 4), (7, 3)):
                    parent = fr[:, :, lo:lo + n]
                    k(dve.tensor_tensor(children(fr, lo, n, 1), parent, fs[:, :, lo:lo + n], ALU.mult))
                    k(dve.tensor_tensor(children(fr, lo, n, 0), parent, children(fr, lo, n, 1), ALU.subtract))
                    for side in range(2):
                        k(dve.tensor_tensor(children(fc, lo, n, side), children(fr, lo, n, side),
                                            fg[:, :, lo:lo + n], ALU.mult))
                last_r, last_c = fr[:, :, LAST:NODES], fc[:, :, LAST:NODES]
                c3 = lambda j: small[:, j, :].rearrange("p (t o) -> p t o", o=1)
                k(dve.tensor_reduce(small[:, 0, :], fr[:, :, 10:15], AX.X, ALU.add))
                k(dve.tensor_tensor(last_r, last_r, c3(0), ALU.add))
                prod = probT[0][:, 0:NT * NODES]\
                    .rearrange("p (t n) -> p t n", n=NODES)
                k(dve.tensor_tensor(prod, fr, fg, ALU.mult))
                k(dve.tensor_reduce(small[:, 1, :], prod[:, :, 10:NODES], AX.X, ALU.add))
                k(dve.tensor_tensor(last_c, last_c, c3(1), ALU.add))
                k(dve.scalar_tensor_tensor(last_c, fg[:, :, LAST:NODES], 5.0, last_c, ALU.mult, ALU.add))
                with dve.Fori(0, NM // 2) as i:
                    for p in range(2):
                        m = 2 * i + p
                        dve.wait_ge(F_["cT_ps"], 2 * i)
                        dve.wait_ge(F_["gelu"], 1)
                        dve.tensor_copy(c4[p].rearrange("p (k n) -> p k n", k=4), fc[:, bass.ds(4 * m, 4), :])\
                            .then_inc(F_["c_ok"], 1)
                    for p in range(2):
                        m = 2 * i + p
                        dve.wait_ge(F_["o_ps"], m + 1)
                        dve.wait_ge(out_st[p], 16 * i)
                        dve.tensor_tensor(ho4[p], ps_s[:, :, 0:D], hres[:, bass.ds(4 * m, 4), :], ALU.add)\
                            .then_inc(F_["o_sb"], 1)

            @block.sync
            def _(sp):
                ov = out.rearrange("t b d -> b t d")
                with sp.Fori(0, NM // 2) as i:
                    for p in range(2):
                        m = 2 * i + p
                        sp.wait_ge(F_["o_sb"], m + 1)
                        settle(sp, spare)
                        sp.dma_start(ov[:, bass.ds(4 * m, 4), :], ho4[p]).then_inc(out_st[p], 16)
                for p in range(2):
                    sp.wait_ge(out_st[p], 16 * (NM // 2))


def rows(w, b):
    out = np.zeros((w.shape[0] + 1, w.shape[1]), np.float32)
    out[:-1] = w
    out[-1] = b
    return out


def head_slots(wq, bq, wk, bk):
    out = np.zeros((D + 1, 2, A, G, 32), np.float32)
    for side, (w, b) in enumerate(((wq, bq), (wk, bk))):
        out[:, side, :, :, 0:DH] = rows(w, b).reshape(D + 1, G, A, DH).transpose(0, 2, 1, 3)
    return out.reshape(D + 1, 2 * A * 128)


def laid_out(v):
    a = {k: np.asarray(x) for k, x in v.items()}
    qkv, qb = a["L1_attn_qkv_w"], a["L1_attn_qkv_b"]
    rel = a["L1_attn_rel_pos_emb"]
    relblk = np.zeros((G, 32, G, REL), np.float32)
    rel32 = np.zeros((G, 32, 1), np.float32)
    for g in range(G):
        relblk[g, 0:DH, g, :] = rel.T
        rel32[g, 0:DH, 0] = rel[REL - 1]
    w1 = np.zeros((E, D + 1, I), np.float32)
    w1[:, :D] = a["L0_ffn_W1"]
    w1[:, D] = a["L0_ffn_b1"]
    return {
        "ids_h": a["x"].T.reshape(NT, 128).T,
        "typ_h": a["mask_BS_i1_0"].T.reshape(NT, 128).T,
        "tok_w": a["L0_tok_tok_w"], "pos_w": a["L0_tok_pos_w"], "type_w": a["L0_tok_type_w"],
        "gamma": a["L0_tok_gamma"].reshape(1, D), "beta": a["L0_tok_beta"].reshape(1, D),
        "wqk0": head_slots(a["L0_attn_Wq"].T, a["L0_attn_bq"], a["L0_attn_Wk"].T, a["L0_attn_bk"]),
        "wv0": rows(a["L0_attn_Wv"].T, a["L0_attn_bv"]),
        "wo0": rows(a["L0_attn_Wout"].T, a["L0_attn_bout"]),
        "w1h": w1,
        "w2h": a["L0_ffn_W2"].reshape(E, NI, 128, D).transpose(0, 2, 1, 3).reshape(E, 128, NI * D),
        "b2h": a["L0_ffn_b2"],
        "wr": rows(a["L0_ffn_Wr"], a["L0_ffn_br"]),
        "wqk1": head_slots(qkv[0:D].T, qb[0:D], qkv[D:2 * D].T, qb[D:2 * D]),
        "wv1": rows(qkv[2 * D:].T, qb[2 * D:]),
        "wo1": rows(a["L1_attn_out_w"].T, a["L1_attn_out_b"]),
        "relblk": relblk.reshape(128, G * REL), "rel32": rel32.reshape(128, 1),
        "win": a["L1_ffn_weights_in"].T, "wout": a["L1_ffn_weights_out"],
    }


def build(nc, arrays, dbg):
    args = [nc.dram_tensor(n, x.shape, mybir.dt.from_np(x.dtype), kind="ExternalInput").ap()
            for n, x in arrays.items()]
    out = nc.dram_tensor("out_0_dram", [T, B, D], F32, kind="ExternalOutput").ap()
    tower(nc, dbg, *args, out)


def kernel(**inputs):
    import concourse.bacc as bacc
    from concourse.bass_utils import run_bass_kernel_spmd

    arrays = {n: np.ascontiguousarray(x) for n, x in laid_out(inputs).items()}
    nc = bacc.Bacc("TRN2", target_bir_lowering=False, num_devices=1)
    build(nc, arrays, {})
    r = run_bass_kernel_spmd(nc, [arrays], core_ids=[0])
    return r.results[0]["out_0_dram"]
```

```python
from contextlib import ExitStack

import numpy as np

import concourse.bass as bass
from concourse import mybir

F32 = mybir.dt.float32
F32R = mybir.dt.float32r
I32 = mybir.dt.int32
U32 = mybir.dt.uint32
ALU = mybir.AluOpType
ACT = mybir.ActivationFunctionType
AX = mybir.AxisListType

T, B = 64, 128
D = 192
D1 = D - 128
NT = T * B // 128
H, DH = 12, 16
G, A = 4, 3
QS = 2
E, TOPK, I = 8, 2, 768
NI = I // 128
BLK = 256
NBLK = T * B * TOPK // BLK + E
REL = 33
MAXREL = 16
LPAD = B - 1 - MAXREL
ROWW = (2 * B - 1) * H
NODES = 21
LAST = NODES - 1
EPS = 1e-5
SCALE = DH ** -0.5


class Chain:

    def __init__(self, eng, sem):
        self.eng, self.sem, self.at, self.base, self.per = eng, sem, 0, 0, 0

    def loop(self, step, per):
        self.base, self.at = self.at + step * per, 0

    def step(self, ins):
        self.at += 1
        ins.then_inc(self.sem, 1)

    def done(self):
        self.eng.wait_ge(self.sem, self.base + self.at)

    def link(self, ins):
        self.step(ins)
        self.done()


def upto(t, tiles=NT):
    return max(0, min(t + 1, tiles)) if isinstance(t, int) else t + 1


def after(eng, sem, value):
    if not isinstance(value, int) or value > 0:
        eng.wait_ge(sem, value)


UNROLL = 4


class Step:

    def __init__(self, ages, n, half_n, p, tiles):
        self.ages, self.n, self.half_n, self.p, self.tiles = ages, n, half_n, p, tiles

    def has(self, k):
        return k in self.ages and (not isinstance(self.n, int) or 0 <= self.n - self.ages[k] < self.tiles)

    def tile(self, k):
        return self.n - self.ages[k]

    def pair(self, k):
        return self.half_n + (self.p % 2 - self.ages[k]) // 2

    def two(self, k):
        return (self.p - self.ages[k]) % 2

    def four(self, k):
        return (self.p - self.ages[k]) % 4


def pipeline(eng, ages, body, links=None, per=0, tiles=NT):
    head = UNROLL * (2 if max(ages.values()) < 8 else 3)

    for n in range(head):
        body(Step(ages, n, n // 2, n % UNROLL, tiles))
    at0 = links.at if links else 0
    with eng.Fori(0, (tiles - head) // UNROLL) as i:
        if links:
            links.base, links.at = at0 + i * (per * UNROLL), 0
        for p in range(UNROLL):
            body(Step(ages, UNROLL * i + (head + p), 2 * i + (head + p) // 2, p, tiles))
    if links:
        assert links.at == per * UNROLL, (links.at, per)
        links.base, links.at = 0, at0 + per * (tiles - head)
    for n in range(tiles, tiles + max(ages.values())):
        body(Step(ages, n, n // 2, n % UNROLL, tiles))


AGES = [dict(gather=0, emb=1, ln=2, xn=3, qk=4, v=5, s=5, pt=6, o=7, y=8, z=9, lg=10),
        dict(gather=0, emb=1, xn=2, qk=3, v=4, r=3, s=5, pt=6, o=7, y=8, z=9, lg=10)]


def settle(eng, spare):
    eng.sem_inc(spare, 1)


def tower(nc, ids_h, typ_h, tok_w, pos_w, type_w, gamma, beta,
          wqk0, wv0, wo0, w1h, b1h, w2h, b2h, wr, wqk1, wv1, wo1, relblk, rel32, win, wout, out):
    h1_d = nc.dram_tensor("h1_d", [T * B, D], F32).ap()
    xs_d = nc.dram_tensor("xs_d", [NBLK * BLK, D], F32).ap()
    ys_d = nc.dram_tensor("ys_d", [NBLK * BLK, D], F32).ap()
    route_d = nc.dram_tensor("route_d", [2 * TOPK, T * B], F32).ap()
    rel_d = [nc.dram_tensor(f"rel_d{p}", [B, ROWW], F32).ap() for p in range(2)]

    with ExitStack() as ctx:
        def sb(name, shape, dt=F32):
            return ctx.enter_context(nc.sbuf_tensor(name, shape, dt))

        def two(name, shape, dt=F32):
            return [sb(f"{name}{p}", shape, dt) for p in range(2)]

        def sem(name):
            return ctx.enter_context(nc.semaphore(name))

        ps_s = ctx.enter_context(nc.psum_tensor("ps_s", [128, G, 512], F32))
        ps_t = ctx.enter_context(nc.psum_tensor("ps_t", [128, 512], F32))
        ps_q = ctx.enter_context(nc.psum_tensor("ps_q", [128, 512], F32))
        ps_k = ctx.enter_context(nc.psum_tensor("ps_k", [128, 512], F32))
        ps_v = ctx.enter_context(nc.psum_tensor("ps_v", [128, 512], F32))
        ps_pt = [ps_q, ps_k]

        ident = sb("ident", [128, 128])
        tri = sb("tri", [128, 128])
        ones = sb("ones", [128, 128])
        mhalf = sb("mhalf", [128, NT])
        epsc = sb("epsc", [128, 1])
        zrow = sb("zrow", [128, LPAD * H])
        gam = sb("gam", [128, D])
        bet = sb("bet", [128, D])
        typ0 = sb("typ0", [128, D])
        typ1 = sb("typ1", [128, D])
        ids = sb("ids", [128, NT], I32)
        typi = sb("typi", [128, NT], I32)
        typf = sb("typf", [128, NT])
        typn = sb("typn", [128, NT])
        relw = sb("relw", [128, A * G * REL])
        rel32s = sb("rel32s", [128, 2])

        def weights(name, n):
            return sb(name + "_c0", [128, n]), sb(name + "_c1", [D1 + 1, n])

        qk_w = [weights("wqk0", (QS + A) * 128), weights("wqk1", (QS + A) * 128)]
        v_w = [weights("wv0", D), weights("wv1", D)]
        o_w = [weights("wo0", D), weights("wo1", D)]
        r_w = weights("wr", E)
        in_w = (sb("win_c0", [128, NODES]), sb("win_c1", [D1, NODES]))
        lg_w = [r_w, in_w]

        hres = sb("hres", [128, NT, D])
        logits = sb("logits", [128, NT, NODES])
        mean = sb("mean", [128, NT])
        rstd = sb("rstd", [128, NT])
        wk = [sb(f"wk{k}", [128, NT]) for k in range(TOPK)]
        posi = [sb(f"posi{k}", [128, NT], U32) for k in range(TOPK)]
        turned = sb("turned", [NT, 2 * TOPK, 128])
        route2 = sb("route2", [128, 2 * TOPK, NT])
        posi2 = [sb(f"posi2{k}", [128, NT], U32) for k in range(TOPK)]

        def four(name, shape, dt=F32):
            return [sb(f"{name}{p}", shape, dt) for p in range(4)]

        idx = two("idx", [128, 1], U32)
        idxb = two("idxb", [128, 1], U32)
        SCAT = 4
        sidx = [[sb(f"sidx{p}{k}", [128, 1], U32) for k in range(TOPK)] for p in range(SCAT)]
        tok = two("tok", [128, D])
        posb = two("posb", [128, D])
        emb = two("emb", [128, D])
        st6 = two("st6", [128, 6])
        st6z = two("st6z", [128, 6])
        mvz = two("mvz", [128, 2])
        rsz = two("rsz", [128, 1])
        vepsz = two("vepsz", [128, 1])
        zn = two("zn", [128, D])
        zT0 = two("zT0", [128, 128])
        zT1 = two("zT1", [D1 + 1, 128])
        mv = two("mv", [128, 2])
        mvb = two("mvb", [128, 2])
        veps = two("veps", [128, 1])
        rs = two("rs", [128, 1])
        rs2 = two("rs2", [128, 1])
        xn = two("xn", [128, D])
        xT0 = two("xT0", [128, 192])
        xT1 = two("xT1", [D1 + 1, 192])
        qT = four("qT", [128, QS, 128])
        kT = four("kT", [128, A, 128])
        vv = four("vv", [128, 2 * (H // 2) * 2 * (DH + 1)])
        score = two("score", [128, G, A, 128])
        mx = two("mx", [128, H])
        prob = two("prob", [128, H * 128])
        probT = two("probT", [128, H * 128])
        rden = two("rden", [128, H])
        on = two("on", [128, D])
        oT0 = two("oT0", [128, 128])
        oT1 = two("oT1", [D1 + 1, 128])

        srow = xn + zn
        w1 = [[score[p][:].rearrange("p g a k -> p (g a k)")[:, c * I:(c + 1) * I] for c in range(2)]
              for p in range(2)]
        b1s = two("b1s", [128, NI])
        w2 = [probT[p][:, 0:NI * D].rearrange("p (c d) -> p c d", c=NI) for p in range(2)]
        hT = [prob[p][:].rearrange("p (c t) -> p c t", c=NI) for p in range(2)]
        b2s = [tok[p][:] for p in range(2)]
        gat = probT[1][:, 0:NT * E].rearrange("p (t e) -> p t e", e=E)
        bigs = [score[j // 3][:].rearrange("p g a k -> p (g a k)")[:, 512 * (j % 3):512 * (j % 3) + 512]
                for j in range(6)]
        small = sb("small", [128, 12, NT])
        etab = sb("etab", [128, NBLK])
        etabi = sb("etabi", [128, NBLK], I32)
        cnt = sb("cnt", [128, 6, E])
        cnti = sb("cnti", [128, E], I32)
        etmp = probT[0][:, 0:NBLK * E].rearrange("p (j e) -> p j e", e=E)
        wout4 = sb("wout4", [128, 4, D])

        def dsem(name):
            return sem("ld_" + name)

        const_ld = dsem("const")
        N_CONST = 14
        ZROWS = 3
        ids_ld = dsem("ids")
        late_ld = dsem("late")
        pool_c = sem("pool_c")
        const_ok = sem("const_ok")
        zero_ok = sem("zero_ok")
        xs_zero = sem("xs_zero")
        rel_zero = sem("rel_zero")
        NAMES = ("idx_ok", "emb_rd", "mv_ok", "rs_ok", "mvb_ok", "rsb_ok", "pool", "dve", "xn_ok", "xT_ps",
                 "xT_sb", "q_ps", "q_sb", "k_ps", "k_sb", "r_ps", "r_sb", "pad_ok", "v_ps", "v_sb", "s_ps",
                 "s_rd", "s_sub", "p_sb", "pt_ps", "pt_sb", "o_ps", "o_sb", "oT_ps", "oT_sb", "y_ps", "y_ok",
                 "mvz_ok", "rsz_ok", "zn_ok", "zT_ps", "zT_sb", "lg_ps", "lg_sb")
        L = [{n: sem(f"L{l}_{n}") for n in NAMES} for l in range(2)]
        DMAS = ("tok", "pos", "h1", "rst", "rld")
        M = [{n: [sem(f"L{l}_{n}{p}") for p in range(2)] for n in DMAS} for l in range(2)]
        dve_c = sem("dve_c")
        spare = sem("spare")
        ctx2 = ExitStack()
        block_a = ctx2.enter_context(nc.Block())
        def pool_steps(pool, l):
            S, M_, ages = L[l], M[l], AGES[l]
            src = [(idx, ids, tok, tok_w, M_["tok"])]
            if l == 1:
                src = [(idx, posi2[0], tok, ys_d, M_["tok"]), (idxb, posi2[1], posb, ys_d, M_["pos"])]

            def rsqrt(t, b, var_ok, var, out_ok, out, veps=veps):
                pool.wait_ge(S[var_ok], upto(t))
                pool.tensor_tensor(veps[b][:], var[b][:, 1:2], epsc[:], ALU.add).then_inc(S["pool"], 1)
                ch.at += 1
                pool.wait_ge(S["pool"], ch.base + ch.at)
                pool.tensor_tensor(out[b][:], veps[b][:], mhalf[:, 0:1], ALU.pow).then_inc(S[out_ok], 1)

            ch = Chain(pool, S["pool"])

            def body(st):
                if st.has("gather"):
                    t, b = st.tile("gather"), st.two("gather")
                    for ix, ids_, dst, table, ld in src:
                        after(pool, ld[b], 16 * st.pair("gather"))
                        pool.tensor_copy(ix[b][:], ids_[:, bass.ds(t, 1)]).then_inc(S["idx_ok"], 1)
                    pool.wait_ge(S["idx_ok"], len(src) * upto(t))
                    after(pool, S["emb_rd"], upto(t - 2))
                    settle(pool, spare)
                    for ix, ids_, dst, table, ld in src:
                        pool.indirect_dma_start(dst[b][:], None, table,
                                                bass.IndirectOffsetOnAxis(ap=ix[b][:], axis=0)).then_inc(ld[b], 16)
                if st.has("ln"):
                    rsqrt(st.tile("ln"), st.two("ln"), "mvb_ok", mvb, "rsb_ok", rs2)
                if st.has("emb"):
                    rsqrt(st.tile("emb"), st.two("emb"), "mv_ok", mv, "rs_ok", rs)
                if st.has("z"):
                    rsqrt(st.tile("z"), st.two("z"), "mvz_ok", mvz, "rsz_ok", rsz, vepsz)
                if st.has("r"):
                    t, b = st.tile("r"), st.two("r")
                    pool.wait_ge(S["r_sb"], upto(t))
                    settle(pool, spare)
                    pool.tensor_scalar(rpad[b][:, 0:LPAD, :],
                                       rpad[b][:, LPAD:LPAD + 1, :].to_broadcast([128, LPAD, H]),
                                       1.0, None, ALU.mult).then_inc(S["pad_ok"], 1)
            pipeline(pool, ages, body, ch, 3 - l)

        def pe_transpose(pe, dst, src):
            pe.transpose(dst[:, 0:128], src[:, 0:128], ident[:])
            return pe.transpose(dst[0:D1, 128:256], src[:, 128:D], ident[:])

        def pe_project(pe, dst, x0, x1, w):
            pe.matmul(dst, x0, w[0][:], start=True, stop=False)
            return pe.matmul(dst, x1, w[1][:], start=False, stop=True)

        def pe_steps(pe, l):
            S, ages = L[l], AGES[l]
            keys = 64 if l == 0 else 128
            npt = 2 if l == 0 else 3
            W = DH + 1

            def body(st):
                done = lambda k: upto(st.n - ages[k])
                before = lambda k: upto(st.n - ages[k] - 1)
                x = st.p % 2 if l == 1 else 0
                bank = (ps_pt[x], ps_pt[1 - x])

                def scores(j):
                    q4, a, g = st.four("s"), j // G, j % G
                    q = slice(32 * g, 32 * g + 32)
                    for c in range(128 // keys):
                        t = slice(keys * c, keys * c + keys)
                        last = pe.matmul(ps_s[t, g, a * keys:a * keys + keys], qT[q4][q, a // 2, t],
                                         kT[q4][q, a, t], start=True, stop=True)
                    if j == H - 1:
                        last.then_inc(S["s_ps"], 1)

                def queries_keys(j):
                    side, slot, chunk = int(j >= 2 * QS), j // 2, j % 2
                    b = st.two("qk")
                    if j == 0:
                        pe.wait_ge(S["xT_sb"], done("qk"))
                        after(pe, S["q_sb"], before("qk"))
                        after(pe, S["k_sb"], before("qk"))
                    if j in (0, 2 * QS):
                        after(pe, S["pt_sb"], npt * before("pt") - 1 + side)
                    o, a = slot * 128, slot - side * QS
                    last = pe.matmul(bank[side][:, a * 128:a * 128 + 128], qk_w[l][chunk][:, o:o + 128],
                                     (xT0, xT1)[chunk][b][:, 0:128], start=(chunk == 0), stop=(chunk == 1))
                    if j in (2 * QS - 1, 2 * (QS + A) - 1):
                        last.then_inc(S["k_ps" if side else "q_ps"], 1)

                def out_project():
                    b = st.two("y")
                    pe.wait_ge(S["oT_sb"], done("y"))
                    after(pe, S["o_sb"], before("o"))
                    after(pe, S["v_sb"], done("v"))
                    pe_project(pe, ps_v[:, 0:D], oT0[b][:], oT1[b][:], o_w[l]).then_inc(S["y_ps"], 1)

                def values():
                    b = st.two("v")
                    pe.wait_ge(S["xT_sb"], done("v"))
                    after(pe, S["v_sb"], before("v"))
                    after(pe, S["y_ok"], before("y"))
                    after(pe, S["o_sb"], before("o"))
                    last = pe_project(pe, ps_v[:, 0:D], xT0[b][:, 0:128], xT1[b][:, 0:128], v_w[l])
                    if l == 0:
                        last = pe_project(pe, ps_v[:, D:2 * D], xT0[b][:, 64:192], xT1[b][:, 64:192], v_w[l])
                    last.then_inc(S["v_ps"], 1)

                def turn_probs(j, per):
                    b, t = st.two("pt"), st.tile("pt")
                    u = j // per
                    if j == 0:
                        pe.wait_ge(S["p_sb"], upto(t))
                        after(pe, S["q_sb"], done("qk"))
                    if j == per:
                        after(pe, S["k_sb"], done("qk"))
                    if j == 2 * per:
                        pe.wait_ge(S["pt_sb"], npt * t + 1)
                    k = j % per
                    last = pe.transpose(bank[u % 2][:, k * 128:k * 128 + 128], prob[b][:, j * 128:j * 128 + 128],
                                        ident[:])
                    if k == per - 1:
                        last.then_inc(S["pt_ps"], 1)

                def sums(j):
                    b, v = st.two("o"), st.four("o")
                    if l == 0:
                        r, c = j // 2, j % 2
                        o = (c * (H // 2) + r) * 2 * W
                        last = pe.matmul(ps_v[64 * c:64 * c + 64, r * 2 * W:(r + 1) * 2 * W],
                                         probT[b][:, r * 128 + 64 * c:r * 128 + 64 * c + 64],
                                         vv[v][:, o:o + 2 * W], start=True, stop=True)
                    else:
                        last = pe.matmul(ps_v[:, j * W:(j + 1) * W], probT[b][:, j * 128:j * 128 + 128],
                                         vv[v][:, j * W:(j + 1) * W], start=True, stop=True)
                    if j == H - 1:
                        last.then_inc(S["o_ps"], 1)

                def bank_t_free(turned_sums, turned_r, turned_x):
                    after(pe, S["oT_sb"], turned_sums("y"))
                    after(pe, S["lg_sb"], turned_sums("lg"))
                    if l == 1:
                        after(pe, S["r_sb"], turned_r("r"))
                    after(pe, S["xT_sb"], turned_x("xn"))
                    after(pe, S["zT_sb"], turned_x("z"))

                def turn_sums():
                    pe.wait_ge(S["o_sb"], done("y"))
                    pe_transpose(pe, ps_t, on[st.two("y")][:]).then_inc(S["oT_ps"], 1)

                def logits_of_outputs():
                    b, (w0, w1) = st.two("lg"), lg_w[l]
                    dst = ps_t[:, 256:256 + w0.shape[1]]
                    pe.wait_ge(S["zT_sb"], done("lg"))
                    pe.matmul(dst, zT0[b][:], w0[:], start=True, stop=False)
                    pe.matmul(dst, zT1[b][0:w1.shape[0], :], w1[:], start=False, stop=True).then_inc(S["lg_ps"], 1)

                def relative():
                    pe.wait_ge(S["q_sb"], done("r"))
                    bank_t_free(done, before, before)
                    q4 = st.four("r")
                    for s, cols in enumerate((slice(0, 2 * G * REL), slice(2 * G * REL, 3 * G * REL))):
                        last = pe.matmul(ps_t[:, cols], qT[q4][:, s, :], relw[:, cols], start=True, stop=True)
                    last.then_inc(S["r_ps"], 1)

                per = 3 if l == 0 else 4
                if st.has("s"):
                    pe.wait_ge(S["q_sb"], done("s"))
                    pe.wait_ge(S["k_sb"], done("s"))
                    after(pe, S["s_rd" if l == 1 else "s_sub"], before("s"))
                    for j in range(H // 2):
                        scores(j)
                if st.has("v"):
                    values()
                bank_t_free(before, before, before)
                if st.has("y"):
                    turn_sums()
                if st.has("lg"):
                    logits_of_outputs()
                if st.has("qk"):
                    for j in range(2 * QS):
                        queries_keys(j)
                if st.has("y"):
                    out_project()
                if st.has("s"):
                    for j in range(H // 2, H):
                        scores(j)
                if st.has("qk"):
                    for j in range(2 * QS, 2 * (QS + A)):
                        queries_keys(j)
                if st.has("pt"):
                    for j in range(per):
                        turn_probs(j, per)
                if st.has("o"):
                    pe.wait_ge(S["pt_sb"], npt * done("o"))
                    after(pe, S["v_sb"], done("v"))
                    after(pe, S["y_ok"], done("y"))
                    for j in range(H // 2):
                        sums(j)
                if st.has("pt"):
                    for j in range(per, 2 * per):
                        turn_probs(j, per)
                if st.has("r"):
                    relative()
                if st.has("o"):
                    for j in range(H // 2, H):
                        sums(j)
                if st.has("pt") and npt == 3:
                    for j in range(2 * per, 3 * per):
                        turn_probs(j, per)
                bank_t_free(done, done, before)
                if st.has("xn"):
                    pe.wait_ge(S["xn_ok"], done("xn"))
                    pe_transpose(pe, ps_t[:, 0:256], xn[st.two("xn")][:]).then_inc(S["xT_ps"], 1)
                if st.has("z"):
                    pe.wait_ge(S["zn_ok"], done("z"))
                    pe_transpose(pe, ps_t[:, 256:512], zn[st.two("z")][:]).then_inc(S["zT_ps"], 1)
            pipeline(pe, ages, body)

        def act_steps(act, l):
            S, ages = L[l], AGES[l]
            keys = 64 if l == 0 else 128
            npt = 2 if l == 0 else 3

            def body(st):
                done = lambda k: upto(st.n - ages[k])
                x = st.p % 2 if l == 1 else 0
                bank = (ps_pt[x], ps_pt[1 - x])

                def turned_probs(u):
                    b, w = st.two("pt"), 384 if l == 0 else 512
                    act.wait_ge(S["pt_ps"], npt * st.tile("pt") + u + 1)
                    act.activation(probT[b][:, u * w:(u + 1) * w], bank[u % 2][:, 0:w], ACT.Copy)\
                        .then_inc(S["pt_sb"], 1)

                def turned_sums():
                    if st.has("y"):
                        b = st.two("y")
                        act.wait_ge(S["oT_ps"], done("y"))
                        after(act, S["lg_ps"], done("lg"))
                        act.activation(oT0[b][:], ps_t[:, 0:128], ACT.Copy)
                        act.activation(oT1[b][0:D1, :], ps_t[0:D1, 128:256], ACT.Copy).then_inc(S["oT_sb"], 1)
                    if st.has("lg"):
                        w = lg_w[l][0].shape[1]
                        act.wait_ge(S["lg_ps"], done("lg"))
                        act.activation(logits[:, bass.ds(st.tile("lg"), 1), 0:w],
                                       ps_t[:, 256:256 + w].rearrange("p (o e) -> p o e", o=1),
                                       ACT.Copy).then_inc(S["lg_sb"], 1)

                if st.has("pt"):
                    b = st.two("pt")
                    act.wait_ge(S["s_sub"], done("pt"))
                    act.activation(prob[b][:, 0:H * keys].rearrange("p (g a k) -> p g a k", g=G, a=A),
                                   score[b][:, :, :, 0:keys], ACT.Exp, scale=SCALE).then_inc(S["p_sb"], 1)
                if st.has("v"):
                    v = st.four("v")
                    act.wait_ge(S["v_ps"], done("v"))
                    if l == 0:
                        vb = vv[v][:].rearrange("p (c r s e) -> p c r s e", c=2, r=H // 2, s=2)
                        pv = ps_v[:, 0:2 * D].rearrange("p (w r s e) -> p w r s e", w=2, r=H // 2, s=2)
                        for c in range(2):
                            for s in range(2):
                                ins = act.activation(vb[64 * s:64 * s + 64, c, :, s, 0:DH],
                                                     pv[64 * s:64 * s + 64, 0 if s == c else 1, :, s, :], ACT.Copy)
                    else:
                        vj = vv[v][:, 0:H * (DH + 1)].rearrange("p (h e) -> p h e", h=H)
                        ins = act.activation(vj[:, :, 0:DH], ps_v[:, 0:D].rearrange("p (h e) -> p h e", h=H),
                                             ACT.Copy)
                    ins.then_inc(S["v_sb"], 1)
                turned_sums()
                if st.has("qk"):
                    q4 = st.four("qk")
                    act.wait_ge(S["q_ps"], done("qk"))
                    act.activation(qT[q4][:], bank[0][:, 0:QS * 128].rearrange("p (a t) -> p a t", a=QS),
                                   ACT.Copy).then_inc(S["q_sb"], 1)
                if st.has("qk"):
                    q4 = st.four("qk")
                    act.wait_ge(S["k_ps"], done("qk"))
                    src = bank[1][:, 0:A * 128].rearrange("p (a t) -> p a t", a=A)
                    if l == 0:
                        act.activation(kT[q4][:], src, ACT.Copy).then_inc(S["k_sb"], 1)
                    else:
                        act.activation(kT[q4][:, 0:3:2], src[:, 0:3:2], ACT.Identity, bias=rel32s[:, 0:1])
                        act.activation(kT[q4][:, 1], src[:, 1], ACT.Identity, bias=rel32s[:, 1:2])\
                            .then_inc(S["k_sb"], 1)
                if st.has("pt"):
                    turned_probs(0)
                    turned_probs(1)
                if st.has("r"):
                    b = st.two("r")
                    act.wait_ge(S["r_ps"], done("r"))
                    after(act, M[l]["rst"][b], 16 * st.pair("r"))
                    src = ps_t[:, 0:A * G * REL].rearrange("p (a g j) -> p a g j", a=A, g=G)
                    dst = rpad[b][:, LPAD:LPAD + REL, :].rearrange("p j (g a) -> p a g j", g=G)
                    for a in range(A):
                        ins = act.activation(dst[:, a], src[:, a], ACT.Copy)
                    ins.then_inc(S["r_sb"], 1)
                if st.has("pt") and npt == 3:
                    turned_probs(2)
                if st.has("xn"):
                    b = st.two("xn")
                    act.wait_ge(S["xT_ps"], done("xn"))
                    after(act, S["zT_ps"], done("z"))
                    if l == 0:
                        act.activation(xT0[b][:, 128:192], ps_t[:, 0:64], ACT.Copy)
                        act.activation(xT1[b][0:D1, 128:192], ps_t[0:D1, 128:192], ACT.Copy)
                    act.activation(xT0[b][:, 0:128], ps_t[:, 0:128], ACT.Copy)
                    act.activation(xT1[b][0:D1, 0:128], ps_t[0:D1, 128:256], ACT.Copy).then_inc(S["xT_sb"], 1)
                if st.has("z"):
                    b = st.two("z")
                    act.wait_ge(S["zT_ps"], done("z"))
                    act.activation(zT0[b][:], ps_t[:, 256:384], ACT.Copy)
                    act.activation(zT1[b][0:D1, :], ps_t[0:D1, 384:512], ACT.Copy).then_inc(S["zT_sb"], 1)
            pipeline(act, ages, body)

        def dve_steps(dve, l):
            S, M_, ages = L[l], M[l], AGES[l]
            keys = 64 if l == 0 else 128
            ch = Chain(dve, S["dve"])

            def moments(x, b, mom, name, st6=st6):
                settle(dve, spare)
                ch.link(dve.bn_stats(st6[b][:], x))
                settle(dve, spare)
                dve.bn_aggr(mom[b][:], st6[b][:]).then_inc(S[name], 1)

            def body(st):
                done = lambda k: upto(st.n - ages[k])
                before2 = lambda k: upto(st.n - ages[k] - 2)
                def embed_and_normalise():
                    te, be, tl, bl = st.tile("emb"), st.two("emb"), st.tile("ln"), st.two("ln")
                    if st.has("emb"):
                        dve.wait_ge(M_["tok"][be], 16 * (st.pair("emb") + 1))
                        dve.wait_ge(M_["pos"][be], 32 * (st.pair("emb") + 1))
                        ch.step(dve.tensor_tensor(emb[be][:], tok[be][:], posb[be][:], ALU.add))
                    if st.has("ln"):
                        dve.wait_ge(S["rs_ok"], upto(tl))
                        dve.wait_ge(S["mv_ok"], upto(tl))
                        h = hres[:, bass.ds(tl, 1), :].rearrange("p o d -> p (o d)")
                        ch.step(dve.scalar_tensor_tensor(emb[bl][:], emb[bl][:], mv[bl][:, 0:1], gam[:],
                                                         ALU.subtract, ALU.mult))
                    ch.done()
                    if st.has("emb"):
                        dve.sem_inc(S["emb_rd"], 1)
                        ch.step(dve.scalar_tensor_tensor(emb[be][:], typ0[:], typn[:, bass.ds(te, 1)], emb[be][:],
                                                         ALU.mult, ALU.add))
                    if st.has("ln"):
                        ch.step(dve.scalar_tensor_tensor(h, emb[bl][:], rs[bl][:, 0:1], bet[:], ALU.mult, ALU.add))
                    ch.done()
                    if st.has("emb"):
                        ch.step(dve.scalar_tensor_tensor(emb[be][:], typ1[:], typf[:, bass.ds(te, 1)], emb[be][:],
                                                         ALU.mult, ALU.add))
                    if st.has("ln"):
                        settle(dve, spare)
                        ch.step(dve.bn_stats(st6[bl][:], h))
                    ch.done()
                    settle(dve, spare)
                    if st.has("emb"):
                        ch.step(dve.bn_stats(st6[be][:], emb[be][:]))
                    if st.has("ln"):
                        dve.bn_aggr(mvb[bl][:], st6[bl][:]).then_inc(S["mvb_ok"], 1)
                    if st.has("emb"):
                        ch.done()
                        settle(dve, spare)
                        dve.bn_aggr(mv[be][:], st6[be][:]).then_inc(S["mv_ok"], 1)

                def outputs():
                    if not st.has("y"):
                        return
                    t, b = st.tile("y"), st.two("y")
                    dve.wait_ge(S["y_ps"], upto(t))
                    h = hres[:, bass.ds(t, 1), :].rearrange("p o d -> p (o d)")
                    dve.tensor_tensor(h, ps_v[:, 0:D], h, ALU.add).then_inc(S["y_ok"], 1)

                if st.has("xn"):
                    t, b = st.tile("xn"), st.two("xn")
                    dve.wait_ge(S["rsb_ok" if l == 0 else "rs_ok"], upto(t))
                    after(dve, S["xT_ps"], before2("xn"))
                    m, r = (mvb, rs2) if l == 0 else (mv, rs)
                    dve.tensor_scalar(xn[b][:].rearrange("p (o d) -> p o d", o=1), hres[:, bass.ds(t, 1), :],
                                      m[b][:, 0:1], r[b][:, 0:1], ALU.subtract, ALU.mult).then_inc(S["xn_ok"], 1)
                if l == 0:
                    if st.has("emb") or st.has("ln"):
                        embed_and_normalise()
                elif st.has("emb"):
                    t, b = st.tile("emb"), st.two("emb")
                    dve.wait_ge(M_["tok"][b], 16 * (st.pair("emb") + 1))
                    dve.wait_ge(M_["pos"][b], 16 * (st.pair("emb") + 1))
                    ch.link(dve.tensor_scalar(emb[b][:], tok[b][:], route2[:, TOPK, bass.ds(t, 1)], None, ALU.mult))
                    ch.link(dve.scalar_tensor_tensor(emb[b][:], posb[b][:], route2[:, TOPK + 1, bass.ds(t, 1)],
                                                     emb[b][:], ALU.mult, ALU.add))
                    dve.sem_inc(S["emb_rd"], 1)
                    ch.link(dve.tensor_tensor(hres[:, bass.ds(t, 1), :],
                                              emb[b][:].rearrange("p (o d) -> p o d", o=1),
                                              hres[:, bass.ds(t, 1), :], ALU.add))
                    moments(hres[:, bass.ds(t, 1), :], b, mv, "mv_ok")
                outputs()
                if st.has("s"):
                    b = st.two("s")
                    sc = score[b][:, :, :, 0:keys]
                    psv = ps_s[:, :, 0:A * keys].rearrange("p g (a k) -> p g a k", a=A)
                    dve.wait_ge(S["s_ps"], done("s"))
                    if l == 0:
                        src = psv
                    else:
                        dve.wait_ge(M_["rld"][b], 16 * (st.pair("s") + 1))
                        for g in range(G):
                            ins = dve.tensor_tensor(sc[:, g], psv[:, g],
                                                    relb[b][:, :, 3 * g:3 * g + 3].rearrange("p s a -> p a s"),
                                                    ALU.add)
                        ins.then_inc(S["s_rd"], 1)
                        dve.wait_ge(S["s_rd"], done("s"))
                        src = sc
                    ch.link(dve.tensor_reduce(mx[b][:].rearrange("p (g a) -> p g a", g=G), src, AX.X, ALU.max))
                if st.has("z"):
                    t, b = st.tile("z"), st.two("z")
                    dve.wait_ge(S["rsz_ok"], upto(t))
                    after(dve, S["zT_ps"], before2("z"))
                    dve.tensor_scalar(zn[b][:].rearrange("p (o d) -> p o d", o=1), hres[:, bass.ds(t, 1), :],
                                      mvz[b][:, 0:1], rsz[b][:, 0:1], ALU.subtract, ALU.mult).then_inc(S["zn_ok"], 1)
                    if l == 0:
                        dve.tensor_copy(mean[:, bass.ds(t, 1)], mvz[b][:, 0:1])
                        dve.tensor_copy(rstd[:, bass.ds(t, 1)], rsz[b][:])
                if st.has("s"):
                    b = st.two("s")
                    m4 = mx[b][:].rearrange("p (g a o) -> p g a o", g=G, o=1).to_broadcast([128, G, A, keys])
                    dve.tensor_tensor(sc, src, m4, ALU.subtract).then_inc(S["s_sub"], 1)
                if st.has("o"):
                    b = st.two("o")
                    dve.wait_ge(S["o_ps"], done("o"))
                    o = ps_v[:, 0:H * (DH + 1)].rearrange("p (h e) -> p h e", h=H)
                    ch.link(dve.reciprocal(rden[b][:].rearrange("p (h o) -> p h o", o=1), o[:, :, DH:DH + 1]))
                    dve.tensor_tensor(on[b][:].rearrange("p (h e) -> p h e", h=H), o[:, :, 0:DH],
                                      rden[b][:].rearrange("p (h o) -> p h o", o=1).to_broadcast([128, H, DH]),
                                      ALU.mult).then_inc(S["o_sb"], 1)
                if st.has("y"):
                    t, b = st.tile("y"), st.two("y")
                    dve.wait_ge(S["y_ok"], upto(t))
                    moments(hres[:, bass.ds(t, 1), :], b, mvz, "mvz_ok", st6z)
            pipeline(dve, ages, body, ch, 10 if l == 0 else 7)

        @block_a.sync
        def _(sp):
            for dst, src in [(ids, ids_h), (typi, typ_h)]:
                sp.dma_start(dst[:], src).then_inc(ids_ld, 16)
            loads = [(relw, relblk), (rel32s, rel32)]
            for (c0, c1), src in [(qk_w[0], wqk0), (v_w[0], wv0), (o_w[0], wo0), (r_w, wr)]:
                loads += [(c0, src[0:128, :]), (c1, src[128:, :])]
            for dst, src in [(gam, gamma), (bet, beta), (typ0, type_w[0:1, :]), (typ1, type_w[1:2, :])]:
                sp.dma_start(dst[:], src.to_broadcast([128, D])).then_inc(const_ld, 16)
            for dst, src in loads:
                sp.dma_start(dst[:], src).then_inc(const_ld, 16)
            assert len(loads) + 4 == N_CONST, len(loads)
            M_, S, ages = M[0], L[0], AGES[0]
            zr = xs_d.rearrange("(n p r) d -> n p (r d)", n=NT, r=ZROWS)
            sp.wait_ge(zero_ok, 2)
            h1_v = h1_d.rearrange("(t n c) d -> n c t d", n=NT, c=2)

            def body(st):
                if st.has("gather"):
                    t, b = st.tile("gather"), st.two("gather")
                    after(sp, S["emb_rd"], upto(t - 2))
                    settle(sp, spare)
                    for c in range(2):
                        sp.dma_start(posb[b][64 * c:64 * c + 64, :],
                                     pos_w[bass.ds(2 * t + c, 1), :].to_broadcast([64, D])).then_inc(M_["pos"][b], 16)
                    sp.dma_start(zr[bass.ds(t, 1)].rearrange("o p d -> (o p) d"), zrow[0:zr.shape[1], 0:ZROWS * D])\
                        .then_inc(xs_zero, 16)
                if st.has("y"):
                    t, b = st.tile("y"), st.two("y")
                    sp.wait_ge(S["y_ok"], upto(t))
                    settle(sp, spare)
                    for c in range(2):
                        sp.dma_start(h1_v[bass.ds(t, 1), c].rearrange("a t d -> (a t) d"),
                                     hres[64 * c:64 * c + 64, bass.ds(t, 1), :].rearrange("p o d -> p (o d)")).then_inc(M_["h1"][b], 16)
            pipeline(sp, ages, body)
            for p in range(2):
                sp.wait_ge(M_["h1"][p], 32 * (NT // 2))

        @block_a.gpsimd
        def _(pool):
            S = L[0]
            pool.memset(ident[:], 0.0).then_inc(pool_c, 1)
            pool.memset(tri[:], 1.0).then_inc(pool_c, 1)
            pool.memset(ones[:], 1.0).then_inc(const_ok, 1)
            pool.memset(mhalf[:], -0.5).then_inc(const_ok, 1)
            pool.memset(epsc[:], EPS).then_inc(pool_c, 1)
            pool.wait_ge(pool_c, 3)
            pool.affine_select(out=ident[:], in_=ident[:], compare_op=ALU.not_equal, fill=1.0, base=0,
                               pattern=[[-1, 128]], channel_multiplier=1).then_inc(const_ok, 1)
            pool.affine_select(out=tri[:], in_=tri[:], compare_op=ALU.is_gt, fill=0.0, base=0,
                               pattern=[[1, 128]], channel_multiplier=-1).then_inc(const_ok, 1)
            pool.memset(wout4[:], 0.0).then_inc(zero_ok, 1)
            pool.memset(zrow[:], 0.0).then_inc(zero_ok, 1)
            pool.wait_ge(ids_ld, 32)
            pool_steps(pool, 0)

        @block_a.tensor
        def _(pe):
            pe.wait_ge(const_ld, 16 * N_CONST)
            pe.wait_ge(const_ok, 8)
            pe_steps(pe, 0)

        @block_a.scalar
        def _(act):
            late = [(wout4[32 * k:32 * k + NODES, k, :], wout) for k in range(4)]
            for (c0, c1), src in [(qk_w[1], wqk1), (v_w[1], wv1), (o_w[1], wo1), (in_w, win)]:
                late += [(c0[:], src[0:128, :]), (c1[:], src[128:, :])]
            act.wait_ge(const_ok, 8)
            act.wait_ge(const_ld, 16 * N_CONST)
            act.wait_ge(zero_ok, 2)
            for dst, src in late:
                act.dma_start(dst, src).then_inc(late_ld, 16)
            for p in range(2):
                act.dma_start(rel_d[p][:, (LPAD + REL) * H:], zrow[:]).then_inc(rel_zero, 16)
            act_steps(act, 0)
            act.wait_ge(late_ld, 16 * len(late))

        @block_a.vector
        def _(dve):
            for p in range(2):
                dve.memset(xT1[p][D1:D1 + 1, :], 1.0)
                dve.memset(zT1[p][D1:D1 + 1, :], 1.0)
                dve.memset(oT1[p][D1:D1 + 1, :], 1.0).then_inc(dve_c, 1)
            for p in range(4):
                dve.memset(vv[p][:], 0.0).then_inc(dve_c, 1)
            dve.wait_ge(dve_c, 6)
            for p in range(4):
                vb = vv[p][:].rearrange("p (c r s e) -> p c r s e", c=2, r=H // 2, s=2)
                for s in range(2):
                    ins = dve.memset(vb[64 * s:64 * s + 64, :, :, s, DH:DH + 1], 1.0)
                ins.then_inc(const_ok, 1)
            dve.wait_ge(const_ld, 16 * N_CONST)
            dve.tensor_copy(typf[:], typi[:]).then_inc(dve_c, 1)
            dve.wait_ge(dve_c, 7)
            dve.tensor_scalar(typn[:], typf[:], -1.0, 1.0, ALU.mult, ALU.add).then_inc(dve_c, 1)
            rw = relw[:].rearrange("p (a g j) -> p a g j", a=A, g=G)
            for g in range(G):
                q = slice(32 * g, 32 * g + 32)
                for a in range(A):
                    ins = dve.tensor_scalar(rw[q, a, g], rw[q, a, g], rel32s[q, a % 2:a % 2 + 1], None, ALU.subtract)
            ins.then_inc(dve_c, 1)
            dve.wait_ge(dve_c, 9)
            dve_steps(dve, 0)

        ctx2.close()

        B_ = {n: sem("B_" + n) for n in ("g_ex", "dve", "cnt_ps", "ready", "pool", "placed", "turned_ps", "turned")}
        route_st, route_ld = sem("route_st"), sem("route_ld")
        h1_ld = [sem(f"h1_ld{c}") for c in range(4)]
        scat = [sem(f"scat{p}") for p in range(SCAT)]
        with nc.Block() as block:
            @block.sync
            def _(sp):
                sp.wait_ge(B_["turned"], 1)
                sp.dma_start(route_d.rearrange("q (n k) -> n q k", n=NT), turned[:]).then_inc(route_st, 16)
                sp.wait_ge(route_st, 16)
                sp.dma_start(route2[:], route_d.rearrange("q (b t) -> b q t", b=B)).then_inc(route_ld, 16)

            @block.gpsimd
            def _(pool):
                pool.iota(etabi[:], pattern=[[BLK, NBLK]], base=0, channel_multiplier=0).then_inc(B_["pool"], 1)
                pool.iota(cnti[:], pattern=[[-1, E]], base=E, channel_multiplier=0).then_inc(B_["pool"], 1)

            @block.tensor
            def _(pe):
                pe.wait_ge(B_["ready"], 1)
                pe.matmul(ps_k[:], tri[:], bigs[5], start=True, stop=True).then_inc(B_["cnt_ps"], 1)
                pe.matmul(ps_v[:], ones[:], bigs[5], start=True, stop=True).then_inc(B_["cnt_ps"], 1)
                pe.wait_ge(B_["placed"], 1)
                for q, src in enumerate((small[:, 5, :], small[:, 6, :], wk[0][:], wk[1][:])):
                    last = pe.transpose(ps_q[0:NT, q * 128:q * 128 + 128], src, ident[:])
                last.then_inc(B_["turned_ps"], 1)

            @block.scalar
            def _(act):
                act.wait_ge(B_["g_ex"], 1)
                act.activation(gat, gat, ACT.Exp).then_inc(B_["g_ex"], 1)
                act.wait_ge(B_["turned_ps"], 1)
                act.activation(turned[:].rearrange("n q k -> n (q k)"), ps_q[0:NT, :], ACT.Copy)\
                    .then_inc(B_["turned"], 1)

            @block.vector
            def _(dve):
                ch = Chain(dve, B_["dve"])
                k = ch.link
                def flat(j):
                    return bigs[j].rearrange("p (t e) -> p t e", e=E)
                def col(j):
                    return small[:, j, :].rearrange("p (t o) -> p t o", o=1)
                def wide(ap):
                    return ap.to_broadcast([128, NT, E])
                rev = cnt[:, 0, :].rearrange("p (o e) -> p o e", o=1).to_broadcast([128, NT, E])
                dve.wait_ge(B_["pool"], 2)
                k(dve.tensor_copy(cnt[:, 0, :], cnti[:]))
                k(dve.tensor_copy(etab[:], etabi[:]))
                k(dve.tensor_reduce(small[:, 0, :], logits[:, :, 0:E], AX.X, ALU.max))
                dve.tensor_tensor(gat, logits[:, :, 0:E], wide(col(0)), ALU.subtract).then_inc(B_["g_ex"], 1)
                dve.wait_ge(B_["g_ex"], 2)
                k(dve.tensor_reduce(small[:, 1, :], gat, AX.X, ALU.add))
                k(dve.reciprocal(small[:, 2, :], small[:, 1, :]))
                k(dve.tensor_tensor(gat, gat, wide(col(2)), ALU.mult))
                for r in range(TOPK):
                    k(dve.tensor_reduce(wk[r][:], gat, AX.X, ALU.max))
                    k(dve.tensor_tensor(flat(2), gat, wide(wk[r][:].rearrange("p (t o) -> p t o", o=1)), ALU.is_equal))
                    k(dve.tensor_tensor(flat(2), flat(2), rev, ALU.mult))
                    k(dve.tensor_reduce(small[:, 3, :], flat(2), AX.X, ALU.max))
                    k(dve.tensor_tensor(flat(r), flat(2), wide(col(3)), ALU.is_equal))
                    if r == 0:
                        k(dve.scalar_tensor_tensor(gat, flat(0), -2.0, gat, ALU.mult, ALU.add))
                dve.tensor_tensor(bigs[5], bigs[0], bigs[1], ALU.add).then_inc(B_["ready"], 1)
                dve.wait_ge(B_["cnt_ps"], 2)
                k(dve.memset(small[:, 4, :], 1.0))
                for e in range(E):
                    sc = dve.tensor_tensor_scan(flat(3)[:, :, e], small[:, 4, :],
                                                ps_v[:].rearrange("p (t e) -> p t e", e=E)[:, :, e],
                                                0.0, ALU.mult, ALU.add)
                    k(sc)
                k(dve.tensor_tensor(bigs[4], bigs[3], ps_v[:], ALU.subtract))
                k(dve.tensor_tensor(bigs[4], bigs[4], ps_k[:], ALU.add))
                k(dve.tensor_scalar(cnti[:], flat(3)[:, NT - 1, :], float(BLK - 1), None, ALU.add))
                k(dve.tensor_scalar(cnti[:], cnti[:], BLK.bit_length() - 1, None, ALU.arith_shift_right))
                k(dve.tensor_copy(cnt[:, 1, :], cnti[:]))
                k(dve.tensor_scalar(cnt[:, 1, :], cnt[:, 1, :], float(BLK), None, ALU.mult))
                k(dve.tensor_tensor_scan(cnt[:, 2, :], small[:, 4, 0:E], cnt[:, 1, :], 0.0, ALU.mult, ALU.add))
                k(dve.tensor_tensor(cnt[:, 3, :], cnt[:, 2, :], cnt[:, 1, :], ALU.subtract))
                start = cnt[:, 3, :].rearrange("p (o e) -> p o e", o=1)
                k(dve.tensor_tensor(flat(4), flat(4), start.to_broadcast([128, NT, E]), ALU.add))
                for r in range(TOPK):
                    k(dve.tensor_tensor(flat(2), flat(r), flat(4), ALU.mult))
                    k(dve.tensor_reduce(small[:, 5 + r, :], flat(2), AX.X, ALU.add))
                    k(dve.tensor_copy(posi[r][:], small[:, 5 + r, :]))
                dve.sem_inc(B_["placed"], 1)
                k(dve.tensor_tensor(etmp, etab[:].rearrange("p (j o) -> p j o", o=1).to_broadcast([128, NBLK, E]),
                                    start.to_broadcast([128, NBLK, E]), ALU.is_ge))
                k(dve.tensor_reduce(etab[:], etmp, AX.X, ALU.add))
                k(dve.tensor_scalar(etabi[:], etab[:], -1.0, None, ALU.add))

        C_ = {n: sem("C_" + n) for n in ("ready",)}
        with nc.Block() as block:
            @block.vector
            def _(dve):
                def body(n, p, k):
                    after(dve, scat[p], 32 * k)
                    dve.tensor_copy(sidx[p][0][:], posi[0][:, bass.ds(n, 1)])
                    dve.tensor_copy(sidx[p][1][:], posi[1][:, bass.ds(n, 1)])
                    dve.tensor_scalar(srow[p][:].rearrange("p (o d) -> p o d", o=1), hres[:, bass.ds(n, 1), :],
                                      mean[:, bass.ds(n, 1)], rstd[:, bass.ds(n, 1)],
                                      ALU.subtract, ALU.mult).then_inc(C_["ready"], 1)
                for p in range(SCAT):
                    body(p, p, 0)
                with dve.Fori(0, NT // SCAT - 1) as i:
                    for p in range(SCAT):
                        body(SCAT * i + (SCAT + p), p, i + 1)

            @block.gpsimd
            def _(pool):
                pool.wait_ge(xs_zero, 16 * NT)
                with pool.Fori(0, NT // SCAT) as i:
                    for p in range(SCAT):
                        for ix in sidx[p]:
                            pool.wait_ge(C_["ready"], SCAT * i + (p + 1))
                            settle(pool, spare)
                            pool.indirect_dma_start(xs_d, bass.IndirectOffsetOnAxis(ap=ix[:], axis=0),
                                                    srow[p][:], None).then_inc(scat[p], 16)
                for p in range(SCAT):
                    pool.wait_ge(scat[p], 32 * (NT // SCAT))

        D_ = {n: sem("D_" + n) for n in ("xT_ps", "xhi_sb", "xlo_sb", "split", "dve", "h_ps", "h_sb", "y_ps", "y_sb")}
        w1_ld = [sem(f"w1_ld{p}") for p in range(2)]
        w2_ld = [sem(f"w2_ld{p}") for p in range(2)]
        y_st = [sem(f"y_st{p}") for p in range(2)]
        ages_d = dict(load=0, h=1, y=2)
        NH = NI // 2
        ps_y = [ps_v, ps_k]
        ctx_d = ExitStack()

        def of_phase_d(name, shape, dt=F32):
            return [ctx_d.enter_context(nc.sbuf_tensor(f"{name}{p}", shape, dt)) for p in range(2)]

        XW = D + D1
        xs, ys = of_phase_d("xs", [128, 2, XW]), of_phase_d("ys", [128, 2, D])
        w1hi = list(zip(of_phase_d("w1hi_c0", [128, I], F32R), of_phase_d("w1hi_c1", [128, I], F32R)))
        w1lo = list(zip(of_phase_d("w1lo_c0", [128, I], F32R), of_phase_d("w1lo_c1", [128, I], F32R)))
        xhi, xlo = of_phase_d("xhi", [128, 2 * BLK], F32R), of_phase_d("xlo", [128, BLK], F32R)
        with nc.Block() as block:
            @block.sync
            def _(sp):
                hv = h1_d.rearrange("(t b) d -> b t d", b=B)

                def body(st):
                    before2 = upto(st.n - 2, NBLK)
                    if isinstance(st.n, int) and 4 <= st.n < 8:
                        c = st.n - 4
                        sp.dma_start(hres[:, 16 * c:16 * c + 16, :], hv[:, 16 * c:16 * c + 16, :])\
                            .then_inc(h1_ld[c], 16)
                    if st.has("load"):
                        t, b = st.tile("load"), st.two("load")
                        ex = sp.value_load(etabi[0:1, bass.ds(t, 1)], min_val=0, max_val=E - 1)
                        after(sp, D_["h_sb"], NH * before2)
                        settle(sp, spare)
                        rows_ = xs_d[bass.ds(t * BLK, BLK), :].rearrange("(s p) d -> p s d", s=2)
                        sp.dma_start(xs[b][:, :, 0:D], rows_).then_inc(w1_ld[b], 16)
                        sp.dma_start(xs[b][:, :, D:XW], rows_[:, :, 128:D]).then_inc(w1_ld[b], 16)
                        loads = [(w1[b][0], w1h[bass.ds(ex, 1), 0:128, :]), (b1s[b][:], b1h[bass.ds(ex, 1)])]
                        loads += [(w1[b][1][r:r + D1, :], w1h[bass.ds(ex, 1), 128:, :]) for r in (0, D1)]
                        for dst, src in loads:
                            sp.dma_start(dst, src.rearrange("o k i -> (o k) i")).then_inc(w1_ld[b], 16)
                        after(sp, D_["y_sb"], before2)
                        settle(sp, spare)
                        sp.dma_start(probT[b][:, 0:NI * D], w2h[bass.ds(ex, 1), :, :].rearrange("o k i -> (o k) i"))\
                            .then_inc(w2_ld[b], 16)
                        sp.dma_start(b2s[b], b2h[bass.ds(ex, 1), :].to_broadcast([128, D])).then_inc(w2_ld[b], 16)
                    if st.has("y"):
                        t, b = st.tile("y"), st.two("y")
                        sp.wait_ge(D_["y_sb"], upto(t, NBLK))
                        settle(sp, spare)
                        sp.dma_start(ys_d[bass.ds(t * BLK, BLK), :].rearrange("(s p) d -> p s d", s=2), ys[b][:])\
                            .then_inc(y_st[b], 16)
                pipeline(sp, ages_d, body, tiles=NBLK)
                for p in range(2):
                    sp.wait_ge(y_st[p], 16 * (NBLK // 2))

            @block.tensor
            def _(pe):
                def body(st):
                    t = st.n - 1
                    if st.has("h"):
                        b = st.two("h")
                        pe.wait_ge(w1_ld[b], 96 * (st.pair("h") + 1))
                        after(pe, D_["xhi_sb"], upto(t - 1, NBLK))
                        after(pe, D_["xlo_sb"], upto(t - 1, NBLK))
                        for s in range(2):
                            pe.transpose(ps_t[:, s * 128:s * 128 + 128], xs[b][:, s, 0:128], ident[:])
                            last = pe.transpose(ps_t[:, BLK + s * 128:BLK + s * 128 + 128], xs[b][:, s, 128:XW],
                                                ident[:])
                        last.then_inc(D_["xT_ps"], 1)
                    if st.has("y"):
                        b = st.two("y")
                        pe.wait_ge(w2_ld[b], 32 * (st.pair("y") + 1))
                        after(pe, D_["y_sb"], upto(t - 2, NBLK))
                        for j in range(NH):
                            pe.wait_ge(D_["h_sb"], NH * st.tile("y") + j + 1)
                            for c in (2 * j, 2 * j + 1):
                                for s in range(2):
                                    last = pe.matmul(ps_y[s][:, 0:D], hT[b][:, c, s * 128:s * 128 + 128],
                                                     w2[b][:, c, :], start=(c == 0), stop=(c == NI - 1))
                        last.then_inc(D_["y_ps"], 1)
                    if st.has("h"):
                        b = st.two("h")
                        pe.wait_ge(D_["xhi_sb"], upto(t, NBLK))
                        pe.wait_ge(D_["xlo_sb"], upto(t, NBLK))
                        pe.wait_ge(D_["split"], upto(t, NBLK))
                        for j in range(NH):
                            if not (isinstance(t, int) and t == 0):
                                pe.wait_ge(D_["h_sb"], NH * (t - 1) + j + 1)
                            for c in (2 * j, 2 * j + 1):
                                dst = ps_s[:, j, (c % 2) * BLK:(c % 2) * BLK + BLK]
                                u = slice(c * 128, c * 128 + 128)
                                terms = [(w1hi[b][0][:, u], xhi[b][:, 0:BLK]),
                                         (w1lo[b][0][:, u], xhi[b][:, 0:BLK]),
                                         (w1hi[b][0][:, u], xlo[b][:]),
                                         (w1hi[b][1][:, u], xhi[b][:, BLK:2 * BLK]),
                                         (w1lo[b][1][:, u], xhi[b][:, BLK:2 * BLK])]
                                for k, (w, x) in enumerate(terms):
                                    last = pe.matmul(dst, w, x, start=(k == 0), stop=(k == len(terms) - 1))
                            last.then_inc(D_["h_ps"], 1)
                pipeline(pe, ages_d, body, tiles=NBLK)

            @block.scalar
            def _(act):
                def body(st):
                    if st.has("h"):
                        t, b = st.tile("h"), st.two("h")
                        act.wait_ge(D_["xT_ps"], upto(t, NBLK))
                        act.activation(xhi[b][:], ps_t[:], ACT.Copy).then_inc(D_["xhi_sb"], 1)
                        for j in range(NH):
                            act.wait_ge(D_["h_ps"], NH * t + j + 1)
                            after(act, D_["y_ps"], upto(t - 2, NBLK))
                            for c in (2 * j, 2 * j + 1):
                                last = act.activation(hT[b][:, c, :], ps_s[:, j, (c % 2) * BLK:(c % 2) * BLK + BLK],
                                                      ACT.Gelu, bias=b1s[b][:, c:c + 1])
                            last.then_inc(D_["h_sb"], 1)
                pipeline(act, ages_d, body, tiles=NBLK)

            @block.vector
            def _(dve):
                ch = Chain(dve, D_["dve"])

                def body(st):
                    if st.has("h"):
                        t, b = st.tile("h"), st.two("h")
                        dve.wait_ge(w1_ld[b], 96 * (st.pair("h") + 1))
                        for c in range(2):
                            ch.step(dve.tensor_copy(w1hi[b][c][:], w1[b][c]))
                        ch.done()
                        dve.tensor_tensor(w1lo[b][0][:], w1[b][0], w1hi[b][0][:].bitcast(F32), ALU.subtract)
                        dve.tensor_tensor(w1lo[b][1][:], w1[b][1], w1hi[b][1][:].bitcast(F32),
                                          ALU.subtract).then_inc(D_["split"], 1)
                        dve.wait_ge(D_["xhi_sb"], upto(t, NBLK))
                        dve.tensor_tensor(xlo[b][:], ps_t[:, 0:BLK], xhi[b][:, 0:BLK].bitcast(F32), ALU.subtract)
                        rest = xhi[b][D1:128, BLK:2 * BLK]
                        dve.tensor_tensor(rest, ps_t[D1:128, BLK:2 * BLK], rest.bitcast(F32), ALU.subtract)\
                            .then_inc(D_["xlo_sb"], 1)
                    if st.has("y"):
                        t, b = st.tile("y"), st.two("y")
                        dve.wait_ge(D_["y_ps"], upto(t, NBLK))
                        after(dve, y_st[b], 16 * st.pair("y"))
                        for s in range(2):
                            ins = dve.tensor_tensor(ys[b][:, s, :], ps_y[s][:, 0:D], b2s[b], ALU.add)
                        ins.then_inc(D_["y_sb"], 1)
                pipeline(dve, ages_d, body, ch, 2, tiles=NBLK)

        ctx_d.close()
        E_ = {"posi2": sem("E_posi2")}
        rpad = two("rpad", [128, LPAD + REL, H])
        relb = two("relb", [128, B, H])
        with nc.Block() as block:
            @block.sync
            def _(sp):
                S, M_ = L[1], M[1]
                sp.wait_ge(rel_zero, 32)

                def body(st):
                    if st.has("r"):
                        t, b = st.tile("r"), st.two("r")
                        sp.wait_ge(S["pad_ok"], upto(t))
                        settle(sp, spare)
                        after(sp, M_["rld"][b], 16 * st.pair("r"))
                        settle(sp, spare)
                        sp.dma_start(rel_d[b][:, 0:(LPAD + REL) * H], rpad[b][:].rearrange("p s h -> p (s h)"))\
                            .then_inc(M_["rst"][b], 16)
                        sp.wait_ge(M_["rst"][b], 16 * (st.pair("r") + 1))
                        settle(sp, spare)
                        after(sp, S["s_rd"], upto(t - 2))
                        settle(sp, spare)
                        w = ROWW - H
                        src = rel_d[b].rearrange("t w -> (t w)")[(B - 1) * H:(B - 1) * H + B * w]
                        sp.dma_start(relb[b][:].rearrange("p s h -> p (s h)"),
                                     src.rearrange("(t w) -> t w", w=w)[:, 0:B * H]).then_inc(M_["rld"][b], 16)
                pipeline(sp, AGES[1], body)

            @block.gpsimd
            def _(pool):
                pool.wait_ge(E_["posi2"], 2)
                pool_steps(pool, 1)

            @block.tensor
            def _(pe):
                pe_steps(pe, 1)

            @block.scalar
            def _(act):
                act_steps(act, 1)

            @block.vector
            def _(dve):
                for p in range(4):
                    vj = vv[p][:, 0:H * (DH + 1)].rearrange("p (h e) -> p h e", h=H)
                    ins = dve.memset(vj[:, :, DH:DH + 1], 1.0)
                ins.then_inc(dve_c, 1)
                dve.wait_ge(dve_c, 10)
                dve.wait_ge(route_ld, 16)
                for k in range(TOPK):
                    dve.tensor_copy(posi2[k][:], route2[:, k, :]).then_inc(E_["posi2"], 1)
                for c in range(4):
                    dve.wait_ge(h1_ld[c], 16)
                dve_steps(dve, 1)

        fg = relb[0][:].rearrange("p s h -> p (s h)")[:, 0:NT * NODES].rearrange("p (t n) -> p t n", n=NODES)
        fs = relb[1][:].rearrange("p s h -> p (s h)")[:, 0:NT * NODES].rearrange("p (t n) -> p t n", n=NODES)
        fr = rpad[0][:].rearrange("p s h -> p (s h)")[:, 0:NT * NODES].rearrange("p (t n) -> p t n", n=NODES)
        fc = sb("fc", [128, NT, 32])
        F_ = {n: sem("F_" + n) for n in ("gelu", "dve", "c_ok", "cT_ps", "cT_sb", "o_ps", "o_sb")}
        out_st = [sem(f"out_st{p}") for p in range(2)]
        c4 = [prob[p][:, 0:128] for p in range(2)]
        cT4 = [prob[p][:, 128:256] for p in range(2)]
        ho4 = [score[p][:].rearrange("p g a k -> p (g a k)")[:, 0:4 * D].rearrange("p (k d) -> p k d", k=4)
               for p in range(2)]
        NM = NT // 4
        turn_bank = [ps_t, ps_q]

        def groups(eng, body):
            for m in range(2):
                body(m, m, 0)
            with eng.Fori(0, NM // 2 - 2) as i:
                for p in range(2):
                    body(2 * i + (2 + p), p, i + 1)
            for m in range(NM - 2, NM):
                body(m, m % 2, m // 2)

        with nc.Block() as block:
            @block.scalar
            def _(act):
                act.activation(fg, logits[:], ACT.Gelu).then_inc(F_["gelu"], 1)

                def body(m, p, k):
                    act.wait_ge(F_["cT_ps"], m + 1)
                    after(act, F_["o_ps"], upto(m - 2))
                    act.activation(cT4[p], turn_bank[p][:, 0:128], ACT.Copy).then_inc(F_["cT_sb"], 1)
                groups(act, body)

            @block.tensor
            def _(pe):
                def turn(m, p):
                    pe.wait_ge(F_["c_ok"], m + 1)
                    after(pe, F_["cT_sb"], upto(m - 2))
                    pe.transpose(turn_bank[p][:, 0:128], c4[p], ident[:]).then_inc(F_["cT_ps"], 1)

                def body(m, p, k):
                    if not isinstance(m, int) or m + 1 < NM:
                        turn(m + 1, 1 - p)
                    pe.wait_ge(F_["cT_sb"], m + 1)
                    after(pe, F_["o_sb"], upto(m - 2))
                    for side in range(2):
                        last = pe.matmul(ps_s[:, 2 * p + side, 0:2 * D], cT4[p],
                                         wout4[:, 2 * side:2 * side + 2, :].rearrange("p k d -> p (k d)"),
                                         start=True, stop=True)
                    last.then_inc(F_["o_ps"], 1)
                turn(0, 0)
                groups(pe, body)

            @block.vector
            def _(dve):
                ch = Chain(dve, F_["dve"])
                k = ch.link
                k(dve.tensor_scalar(fs, logits[:], 0.0, None, ALU.is_gt))
                k(dve.memset(fc[:], 0.0))
                k(dve.memset(fr, 1.0))
                dve.wait_ge(F_["gelu"], 1)

                def children(t, lo, n, side):
                    return t[:, :, 2 * lo + 1:2 * lo + 1 + 2 * n].rearrange("p t (n s) -> p t n s", s=2)[:, :, :, side]

                for lo, n in ((0, 1), (1, 2), (3, 4), (7, 3)):
                    parent = fr[:, :, lo:lo + n]
                    k(dve.tensor_tensor(children(fr, lo, n, 1), parent, fs[:, :, lo:lo + n], ALU.mult))
                    k(dve.tensor_tensor(children(fr, lo, n, 0), parent, children(fr, lo, n, 1), ALU.subtract))
                    for side in range(2):
                        k(dve.tensor_tensor(children(fc, lo, n, side), children(fr, lo, n, side),
                                            fg[:, :, lo:lo + n], ALU.mult))
                last_r, last_c = fr[:, :, LAST:NODES], fc[:, :, LAST:NODES]
                c3 = lambda j: small[:, j, :].rearrange("p (t o) -> p t o", o=1)
                k(dve.tensor_reduce(small[:, 0, :], fr[:, :, 10:15], AX.X, ALU.add))
                k(dve.tensor_tensor(last_r, last_r, c3(0), ALU.add))
                prod = probT[0][:, 0:NT * NODES]\
                    .rearrange("p (t n) -> p t n", n=NODES)
                k(dve.tensor_tensor(prod, fr, fg, ALU.mult))
                k(dve.tensor_reduce(small[:, 1, :], prod[:, :, 10:NODES], AX.X, ALU.add))
                k(dve.tensor_tensor(last_c, last_c, c3(1), ALU.add))
                k(dve.scalar_tensor_tensor(last_c, fg[:, :, LAST:NODES], 5.0, last_c, ALU.mult, ALU.add))

                def gather_coefficients(m, p):
                    after(dve, F_["cT_ps"], upto(m - 2))
                    dve.tensor_copy(c4[p].rearrange("p (k n) -> p k n", k=4), fc[:, bass.ds(4 * m, 4), :])\
                        .then_inc(F_["c_ok"], 1)

                def body(m, p, k):
                    if not isinstance(m, int) or m + 2 < NM:
                        gather_coefficients(m + 2, p)
                    dve.wait_ge(F_["o_ps"], m + 1)
                    after(dve, out_st[p], 16 * k)
                    dve.tensor_tensor(ho4[p].rearrange("p (s k) d -> p s (k d)", s=2),
                                      ps_s[:, 2 * p:2 * p + 2, 0:2 * D],
                                      hres[:, bass.ds(4 * m, 4), :].rearrange("p (s k) d -> p s (k d)", s=2),
                                      ALU.add).then_inc(F_["o_sb"], 1)
                for m in range(2):
                    gather_coefficients(m, m)
                groups(dve, body)

            @block.sync
            def _(sp):
                ov = out.rearrange("t b d -> b t d")

                def body(m, p, k):
                    sp.wait_ge(F_["o_sb"], m + 1)
                    settle(sp, spare)
                    sp.dma_start(ov[:, bass.ds(4 * m, 4), :], ho4[p]).then_inc(out_st[p], 16)
                groups(sp, body)
                for p in range(2):
                    sp.wait_ge(out_st[p], 16 * (NM // 2))


def rows(w, b):
    out = np.zeros((w.shape[0] + 1, w.shape[1]), np.float32)
    out[:-1] = w
    out[-1] = b
    return out


def head_slots(wq, bq, wk, bk):
    out = np.zeros((D + 1, QS + A, G, 2, DH), np.float32)
    q, k = [rows(w, b).reshape(D + 1, G, A, DH) for w, b in ((wq, bq), (wk, bk))]
    for a in range(A):
        out[:, a // 2, :, a % 2] = q[:, :, a]
        out[:, QS + a, :, a % 2] = k[:, :, a]
    return out.reshape(D + 1, (QS + A) * 128)


def laid_out(v):
    a = {k: np.asarray(x) for k, x in v.items()}
    qkv, qb = a["L1_attn_qkv_w"], a["L1_attn_qkv_b"]
    rel = a["L1_attn_rel_pos_emb"]
    relblk = np.zeros((G, 2, DH, A, G, REL), np.float32)
    rel32 = np.zeros((G, 2, DH, 2), np.float32)
    for g in range(G):
        for j in range(A):
            relblk[g, j % 2, :, j, g, :] = rel.T
            rel32[g, j % 2, :, j % 2] = rel[REL - 1]
    return {
        "ids_h": a["x"].T.reshape(NT, 128).T,
        "typ_h": a["mask_BS_i1_0"].T.reshape(NT, 128).T,
        "tok_w": a["L0_tok_tok_w"], "pos_w": a["L0_tok_pos_w"], "type_w": a["L0_tok_type_w"],
        "gamma": a["L0_tok_gamma"].reshape(1, D), "beta": a["L0_tok_beta"].reshape(1, D),
        "wqk0": head_slots(a["L0_attn_Wq"].T, a["L0_attn_bq"], a["L0_attn_Wk"].T, a["L0_attn_bk"]),
        "wv0": rows(a["L0_attn_Wv"].T, a["L0_attn_bv"]),
        "wo0": rows(a["L0_attn_Wout"].T, a["L0_attn_bout"]),
        "w1h": a["L0_ffn_W1"],
        "b1h": a["L0_ffn_b1"].reshape(E, NI, 128).transpose(0, 2, 1),
        "w2h": a["L0_ffn_W2"].reshape(E, NI, 128, D).transpose(0, 2, 1, 3).reshape(E, 128, NI * D),
        "b2h": a["L0_ffn_b2"],
        "wr": rows(a["L0_ffn_Wr"], a["L0_ffn_br"]),
        "wqk1": head_slots(qkv[0:D].T, qb[0:D], qkv[D:2 * D].T, qb[D:2 * D]),
        "wv1": rows(qkv[2 * D:].T, qb[2 * D:]),
        "wo1": rows(a["L1_attn_out_w"].T, a["L1_attn_out_b"]),
        "relblk": relblk.reshape(128, A * G * REL), "rel32": rel32.reshape(128, 2),
        "win": a["L1_ffn_weights_in"].T, "wout": a["L1_ffn_weights_out"],
    }


def build(nc, arrays):
    args = [nc.dram_tensor(n, x.shape, mybir.dt.from_np(x.dtype), kind="ExternalInput").ap()
            for n, x in arrays.items()]
    out = nc.dram_tensor("out_0_dram", [T, B, D], F32, kind="ExternalOutput").ap()
    tower(nc, *args, out)


def kernel(**inputs):
    import concourse.bacc as bacc
    from concourse.bass_utils import run_bass_kernel_spmd

    arrays = {n: np.ascontiguousarray(x) for n, x in laid_out(inputs).items()}
    nc = bacc.Bacc("TRN2", target_bir_lowering=False, num_devices=1)
    build(nc, arrays)
    r = run_bass_kernel_spmd(nc, [arrays], core_ids=[0])
    return r.results[0]["out_0_dram"]
```
